# Optimizing a Trainium2 kernel written in Bass

```python
import numpy as np
import jax
import jax.numpy as jnp

def _softmax(x, axis=-1):
    return jax.nn.softmax(x, axis=axis)

def _gelu(x):
    return jax.nn.gelu(x, approximate=True)

def _silu(x):
    return jax.nn.silu(x)

def _sigmoid(x):
    return jax.nn.sigmoid(x)

def _layernorm(x, axis=-1, eps=1e-05):
    m = jnp.mean(x, axis=axis, keepdims=True)
    v = jnp.var(x, axis=axis, keepdims=True)
    return (x - m) / jnp.sqrt(v + eps)

def _scatter_add(tgt, idx, src, axis=0):
    return tgt.at[idx].add(src)

def _segment_sum(src, seg, n):
    return jax.ops.segment_sum(src, seg, n)
kernel_name = 'mk_recurrent_d4_jaxref_r8_60350e'

def setup_inputs(seed: int=0):
    np.random.seed(seed)
    _w = jnp.asarray

    def _L0_attn_setup():
        import jax, jax.numpy as jnp
        import numpy as np
        B, T, E, H = (2, 512, 128, 16)
        D = E // H
        EPS = 1e-06

        def _feature_map(x):
            return jnp.where(x > 0, x + 1.0, jnp.exp(x))
        key = jax.random.key(seed)
        ks = jax.random.split(key, 9)
        s = 1.0 / np.sqrt(E)
        return {'x': jax.random.normal(ks[0], (B, T, E), dtype=jnp.float32), 'wq': jax.random.uniform(ks[1], (E, E), jnp.float32, -s, s), 'bq': jax.random.uniform(ks[2], (E,), jnp.float32, -s, s), 'wk': jax.random.uniform(ks[3], (E, E), jnp.float32, -s, s), 'bk': jax.random.uniform(ks[4], (E,), jnp.float32, -s, s), 'wv': jax.random.uniform(ks[5], (E, E), jnp.float32, -s, s), 'bv': jax.random.uniform(ks[6], (E,), jnp.float32, -s, s), 'wo': jax.random.uniform(ks[7], (E, E), jnp.float32, -s, s), 'bo': jax.random.uniform(ks[8], (E,), jnp.float32, -s, s)}
    _L0_attn_in = _L0_attn_setup()

    def _L0_ffn_setup():
        import jax, jax.numpy as jnp
        import numpy as np
        DIM = 128
        DEPTH = 6
        HEADS = 16
        DIM_HEAD = 64
        WINDOW = 32
        INNER = HEADS * DIM_HEAD
        DIM_INNER = int(DIM * 4 * 2 / 3)
        QK_SCALE = 8.0

        def shift_tokens(t):
            a, s = jnp.split(t, 2, -1)
            s = jnp.pad(s, ((0, 0), (1, 0), (0, 0)))[:, :-1]
            return jnp.concatenate([a, s], -1)

        def l2norm(t):
            return t / jnp.maximum(jnp.linalg.norm(t, axis=-1, keepdims=True), 1e-12)

        def rotate_half(x):
            x1, x2 = jnp.split(x, 2, -1)
            return jnp.concatenate([-x2, x1], -1)

        def rotary_tables(n):
            half = jnp.arange(0, DIM_HEAD, 2, dtype=jnp.float32)
            inv_freq = 1.0 / 10000.0 ** (half / DIM_HEAD)
            t = jnp.arange(n, dtype=jnp.float32)
            freqs = t[:, None] * inv_freq[None, :]
            freqs = jnp.concatenate([freqs, freqs], -1)
            base_scale = (half + 0.4 * DIM_HEAD) / (1.4 * DIM_HEAD)
            power = (t - n // 2) / (WINDOW // 2)
            scale = base_scale[None, :] ** power[:, None]
            scale = jnp.concatenate([scale, scale], -1)
            return (freqs, scale)

        def local_attention(q, k, v):
            b, h, n, d = q.shape
            w = WINDOW
            nw = n // w
            bq = q.reshape(b, h, nw, w, d)
            bk = k.reshape(b, h, nw, w, d)
            bv = v.reshape(b, h, nw, w, d)

            def look(t):
                p = jnp.pad(t, ((0, 0), (0, 0), (1, 0), (0, 0), (0, 0)))
                return jnp.concatenate([p[:, :, :nw], p[:, :, 1:]], axis=3)
            bk2, bv2 = (look(bk), look(bv))
            seq = jnp.arange(n).reshape(nw, w)
            seq_p = jnp.pad(seq, ((1, 0), (0, 0)), constant_values=-1)
            jt = jnp.concatenate([seq_p[:nw], seq_p[1:]], axis=1)
            it = seq[:, :, None]
            jb = jt[:, None, :]
            mask = (it < jb) | (it > jb + w) | (jb == -1)
            sim = jnp.einsum('bhwie,bhwje->bhwij', bq, bk2) * QK_SCALE
            sim = jnp.where(mask, -jnp.finfo(sim.dtype).max, sim)
            attn = jax.nn.softmax(sim, -1)
            out = jnp.einsum('bhwij,bhwje->bhwie', attn, bv2)
            return out.reshape(b, h, n, d)

        def attn_layer(x, Wqkv, qs, ksc, Wo):
            b, n, _ = x.shape
            qkv = x @ Wqkv
            q, k, v = jnp.split(qkv, 3, -1)
            sh = lambda t: t.reshape(b, n, HEADS, DIM_HEAD).transpose(0, 2, 1, 3)
            q, k, v = (sh(q), sh(k), sh(v))
            q = l2norm(q) * qs
            k = l2norm(k) * ksc
            freqs, scale = rotary_tables(n)
            cos, sin = (jnp.cos(freqs), jnp.sin(freqs))
            q = q * cos * scale + rotate_half(q) * sin * scale
            inv = 1.0 / scale
            k = k * cos * inv + rotate_half(k) * sin * inv
            out = local_attention(q, k, v)
            out = out.transpose(0, 2, 1, 3).reshape(b, n, INNER)
            return out @ Wo

        def ffn_layer(x, g, bln, W1, b1, W2, b2):
            mu = x.mean(-1, keepdims=True)
            var = ((x - mu) ** 2).mean(-1, keepdims=True)
            xn = (x - mu) / jnp.sqrt(var + 1e-05) * g + bln
            hg = xn @ W1 + b1
            a, gate = jnp.split(hg, 2, -1)
            return a * jax.nn.gelu(gate, approximate=False) @ W2 + b2
        key = jax.random.key(seed)
        ks = jax.random.split(key, 8)
        B, N = (2, 256)
        init = lambda k, shape: jax.random.normal(k, shape, jnp.float32) * 0.02
        return {'x': jax.random.normal(ks[0], (B, N, DIM), jnp.float32), 'Wqkv': init(ks[1], (DEPTH, DIM, 3 * INNER)), 'q_scale': jnp.ones((DEPTH, DIM_HEAD), jnp.float32), 'k_scale': jnp.ones((DEPTH, DIM_HEAD), jnp.float32), 'Wo': init(ks[2], (DEPTH, INNER, DIM)), 'ln_g': jnp.ones((DEPTH, DIM), jnp.float32), 'ln_b': jnp.zeros((DEPTH, DIM), jnp.float32), 'W1': init(ks[3], (DEPTH, DIM, 2 * DIM_INNER)), 'b1': jnp.zeros((DEPTH, 2 * DIM_INNER), jnp.float32), 'W2': init(ks[4], (DEPTH, DIM_INNER, DIM)), 'b2': jnp.zeros((DEPTH, DIM), jnp.float32)}
    _L0_ffn_in = _L0_ffn_setup()

    def _L1_attn_setup():
        import jax, jax.numpy as jnp
        import numpy as np
        HEADS = 16
        THETA = 10000.0

        def _rope(x):
            b, n, d = x.shape
            half = d // 2
            inv_freq = 1.0 / THETA ** (jnp.arange(0, d, 2, dtype=jnp.float32) / d)
            ang = jnp.arange(n, dtype=jnp.float32)[:, None] * inv_freq
            cos, sin = (jnp.cos(ang), jnp.sin(ang))
            xp = x.reshape(b, n, half, 2)
            x1, x2 = (xp[..., 0], xp[..., 1])
            out = jnp.stack([x1 * cos - x2 * sin, x2 * cos + x1 * sin], axis=-1)
            return out.reshape(b, n, d)
        key = jax.random.key(seed)
        ks = jax.random.split(key, 8)
        B, N, C = (8, 256, 128)
        s = C ** (-0.5)
        return {'x': jax.random.normal(ks[0], (B, N, C), jnp.float32), 'Wq': jax.random.normal(ks[1], (C, C), jnp.float32) * s, 'bq': jax.random.normal(ks[2], (C,), jnp.float32) * 0.01, 'Wk': jax.random.normal(ks[3], (C, C), jnp.float32) * s, 'bk': jax.random.normal(ks[4], (C,), jnp.float32) * 0.01, 'Wv': jax.random.normal(ks[5], (C, C), jnp.float32) * s, 'bv': jax.random.normal(ks[6], (C,), jnp.float32) * 0.01, 'gamma': jnp.ones((C,), jnp.float32), 'beta': jnp.zeros((C,), jnp.float32)}
    _L1_attn_in = _L1_attn_setup()

    def _L1_ffn_setup():
        import math
        import jax, jax.numpy as jnp
        import numpy as np
        D_MODEL = 128
        D_FF = 512
        N_EXPERTS = 8
        CAPACITY_FACTOR = 1.25
        L, B = (64, 8)

        def _route(tokens, router_w):
            T = tokens.shape[0]
            E = router_w.shape[0]
            capacity = int(math.ceil(T / E * CAPACITY_FACTOR))
            logits = tokens @ router_w.T
            probs = jax.nn.softmax(logits, axis=-1)
            top1_idx = jnp.argmax(probs, axis=-1)
            top1_prob = jnp.max(probs, axis=-1)
            order = jnp.lexsort((-top1_prob, top1_idx))
            sorted_e = top1_idx[order]
            counts = jnp.bincount(top1_idx, length=E)
            start = jnp.cumsum(counts) - counts
            pos_in_group = jnp.arange(T) - start[sorted_e]
            keep_sorted = pos_in_group < capacity
            keep = jnp.zeros((T,), bool).at[order].set(keep_sorted)
            return jnp.where(keep, top1_idx, 0).astype(jnp.int32)
        key = jax.random.key(seed)
        ks = jax.random.split(key, 6)
        s_in = 1.0 / math.sqrt(D_MODEL)
        s_ff = 1.0 / math.sqrt(D_FF)
        return {'x': jax.random.normal(ks[0], (L, B, D_MODEL), dtype=jnp.float32), 'router_w': jax.random.uniform(ks[1], (N_EXPERTS, D_MODEL), minval=-s_in, maxval=s_in), 'W1': jax.random.uniform(ks[2], (N_EXPERTS, D_MODEL, D_FF), minval=-s_in, maxval=s_in), 'b1': jax.random.uniform(ks[3], (N_EXPERTS, D_FF), minval=-s_in, maxval=s_in), 'W2': jax.random.uniform(ks[4], (N_EXPERTS, D_FF, D_MODEL), minval=-s_ff, maxval=s_ff), 'b2': jax.random.uniform(ks[5], (N_EXPERTS, D_MODEL), minval=-s_ff, maxval=s_ff)}
    _L1_ffn_in = _L1_ffn_setup()

    def _L2_attn_setup():
        import jax, jax.numpy as jnp
        import numpy as np
        N_EMBD = 128
        N_HEAD = 16
        HEAD_SIZE = 64
        LN_EPS = 0.001
        key = jax.random.key(seed)
        ks = jax.random.split(key, 7)
        B, S, D, H, E = (4, 256, N_EMBD, N_HEAD, HEAD_SIZE)
        x = jax.random.normal(ks[0], (B, S, D), dtype=jnp.float32)
        scale = 1.0 / np.sqrt(D)
        Wq = jax.random.normal(ks[1], (H, D, E), dtype=jnp.float32) * scale
        Wk = jax.random.normal(ks[2], (H, D, E), dtype=jnp.float32) * scale
        Wv = jax.random.normal(ks[3], (H, D, E), dtype=jnp.float32) * scale
        Wo = jax.random.normal(ks[4], (H * E, D), dtype=jnp.float32) * scale
        gamma = jnp.ones((D,), dtype=jnp.float32)
        beta = jnp.zeros((D,), dtype=jnp.float32)
        return {'x': x, 'Wq': Wq, 'Wk': Wk, 'Wv': Wv, 'Wo': Wo, 'gamma': gamma, 'beta': beta}
    _L2_attn_in = _L2_attn_setup()

    def _L2_ffn_setup():
        import jax, jax.numpy as jnp
        import numpy as np
        from functools import partial
        DIM = 128
        LIGHT_HID = 64
        HEAVY_HID = 512
        NUM_HEAVY = 128
        N_ITERS = 50
        K_ROUTE = 8.0
        EPS = 0.1

        def rms_norm(x, gamma):
            norm = jnp.linalg.norm(x, axis=-1, keepdims=True)
            normed = x / jnp.maximum(norm, 1e-12)
            return normed * x.shape[-1] ** 0.5 * gamma

        def ffn(x, gamma, w1, b1, w2, b2):
            h = rms_norm(x, gamma)
            h = jax.nn.gelu(h @ w1 + b1, approximate=False)
            return h @ w2 + b2

        def coor_descent_route(x, routing_token, num_tokens):
            s = jnp.einsum('bnd,d->bn', x, routing_token)
            constant = EPS * jnp.log(jnp.asarray(K_ROUTE, dtype=s.dtype))
            b0 = -jax.nn.relu(s)
            a0 = jnp.zeros((s.shape[0], 1), dtype=s.dtype)

            def step(carry, _):
                a_prev, b = carry
                a = constant - EPS * jax.nn.logsumexp((s + b) / EPS, axis=-1, keepdims=True)
                b = -jax.nn.relu(s + a)
                return ((a, b), None)
            (a, b), _ = jax.lax.scan(step, (a0, b0), None, length=N_ITERS)
            scores = jnp.exp((s + a + b) / EPS)
            sel_scores, sel_idx = jax.lax.top_k(scores, num_tokens)
            sel_scores = sel_scores + jax.lax.stop_gradient(1.0 - sel_scores)
            return (sel_scores, sel_idx)
        key = jax.random.key(seed)
        ks = jax.random.split(key, 12)

        def lin(k, fan_in, fan_out):
            lim = 1.0 / np.sqrt(fan_in)
            kw, kb = jax.random.split(k)
            w = jax.random.uniform(kw, (fan_in, fan_out), jnp.float32, -lim, lim)
            b = jax.random.uniform(kb, (fan_out,), jnp.float32, -lim, lim)
            return (w, b)
        x = jax.random.normal(ks[0], (4, 1024, DIM), jnp.float32)
        routing_token = jax.random.normal(ks[1], (DIM,), jnp.float32)
        gamma_light = jnp.ones((DIM,), jnp.float32)
        w1_l, b1_l = lin(ks[2], DIM, LIGHT_HID)
        w2_l, b2_l = lin(ks[3], LIGHT_HID, DIM)
        gamma_heavy = jnp.ones((DIM,), jnp.float32)
        w1_h, b1_h = lin(ks[4], DIM, HEAVY_HID)
        w2_h, b2_h = lin(ks[5], HEAVY_HID, DIM)
        return dict(x=x, routing_token=routing_token, gamma_light=gamma_light, w1_light=w1_l, b1_light=b1_l, w2_light=w2_l, b2_light=b2_l, gamma_heavy=gamma_heavy, w1_heavy=w1_h, b1_heavy=b1_h, w2_heavy=w2_h, b2_heavy=b2_h)
    _L2_ffn_in = _L2_ffn_setup()

    def _L3_attn_setup():
        import jax, jax.numpy as jnp
        import numpy as np
        NUM_HEADS = 16
        THETA = 10000.0

        def _rotate_half(x):
            x = x.reshape(x.shape[:-1] + (-1, 2))
            x1, x2 = (x[..., 0], x[..., 1])
            return jnp.stack((-x2, x1), axis=-1).reshape(x.shape[:-2] + (-1,))

        def _rope(x):
            d_k = x.shape[-1]
            seq_len = x.shape[-2]
            inv_freq = 1.0 / THETA ** (jnp.arange(0, d_k, 2, dtype=jnp.float32) / d_k)
            pos = jnp.arange(seq_len, dtype=jnp.float32)
            theta = pos[:, None] * inv_freq[None, :]
            cos = jnp.repeat(jnp.cos(theta), 2, axis=-1)
            sin = jnp.repeat(jnp.sin(theta), 2, axis=-1)
            return x * cos + _rotate_half(x) * sin
        key = jax.random.key(seed)
        kx, kq, kk, kv, ko = jax.random.split(key, 5)
        B, S, D = (2, 256, 128)
        std = 1.0 / (2.0 * (2 * D) ** 0.5)
        return {'x': jax.random.normal(kx, (B, S, D), dtype=jnp.float32), 'Wq': jax.random.normal(kq, (D, D), dtype=jnp.float32) * std, 'Wk': jax.random.normal(kk, (D, D), dtype=jnp.float32) * std, 'Wv': jax.random.normal(kv, (D, D), dtype=jnp.float32) * std, 'Wo': jax.random.normal(ko, (D, D), dtype=jnp.float32) * std}
    _L3_attn_in = _L3_attn_setup()

    def _L3_ffn_setup():
        import jax, jax.numpy as jnp
        import numpy as np
        NUM_GEMMS = 8
        HIDDEN = 128
        INTER = 512
        key = jax.random.key(seed)
        k_x, k_w1, k_b1, k_w2, k_b2 = jax.random.split(key, 5)
        x = jax.random.normal(k_x, (8, 256, HIDDEN), dtype=jnp.float32)
        s1 = 1.0 / np.sqrt(HIDDEN)
        s2 = 1.0 / np.sqrt(INTER)
        W1 = jax.random.uniform(k_w1, (NUM_GEMMS, INTER, HIDDEN), jnp.float32, -s1, s1)
        b1 = jax.random.uniform(k_b1, (NUM_GEMMS, INTER), jnp.float32, -s1, s1)
        W2 = jax.random.uniform(k_w2, (NUM_GEMMS, HIDDEN, INTER), jnp.float32, -s2, s2)
        b2 = jax.random.uniform(k_b2, (NUM_GEMMS, HIDDEN), jnp.float32, -s2, s2)
        return {'x': x, 'W1': W1, 'b1': b1, 'W2': W2, 'b2': b2}
    _L3_ffn_in = _L3_ffn_setup()
    _d = {'L0_attn_x': _L0_attn_in['x'], 'L0_attn_wq': _L0_attn_in['wq'], 'L0_attn_bq': _L0_attn_in['bq'], 'L0_attn_wk': _L0_attn_in['wk'], 'L0_attn_bk': _L0_attn_in['bk'], 'L0_attn_wv': _L0_attn_in['wv'], 'L0_attn_bv': _L0_attn_in['bv'], 'L0_attn_wo': _L0_attn_in['wo'], 'L0_attn_bo': _L0_attn_in['bo'], 'L0_ffn_Wqkv': _L0_ffn_in['Wqkv'], 'L0_ffn_q_scale': _L0_ffn_in['q_scale'], 'L0_ffn_k_scale': _L0_ffn_in['k_scale'], 'L0_ffn_Wo': _L0_ffn_in['Wo'], 'L0_ffn_ln_g': _L0_ffn_in['ln_g'], 'L0_ffn_ln_b': _L0_ffn_in['ln_b'], 'L0_ffn_W1': _L0_ffn_in['W1'], 'L0_ffn_b1': _L0_ffn_in['b1'], 'L0_ffn_W2': _L0_ffn_in['W2'], 'L0_ffn_b2': _L0_ffn_in['b2'], 'L1_attn_Wq': _L1_attn_in['Wq'], 'L1_attn_bq': _L1_attn_in['bq'], 'L1_attn_Wk': _L1_attn_in['Wk'], 'L1_attn_bk': _L1_attn_in['bk'], 'L1_attn_Wv': _L1_attn_in['Wv'], 'L1_attn_bv': _L1_attn_in['bv'], 'L1_attn_gamma': _L1_attn_in['gamma'], 'L1_attn_beta': _L1_attn_in['beta'], 'L1_ffn_router_w': _L1_ffn_in['router_w'], 'L1_ffn_W1': _L1_ffn_in['W1'], 'L1_ffn_b1': _L1_ffn_in['b1'], 'L1_ffn_W2': _L1_ffn_in['W2'], 'L1_ffn_b2': _L1_ffn_in['b2'], 'L2_attn_Wq': _L2_attn_in['Wq'], 'L2_attn_Wk': _L2_attn_in['Wk'], 'L2_attn_Wv': _L2_attn_in['Wv'], 'L2_attn_Wo': _L2_attn_in['Wo'], 'L2_attn_gamma': _L2_attn_in['gamma'], 'L2_attn_beta': _L2_attn_in['beta'], 'L2_ffn_routing_token': _L2_ffn_in['routing_token'], 'L2_ffn_gamma_light': _L2_ffn_in['gamma_light'], 'L2_ffn_w1_light': _L2_ffn_in['w1_light'], 'L2_ffn_b1_light': _L2_ffn_in['b1_light'], 'L2_ffn_w2_light': _L2_ffn_in['w2_light'], 'L2_ffn_b2_light': _L2_ffn_in['b2_light'], 'L2_ffn_gamma_heavy': _L2_ffn_in['gamma_heavy'], 'L2_ffn_w1_heavy': _L2_ffn_in['w1_heavy'], 'L2_ffn_b1_heavy': _L2_ffn_in['b1_heavy'], 'L2_ffn_w2_heavy': _L2_ffn_in['w2_heavy'], 'L2_ffn_b2_heavy': _L2_ffn_in['b2_heavy'], 'L3_attn_Wq': _L3_attn_in['Wq'], 'L3_attn_Wk': _L3_attn_in['Wk'], 'L3_attn_Wv': _L3_attn_in['Wv'], 'L3_attn_Wo': _L3_attn_in['Wo'], 'L3_ffn_W1': _L3_ffn_in['W1'], 'L3_ffn_b1': _L3_ffn_in['b1'], 'L3_ffn_W2': _L3_ffn_in['W2'], 'L3_ffn_b2': _L3_ffn_in['b2']}
    _x0 = _d['L0_attn_x']
    _d['L0_attn_x'] = jax.random.normal(jax.random.fold_in(jax.random.key(seed), 1), (16, 256, 128), dtype=_x0.dtype)
    del _x0
    return _d

def reference(L0_attn_x, L0_attn_wq, L0_attn_bq, L0_attn_wk, L0_attn_bk, L0_attn_wv, L0_attn_bv, L0_attn_wo, L0_attn_bo, L0_ffn_Wqkv, L0_ffn_q_scale, L0_ffn_k_scale, L0_ffn_Wo, L0_ffn_ln_g, L0_ffn_ln_b, L0_ffn_W1, L0_ffn_b1, L0_ffn_W2, L0_ffn_b2, L1_attn_Wq, L1_attn_bq, L1_attn_Wk, L1_attn_bk, L1_attn_Wv, L1_attn_bv, L1_attn_gamma, L1_attn_beta, L1_ffn_router_w, L1_ffn_W1, L1_ffn_b1, L1_ffn_W2, L1_ffn_b2, L2_attn_Wq, L2_attn_Wk, L2_attn_Wv, L2_attn_Wo, L2_attn_gamma, L2_attn_beta, L2_ffn_routing_token, L2_ffn_gamma_light, L2_ffn_w1_light, L2_ffn_b1_light, L2_ffn_w2_light, L2_ffn_b2_light, L2_ffn_gamma_heavy, L2_ffn_w1_heavy, L2_ffn_b1_heavy, L2_ffn_w2_heavy, L2_ffn_b2_heavy, L3_attn_Wq, L3_attn_Wk, L3_attn_Wv, L3_attn_Wo, L3_ffn_W1, L3_ffn_b1, L3_ffn_W2, L3_ffn_b2):

    def _L0_attn_ref(x, wq, bq, wk, bk, wv, bv, wo, bo):
        import jax, jax.numpy as jnp
        import numpy as np
        B, T, E, H = (2, 512, 128, 16)
        D = E // H
        EPS = 1e-06

        def _feature_map(x):
            return jnp.where(x > 0, x + 1.0, jnp.exp(x))
        b, t, e = x.shape
        q = _feature_map(x @ wq + bq).reshape(b, t, H, D)
        k = _feature_map(x @ wk + bk).reshape(b, t, H, D)
        v = (x @ wv + bv).reshape(b, t, H, D)
        qT = jnp.moveaxis(q, 1, 0)
        kT = jnp.moveaxis(k, 1, 0)
        vT = jnp.moveaxis(v, 1, 0)
        S0 = jnp.zeros((b, H, D, D), dtype=x.dtype)
        z0 = jnp.zeros((b, H, D), dtype=x.dtype)

        def step(carry, qkv):
            S, z = carry
            qt, kt, vt = qkv
            S = S + jnp.einsum('bhd,bhe->bhde', kt, vt)
            z = z + kt
            num = jnp.einsum('bhd,bhde->bhe', qt, S)
            den = jnp.einsum('bhd,bhd->bh', qt, z)[..., None] + EPS
            return ((S, z), num / den)
        _, outT = jax.lax.scan(step, (S0, z0), (qT, kT, vT))
        out = jnp.moveaxis(outT, 0, 1).reshape(b, t, e)
        return out @ wo + bo

    def _L0_ffn_ref(x, Wqkv, q_scale, k_scale, Wo, ln_g, ln_b, W1, b1, W2, b2):
        import jax, jax.numpy as jnp
        import numpy as np
        DIM = 128
        DEPTH = 6
        HEADS = 16
        DIM_HEAD = 64
        WINDOW = 32
        INNER = HEADS * DIM_HEAD
        DIM_INNER = int(DIM * 4 * 2 / 3)
        QK_SCALE = 8.0

        def shift_tokens(t):
            a, s = jnp.split(t, 2, -1)
            s = jnp.pad(s, ((0, 0), (1, 0), (0, 0)))[:, :-1]
            return jnp.concatenate([a, s], -1)

        def l2norm(t):
            return t / jnp.maximum(jnp.linalg.norm(t, axis=-1, keepdims=True), 1e-12)

        def rotate_half(x):
            x1, x2 = jnp.split(x, 2, -1)
            return jnp.concatenate([-x2, x1], -1)

        def rotary_tables(n):
            half = jnp.arange(0, DIM_HEAD, 2, dtype=jnp.float32)
            inv_freq = 1.0 / 10000.0 ** (half / DIM_HEAD)
            t = jnp.arange(n, dtype=jnp.float32)
            freqs = t[:, None] * inv_freq[None, :]
            freqs = jnp.concatenate([freqs, freqs], -1)
            base_scale = (half + 0.4 * DIM_HEAD) / (1.4 * DIM_HEAD)
            power = (t - n // 2) / (WINDOW // 2)
            scale = base_scale[None, :] ** power[:, None]
            scale = jnp.concatenate([scale, scale], -1)
            return (freqs, scale)

        def local_attention(q, k, v):
            b, h, n, d = q.shape
            w = WINDOW
            nw = n // w
            bq = q.reshape(b, h, nw, w, d)
            bk = k.reshape(b, h, nw, w, d)
            bv = v.reshape(b, h, nw, w, d)

            def look(t):
                p = jnp.pad(t, ((0, 0), (0, 0), (1, 0), (0, 0), (0, 0)))
                return jnp.concatenate([p[:, :, :nw], p[:, :, 1:]], axis=3)
            bk2, bv2 = (look(bk), look(bv))
            seq = jnp.arange(n).reshape(nw, w)
            seq_p = jnp.pad(seq, ((1, 0), (0, 0)), constant_values=-1)
            jt = jnp.concatenate([seq_p[:nw], seq_p[1:]], axis=1)
            it = seq[:, :, None]
            jb = jt[:, None, :]
            mask = (it < jb) | (it > jb + w) | (jb == -1)
            sim = jnp.einsum('bhwie,bhwje->bhwij', bq, bk2) * QK_SCALE
            sim = jnp.where(mask, -jnp.finfo(sim.dtype).max, sim)
            attn = jax.nn.softmax(sim, -1)
            out = jnp.einsum('bhwij,bhwje->bhwie', attn, bv2)
            return out.reshape(b, h, n, d)

        def attn_layer(x, Wqkv, qs, ksc, Wo):
            b, n, _ = x.shape
            qkv = x @ Wqkv
            q, k, v = jnp.split(qkv, 3, -1)
            sh = lambda t: t.reshape(b, n, HEADS, DIM_HEAD).transpose(0, 2, 1, 3)
            q, k, v = (sh(q), sh(k), sh(v))
            q = l2norm(q) * qs
            k = l2norm(k) * ksc
            freqs, scale = rotary_tables(n)
            cos, sin = (jnp.cos(freqs), jnp.sin(freqs))
            q = q * cos * scale + rotate_half(q) * sin * scale
            inv = 1.0 / scale
            k = k * cos * inv + rotate_half(k) * sin * inv
            out = local_attention(q, k, v)
            out = out.transpose(0, 2, 1, 3).reshape(b, n, INNER)
            return out @ Wo

        def ffn_layer(x, g, bln, W1, b1, W2, b2):
            mu = x.mean(-1, keepdims=True)
            var = ((x - mu) ** 2).mean(-1, keepdims=True)
            xn = (x - mu) / jnp.sqrt(var + 1e-05) * g + bln
            hg = xn @ W1 + b1
            a, gate = jnp.split(hg, 2, -1)
            return a * jax.nn.gelu(gate, approximate=False) @ W2 + b2
        for i in range(DEPTH):
            x = attn_layer(shift_tokens(x), Wqkv[i], q_scale[i], k_scale[i], Wo[i]) + x
            x = ffn_layer(shift_tokens(x), ln_g[i], ln_b[i], W1[i], b1[i], W2[i], b2[i]) + x
        return x

    def _L1_attn_ref(x, Wq, bq, Wk, bk, Wv, bv, gamma, beta):
        import jax, jax.numpy as jnp
        import numpy as np
        HEADS = 16
        THETA = 10000.0

        def _rope(x):
            b, n, d = x.shape
            half = d // 2
            inv_freq = 1.0 / THETA ** (jnp.arange(0, d, 2, dtype=jnp.float32) / d)
            ang = jnp.arange(n, dtype=jnp.float32)[:, None] * inv_freq
            cos, sin = (jnp.cos(ang), jnp.sin(ang))
            xp = x.reshape(b, n, half, 2)
            x1, x2 = (xp[..., 0], xp[..., 1])
            out = jnp.stack([x1 * cos - x2 * sin, x2 * cos + x1 * sin], axis=-1)
            return out.reshape(b, n, d)
        b, n, c = x.shape
        h = HEADS
        d = c // h
        gelu = lambda t: jax.nn.gelu(t, approximate=False)
        q = gelu(x @ Wq.T + bq) + 0.21
        k = gelu(x @ Wk.T + bk) + 0.21
        v = x @ Wv.T + bv
        q_r = _rope(q)
        k_r = _rope(k)
        split = lambda t: t.reshape(b, n, h, d).transpose(0, 2, 1, 3)
        qh, kh, vh, qrh, krh = (split(q), split(k), split(v), split(q_r), split(k_r))
        z = 1.0 / (jnp.einsum('bhnd,bhd->bhn', qh, kh.mean(axis=2)) + 1e-06)
        scale = n ** (-0.5)
        kv = jnp.einsum('bhnd,bhne->bhde', krh * scale, vh * scale)
        out = jnp.einsum('bhnd,bhde->bhne', qrh, kv) * z[..., None]
        out = out.transpose(0, 2, 1, 3).reshape(b, n, c)
        res = out + x
        mu = res.mean(-1, keepdims=True)
        var = res.var(-1, keepdims=True)
        return (res - mu) / jnp.sqrt(var + 1e-12) * gamma + beta

    def _L1_ffn_ref(x, router_w, W1, b1, W2, b2):
        import math
        import jax, jax.numpy as jnp
        import numpy as np
        D_MODEL = 128
        D_FF = 512
        N_EXPERTS = 8
        CAPACITY_FACTOR = 1.25
        L, B = (64, 8)

        def _route(tokens, router_w):
            T = tokens.shape[0]
            E = router_w.shape[0]
            capacity = int(math.ceil(T / E * CAPACITY_FACTOR))
            logits = tokens @ router_w.T
            probs = jax.nn.softmax(logits, axis=-1)
            top1_idx = jnp.argmax(probs, axis=-1)
            top1_prob = jnp.max(probs, axis=-1)
            order = jnp.lexsort((-top1_prob, top1_idx))
            sorted_e = top1_idx[order]
            counts = jnp.bincount(top1_idx, length=E)
            start = jnp.cumsum(counts) - counts
            pos_in_group = jnp.arange(T) - start[sorted_e]
            keep_sorted = pos_in_group < capacity
            keep = jnp.zeros((T,), bool).at[order].set(keep_sorted)
            return jnp.where(keep, top1_idx, 0).astype(jnp.int32)
        Lx, Bx, D = x.shape
        T = Lx * Bx
        E = router_w.shape[0]
        tokens = x.reshape(T, D)
        final_e = _route(tokens, router_w)
        out = jnp.zeros_like(tokens)
        for e in range(E):
            h = jax.nn.relu(tokens @ W1[e] + b1[e])
            y = h @ W2[e] + b2[e]
            out = out + jnp.where((final_e == e)[:, None], y, 0.0)
        return out.reshape(Lx, Bx, D)

    def _L2_attn_ref(x, Wq, Wk, Wv, Wo, gamma, beta):
        import jax, jax.numpy as jnp
        import numpy as np
        N_EMBD = 128
        N_HEAD = 16
        HEAD_SIZE = 64
        LN_EPS = 0.001
        B, S, D = x.shape
        H, _, E = Wq.shape
        q = jnp.einsum('bsd,hde->bhse', x, Wq)
        k = jnp.einsum('bsd,hde->bhse', x, Wk)
        v = jnp.einsum('bsd,hde->bhse', x, Wv)
        scores = jnp.einsum('bhse,bhte->bhst', q, k)
        causal = jnp.tril(jnp.ones((S, S), dtype=bool))
        scores = jnp.where(causal, scores / jnp.sqrt(jnp.float32(E)), jnp.float32(-jnp.inf))
        attn = jax.nn.softmax(scores, axis=-1)
        out = jnp.einsum('bhst,bhte->bhse', attn, v)
        heads = out.transpose(0, 2, 1, 3).reshape(B, S, H * E)
        y = x + heads @ Wo
        mu = jnp.mean(y, axis=-1, keepdims=True)
        var = jnp.mean(jnp.square(y - mu), axis=-1, keepdims=True)
        y = (y - mu) * jax.lax.rsqrt(var + LN_EPS) * gamma + beta
        return y

    def _L2_ffn_ref(x, routing_token, gamma_light, w1_light, b1_light, w2_light, b2_light, gamma_heavy, w1_heavy, b1_heavy, w2_heavy, b2_heavy):
        import jax, jax.numpy as jnp
        import numpy as np
        from functools import partial
        DIM = 128
        LIGHT_HID = 64
        HEAVY_HID = 512
        NUM_HEAVY = 128
        N_ITERS = 50
        K_ROUTE = 8.0
        EPS = 0.1

        def rms_norm(x, gamma):
            norm = jnp.linalg.norm(x, axis=-1, keepdims=True)
            normed = x / jnp.maximum(norm, 1e-12)
            return normed * x.shape[-1] ** 0.5 * gamma

        def ffn(x, gamma, w1, b1, w2, b2):
            h = rms_norm(x, gamma)
            h = jax.nn.gelu(h @ w1 + b1, approximate=False)
            return h @ w2 + b2

        def coor_descent_route(x, routing_token, num_tokens):
            s = jnp.einsum('bnd,d->bn', x, routing_token)
            constant = EPS * jnp.log(jnp.asarray(K_ROUTE, dtype=s.dtype))
            b0 = -jax.nn.relu(s)
            a0 = jnp.zeros((s.shape[0], 1), dtype=s.dtype)

            def step(carry, _):
                a_prev, b = carry
                a = constant - EPS * jax.nn.logsumexp((s + b) / EPS, axis=-1, keepdims=True)
                b = -jax.nn.relu(s + a)
                return ((a, b), None)
            (a, b), _ = jax.lax.scan(step, (a0, b0), None, length=N_ITERS)
            scores = jnp.exp((s + a + b) / EPS)
            sel_scores, sel_idx = jax.lax.top_k(scores, num_tokens)
            sel_scores = sel_scores + jax.lax.stop_gradient(1.0 - sel_scores)
            return (sel_scores, sel_idx)
        bsz = x.shape[0]
        light_out = ffn(x, gamma_light, w1_light, b1_light, w2_light, b2_light)
        sel_scores, sel_idx = coor_descent_route(x, routing_token, NUM_HEAVY)
        batch_range = jnp.arange(bsz)[:, None]
        routed = x[batch_range, sel_idx]
        routed_out = ffn(routed, gamma_heavy, w1_heavy, b1_heavy, w2_heavy, b2_heavy)
        routed_out = routed_out * sel_scores[..., None]
        heavy_out = jnp.zeros_like(x).at[batch_range, sel_idx].set(routed_out)
        return light_out + heavy_out

    def _L3_attn_ref(x, Wq, Wk, Wv, Wo):
        import jax, jax.numpy as jnp
        import numpy as np
        NUM_HEADS = 16
        THETA = 10000.0

        def _rotate_half(x):
            x = x.reshape(x.shape[:-1] + (-1, 2))
            x1, x2 = (x[..., 0], x[..., 1])
            return jnp.stack((-x2, x1), axis=-1).reshape(x.shape[:-2] + (-1,))

        def _rope(x):
            d_k = x.shape[-1]
            seq_len = x.shape[-2]
            inv_freq = 1.0 / THETA ** (jnp.arange(0, d_k, 2, dtype=jnp.float32) / d_k)
            pos = jnp.arange(seq_len, dtype=jnp.float32)
            theta = pos[:, None] * inv_freq[None, :]
            cos = jnp.repeat(jnp.cos(theta), 2, axis=-1)
            sin = jnp.repeat(jnp.sin(theta), 2, axis=-1)
            return x * cos + _rotate_half(x) * sin
        B, S, D = x.shape
        H = NUM_HEADS
        d_k = D // H

        def split_heads(t):
            return t.reshape(B, S, H, d_k).transpose(0, 2, 1, 3)
        Q = split_heads(x @ Wq)
        K = split_heads(x @ Wk)
        V = split_heads(x @ Wv)
        Q = _rope(Q)
        K = _rope(K)
        scores = jnp.einsum('bhqd,bhkd->bhqk', Q, K) / jnp.sqrt(jnp.float32(d_k))
        causal = jnp.tril(jnp.ones((S, S), dtype=bool))
        scores = jnp.where(causal[None, None], scores, -jnp.inf)
        attn = jax.nn.softmax(scores, axis=-1)
        out = jnp.einsum('bhqk,bhkd->bhqd', attn, V)
        out = out.transpose(0, 2, 1, 3).reshape(B, S, D)
        return out @ Wo

    def _L3_ffn_ref(x, W1, b1, W2, b2):
        import jax, jax.numpy as jnp
        import numpy as np
        NUM_GEMMS = 8
        HIDDEN = 128
        INTER = 512
        orig_shape = x.shape
        token_num = int(np.prod(orig_shape[:-1]))
        m = token_num // NUM_GEMMS
        xg = x.reshape(NUM_GEMMS, m, HIDDEN)
        h1 = jnp.einsum('gmh,goh->gmo', xg, W1) + b1[:, None, :]
        h2 = jnp.einsum('gmo,gho->gmh', h1, W2) + b2[:, None, :]
        return h2.reshape(orig_shape)
    x = L0_attn_x
    xn = _layernorm(x, axis=-1)
    s = _L0_attn_ref(xn, L0_attn_wq, L0_attn_bq, L0_attn_wk, L0_attn_bk, L0_attn_wv, L0_attn_bv, L0_attn_wo, L0_attn_bo)
    g = _silu(_L0_ffn_ref(xn, L0_ffn_Wqkv, L0_ffn_q_scale, L0_ffn_k_scale, L0_ffn_Wo, L0_ffn_ln_g, L0_ffn_ln_b, L0_ffn_W1, L0_ffn_b1, L0_ffn_W2, L0_ffn_b2))
    x = x + s * g
    xn = _layernorm(x, axis=-1)
    s = _L1_attn_ref(xn, L1_attn_Wq, L1_attn_bq, L1_attn_Wk, L1_attn_bk, L1_attn_Wv, L1_attn_bv, L1_attn_gamma, L1_attn_beta)
    g = _silu(_L1_ffn_ref(xn, L1_ffn_router_w, L1_ffn_W1, L1_ffn_b1, L1_ffn_W2, L1_ffn_b2))
    x = x + s * g
    xn = _layernorm(x, axis=-1)
    s = _L2_attn_ref(xn, L2_attn_Wq, L2_attn_Wk, L2_attn_Wv, L2_attn_Wo, L2_attn_gamma, L2_attn_beta)
    g = _silu(_L2_ffn_ref(xn, L2_ffn_routing_token, L2_ffn_gamma_light, L2_ffn_w1_light, L2_ffn_b1_light, L2_ffn_w2_light, L2_ffn_b2_light, L2_ffn_gamma_heavy, L2_ffn_w1_heavy, L2_ffn_b1_heavy, L2_ffn_w2_heavy, L2_ffn_b2_heavy))
    x = x + s * g
    xn = _layernorm(x, axis=-1)
    s = _L3_attn_ref(xn, L3_attn_Wq, L3_attn_Wk, L3_attn_Wv, L3_attn_Wo)
    g = _silu(_L3_ffn_ref(xn, L3_ffn_W1, L3_ffn_b1, L3_ffn_W2, L3_ffn_b2))
    x = x + s * g
    return x

_drawn_inputs = setup_inputs


def setup_inputs(seed=0):
    import zlib

    import numpy as np

    out = dict(_drawn_inputs(seed))
    spreads = {'L0_ffn_q_scale': (1.0, 0.6),
     'L0_ffn_k_scale': (1.0, 0.6),
     'L0_ffn_ln_g': (1.0, 0.6),
     'L0_ffn_ln_b': (0.0, 0.8),
     'L0_ffn_b1': (0.0, 0.8),
     'L0_ffn_b2': (0.0, 0.3),
     'L1_attn_gamma': (1.0, 0.6),
     'L1_attn_beta': (0.0, 2.0),
     'L2_attn_gamma': (1.0, 0.6),
     'L2_attn_beta': (0.0, 2.0),
     'L2_ffn_gamma_light': (1.0, 0.6),
     'L2_ffn_gamma_heavy': (1.0, 0.6)}
    factors = {'L0_attn_wq': 8.0,
     'L0_attn_bq': 8.0,
     'L0_attn_wk': 4.432,
     'L0_attn_bk': 8.0,
     'L0_ffn_Wqkv': 3.725,
     'L0_ffn_Wo': 3.807,
     'L0_ffn_W1': 8.0,
     'L0_ffn_W2': 8.0,
     'L1_attn_Wq': 56.256,
     'L1_attn_bq': 178.298,
     'L1_attn_Wk': 54.448,
     'L1_attn_bk': 64.0,
     'L1_attn_Wv': 17.678,
     'L1_attn_bv': 64.0,
     'L1_ffn_b1': 34.472,
     'L1_ffn_b2': 28.056,
     'L2_ffn_b1_light': 49.24,
     'L2_ffn_b1_heavy': 64.0,
     'L2_ffn_b2_heavy': 49.48,
     'L3_attn_Wq': 8.0,
     'L3_attn_Wk': 8.0,
     'L3_attn_Wv': 8.0,
     'L3_attn_Wo': 8.0,
     'L3_ffn_W1': 8.0,
     'L3_ffn_b1': 8.0,
     'L3_ffn_W2': 8.0,
     'L3_ffn_b2': 52.145,
     'L1_ffn_router_w': 3.543,
     'L1_ffn_W1': 4.77,
     'L1_ffn_W2': 3.714,
     'L2_attn_Wq': 8.0,
     'L2_attn_Wk': 8.0,
     'L2_attn_Wv': 3.297,
     'L2_attn_Wo': 3.283,
     'L2_ffn_routing_token': 5.383,
     'L2_ffn_w1_light': 3.508,
     'L2_ffn_w2_light': 3.441,
     'L2_ffn_b2_light': 8.0,
     'L2_ffn_w1_heavy': 4.409,
     'L2_ffn_w2_heavy': 3.538}
    for name, (base, spread) in spreads.items():
        noise = np.random.default_rng([zlib.crc32(name.encode()), seed]).standard_normal(out[name].shape)
        drawn = base * np.exp(spread * noise) if base else spread * noise
        out[name] = jnp.asarray(drawn.astype(out[name].dtype))
    for name, factor in factors.items():
        out[name] = (out[name] * factor).astype(out[name].dtype)
    return out
```

```python
from contextlib import ExitStack, contextmanager

import numpy as np

import concourse.bass as bass
from concourse import mybir

F32 = mybir.dt.float32
I32 = mybir.dt.int32
BF16 = mybir.dt.bfloat16
ALU = mybir.AluOpType
ACT = mybir.ActivationFunctionType
AX = mybir.AxisListType

P = 128
NB, SEQ = 16, 256
TPB = SEQ // P
NT = NB * TPB
TOK = NB * SEQ
HEADS = 16
NEG = -1.0e20
LOWEST = -3.0e38

DEPTH, DH, WINDOW = 6, 64, 32
INNER = HEADS * DH
DIM_INNER = int(P * 4 * 2 / 3)
HID_CHUNKS = [(0, 128), (128, 128), (256, DIM_INNER - 256)]
QK_SCALE = 8.0
NE, DFF = 8, 512
CAPACITY = int(np.ceil(TOK / NE * 1.25))
ROUTE_ITERS, EPS_ROUTE, K_ROUTE, NUM_HEAVY = 50, 0.1, 8.0, 128
LIGHT, HEAVY = 64, 512
NG, INTER = 8, 512
GTOK = TOK // NG


def shape_constants():
    c = {}
    i = np.arange(P)
    c["ident"] = np.eye(P, dtype=np.float32)
    c["upto"] = (i[:, None] <= i[None, :]).astype(np.float32)
    causal = np.full((P, TPB, SEQ), NEG, np.float32)
    local = np.full((P, TPB, SEQ), NEG, np.float32)
    for t in range(TPB):
        q = t * P + i
        k = np.arange(SEQ)
        causal[:, t][k[None, :] <= q[:, None]] = 0.0
        first = local_first_key(t)
        w = local_width(t)
        kk = first + np.arange(w)
        ok = (kk[None, :] <= q[:, None]) & (q[:, None] <= kk[None, :] + WINDOW)
        ok &= (kk[None, :] // WINDOW) >= (q[:, None] // WINDOW - 1)
        local[:, t, :w][ok] = 0.0
    c["mask_causal"], c["mask_local"] = causal, local
    half = np.arange(0, DH, 2, dtype=np.float32)
    inv_freq = (np.float32(1.0) / np.float32(10000.0) ** (half / np.float32(DH))).astype(np.float32)
    t = np.arange(SEQ, dtype=np.float32)
    freqs = (t[:, None] * inv_freq[None, :]).astype(np.float32)
    freqs = np.concatenate([freqs, freqs], -1)
    base = ((half + np.float32(0.4 * DH)) / np.float32(1.4 * DH)).astype(np.float32)
    power = ((t - SEQ // 2) / np.float32(WINDOW // 2)).astype(np.float32)
    scale = (base[None, :] ** power[:, None]).astype(np.float32)
    scale = np.concatenate([scale, scale], -1)
    sign = np.where(np.arange(DH) < DH // 2, -1.0, 1.0).astype(np.float32)
    cos, sin = np.cos(freqs), np.sin(freqs) * sign
    inv = (np.float32(1.0) / scale).astype(np.float32)
    tab = np.stack([cos * scale, sin * scale, cos * inv, sin * inv], 1)
    c["rope_local"] = np.ascontiguousarray(tab.reshape(TPB, P, 4, DH).transpose(1, 0, 2, 3)).astype(np.float32)
    for name, d in (("rope_l1", P), ("rope_l3", 8)):
        f = (np.float32(1.0) / np.float32(10000.0) ** (np.arange(0, d, 2, dtype=np.float32) / np.float32(d))).astype(np.float32)
        ang = (t[:, None] * f[None, :]).astype(np.float32)
        both = np.stack([np.repeat(np.cos(ang), 2, 1), np.repeat(np.sin(ang), 2, 1)], 0)
        c[name] = np.ascontiguousarray(np.tile(both, (1, 1, P // d)).transpose(2, 0, 1)).astype(np.float32)
    swap = np.zeros((P, P), np.float32)
    swap[np.arange(1, P, 2), np.arange(0, P, 2)] = -1.0
    swap[np.arange(0, P, 2), np.arange(1, P, 2)] = 1.0
    c["swap"] = swap
    c["strictly_before"] = (i[:, None] < i[None, :]).astype(np.float32)
    c["head_block"] = (i[:, None] // 8 == i[None, :] // 8).astype(np.float32)
    c["head_of_4"] = (((i[:, None] // 8) % 4) == np.arange(4)[None, :]).astype(np.float32)
    before = np.arange(SEQ)[None, None, :] < (np.arange(TPB)[None, :, None] * P + i[:, None, None])
    c["before"] = before.astype(np.float32)
    c["expert_no"] = np.tile(np.arange(NE, dtype=np.float32), (P, NT, 1))
    return c


def local_first_key(t):
    return 0 if t == 0 else t * P - WINDOW


def local_width(t):
    return (t + 1) * P - local_first_key(t)


@contextmanager
def signals(nc, names):
    with ExitStack() as c:
        s = [c.enter_context(nc.semaphore(n)) for n in names]

        def zero():
            numbers = sorted(x.num for x in s)
            starts = [n for n in numbers if n - 1 not in numbers]
            for first in starts:
                end = first
                while end in numbers:
                    end += 1
                nc.sync.sem_clear(range(first, end))
            nc.all_engine_barrier(sem_only=True)

        zero()
        yield s, zero


def chain(eng, sem):
    n = [0]

    def after(ins):
        n[0] += 1
        ins.then_inc(sem, 1)
        eng.wait_ge(sem, n[0])

    return after


def rsqrt(nc, after, out, x, tmp):
    after(nc.vector.tensor_scalar(tmp.bitcast(I32), x.bitcast(I32), 1, None, ALU.logical_shift_right))
    after(nc.vector.tensor_scalar(out.bitcast(I32), tmp.bitcast(I32), -1.0, float(0x5F3759DF), ALU.mult, ALU.add))
    for _ in range(4):
        after(nc.vector.tensor_tensor(tmp, out, out, ALU.mult))
        after(nc.vector.tensor_tensor(tmp, tmp, x, ALU.mult))
        after(nc.vector.tensor_scalar(tmp, tmp, -0.5, 1.5, ALU.mult, ALU.add))
        after(nc.vector.tensor_tensor(out, out, tmp, ALU.mult))


class Core:

    def __init__(self, nc, dram, ctx):
        self.nc, self.dram, self.stage = nc, dram, 0

        def sb(name, shape, dt=F32):
            return ctx.enter_context(nc.sbuf_tensor(name, shape, dt))

        self.x = sb("x_rows", [P, NT, P])
        self.xn = sb("xn_rows", [P, NT, P])
        self.xnt = sb("xn_cols", [P, TOK])
        self.s = sb("s_rows", [P, NT, P])
        self.y = sb("y_rows", [P, NT, P])
        self.ident = sb("ident", [P, P])
        self.bank = [ctx.enter_context(nc.psum_tensor(f"bank{i}", [P, 512], F32)) for i in range(8)]

    def name(self, base):
        return f"{base}_{self.stage}"


def load(core, pairs):
    nc = core.nc
    with signals(nc, ["loaded"]) as ((loaded,), zero):
        with nc.Block() as block:
            @block.sync
            def _(sp):
                for dst, src in pairs:
                    sp.dma_start(dst, src).then_inc(loaded, 16)
                sp.wait_ge(loaded, 16 * len(pairs))
        zero()


def column(ap):
    return ap.rearrange("(p a) -> p a", a=1)


def spread(ap):
    return ap.rearrange("(a n) -> a n", a=1).to_broadcast([P, ap.shape[0]])


def normalise_rows(nc, after, x_tiles, out_tiles, stats, mv, rstd, tmp, eps):
    n = len(x_tiles)
    for j in range(n):
        after(nc.vector.bn_stats(stats[:, j, :], x_tiles[j]))
    for j in range(n):
        after(nc.vector.bn_aggr(mv[:, j, :], stats[:, j, :]))
    after(nc.vector.tensor_scalar(mv[:, 0:n, 1], mv[:, 0:n, 1], eps, None, ALU.add))
    rsqrt(nc, after, rstd[:, 0:n], mv[:, 0:n, 1], tmp[:, 0:n])
    ins = []
    for j in range(n):
        ins.append(nc.vector.tensor_scalar(out_tiles[j], x_tiles[j], mv[:, j, 0:1], rstd[:, j:j + 1],
                                           ALU.subtract, ALU.mult))
    return ins[-1]


def layer_norm_stage(core):
    nc, G = core.nc, 4
    with ExitStack() as ctx:
        xt = ctx.enter_context(nc.sbuf_tensor(core.name("ln_xt"), [P, G, P], F32))
        stats = ctx.enter_context(nc.sbuf_tensor(core.name("ln_stats"), [P, G, 6], F32))
        mv = ctx.enter_context(nc.sbuf_tensor(core.name("ln_mv"), [P, G, 2], F32))
        rstd = ctx.enter_context(nc.sbuf_tensor(core.name("ln_rstd"), [P, G], F32))
        tmp = ctx.enter_context(nc.sbuf_tensor(core.name("ln_tmp"), [P, G], F32))
        (dve_step, rows_ready, cols_ready, stored), zero = ctx.enter_context(
            signals(nc, [core.name(n) for n in ("ln_dve_step", "ln_rows_ready", "ln_cols_ready", "ln_stored")]))
        with nc.Fori(0, NT // G) as i:
            with nc.Block() as block:
                @block.vector
                def _(dve):
                    after = chain(dve, dve_step)
                    normalise_rows(nc, after, [core.x[:, bass.ds(i * G + j, 1), :] for j in range(G)],
                                   [xt[:, j:j + 1, :] for j in range(G)], stats, mv, rstd, tmp, 1e-5).then_inc(rows_ready, 1)

                @block.tensor
                def _(pe):
                    pe.wait_ge(rows_ready, 1)
                    for j in range(G):
                        last = nc.tensor.transpose(core.bank[0][:, j * P:(j + 1) * P], xt[:, j, :], core.ident[:, :])
                    last.then_inc(cols_ready, 1)

                @block.gpsimd
                def _(pool):
                    pool.wait_ge(rows_ready, 1)
                    nc.gpsimd.tensor_copy(core.xn[:, bass.ds(i * G, G), :], xt[:, :, :]).then_inc(stored, 1)

                @block.scalar
                def _(act):
                    act.wait_ge(cols_ready, 1)
                    nc.scalar.copy(core.xnt[:, bass.ds(i * G * P, G * P)], core.bank[0][:, :]).then_inc(stored, 1)
            zero()


def combine_stage(core):
    nc, G = core.nc, 4
    with ExitStack() as ctx:
        gate = ctx.enter_context(nc.sbuf_tensor(core.name("gate"), [P, G, P], F32))
        (gated, multiplied, added), zero = ctx.enter_context(signals(nc, [core.name(n) for n in ("cb_gated", "cb_multiplied", "cb_added")]))
        with nc.Fori(0, NT // G) as i:
            with nc.Block() as block:
                @block.scalar
                def _(act):
                    nc.scalar.activation(gate[:, :, :], core.y[:, bass.ds(i * G, G), :], ACT.Silu).then_inc(gated, 1)

                @block.vector
                def _(dve):
                    dve.wait_ge(gated, 1)
                    nc.vector.tensor_tensor(gate[:, :, :], gate[:, :, :], core.s[:, bass.ds(i * G, G), :],
                                            ALU.mult).then_inc(multiplied, 1)
                    dve.wait_ge(multiplied, 1)
                    nc.vector.tensor_tensor(core.x[:, bass.ds(i * G, G), :], gate[:, :, :],
                                            core.x[:, bass.ds(i * G, G), :], ALU.add).then_inc(added, 1)
            zero()


def linear_attention_stage(core):
    nc, dram, bank = core.nc, core.dram, core.bank
    with ExitStack() as ctx:
        def sb(name, shape, dt=F32):
            return ctx.enter_context(nc.sbuf_tensor("l0a_" + name, shape, dt))

        w = {n: sb(n, [P, P]) for n in ("wq", "wk", "wv", "wo")}
        bq, bk = sb("bq", [P, 1]), sb("bk", [P, 1])
        bv, bo = sb("bv", [P, P]), sb("bo", [P, P])
        keep, head4 = sb("keep", [P, 3, P]), sb("head4", [P, 4])
        xb, low, qk = sb("xb", [P, SEQ]), sb("low", [P, 2, SEQ]), sb("qk", [P, 2, SEQ])
        kh = sb("kh", [P, 4, SEQ])
        v = sb("v", [P, TPB, HEADS, 9])
        st = sb("st", [P, 2, 3 * P])
        rec, on, ot = sb("rec", [P, TPB, HEADS]), sb("on", [P, TPB, P]), sb("ot", [P, SEQ])
        load(core, [(w[n][:, :], dram["L0_attn_" + n]) for n in w] +
             [(bq[:, :], column(dram["L0_attn_bq"])), (bk[:, :], column(dram["L0_attn_bk"])),
              (bv[:, :], spread(dram["L0_attn_bv"])), (bo[:, :], spread(dram["L0_attn_bo"])),
              (keep[:, 0, :], dram["upto"]), (keep[:, 2, :], dram["upto"]), (head4[:, :], dram["head_of_4"])])
        (set_up, x_ready, qk_proj, v_proj, low_ready, exp_ready, qk_ready, v_ready, kh_ready, scored, masked,
         o_ready, on_ready, ot_done, ot_ready, y_done, stored, dve_step), zero = ctx.enter_context(signals(nc, [
             "l0a_" + n for n in ("set_up", "x_ready", "qk_proj", "v_proj", "low_ready", "exp_ready", "qk_ready",
                                  "v_ready", "kh_ready", "scored", "masked", "o_ready", "on_ready", "ot_done",
                                  "ot_ready", "y_done", "stored", "dve_step")]))
        with nc.Block() as block:
            @block.vector
            def _(dve):
                nc.vector.memset(keep[:, 1, :], 1.0).then_inc(set_up, 1)
                nc.vector.memset(v[:, :, :, 8:9], 1.0).then_inc(set_up, 1)
        zero()
        with nc.Fori(0, NB) as b:
            with nc.Block() as block:
                @block.scalar
                def _(act):
                    nc.scalar.copy(xb[:, :], core.xnt[:, bass.ds(b * SEQ, SEQ)]).then_inc(x_ready, 1)
                    act.wait_ge(low_ready, 2)
                    nc.scalar.activation(low[:, :, :], low[:, :, :], ACT.Exp).then_inc(exp_ready, 1)
                    act.wait_ge(ot_done, 1)
                    nc.scalar.copy(ot[:, :], bank[5][:, 0:SEQ]).then_inc(ot_ready, 1)

                @block.tensor
                def _(pe):
                    pe.wait_ge(x_ready, 1)
                    nc.tensor.matmul(bank[0][:, 0:SEQ], w["wq"][:, :], xb[:, :], start=True, stop=True)
                    nc.tensor.matmul(bank[0][:, SEQ:2 * SEQ], w["wk"][:, :], xb[:, :], start=True,
                                     stop=True).then_inc(qk_proj, 1)
                    for t in range(TPB):
                        last = nc.tensor.matmul(bank[1][:, t * P:(t + 1) * P], xb[:, t * P:(t + 1) * P], w["wv"][:, :],
                                                start=True, stop=True)
                    last.then_inc(v_proj, 1)

                    def values(h):
                        pe.wait_ge(masked, h + 1)
                        m = h % 2
                        nc.tensor.matmul(bank[4][:, h * 9:h * 9 + 9], st[:, m, 0:P], v[:, 0, h, :], start=True, stop=True)
                        c = 256 + h * 9
                        nc.tensor.matmul(bank[4][:, c:c + 9], st[:, m, P:2 * P], v[:, 0, h, :], start=True, stop=False)
                        nc.tensor.matmul(bank[4][:, c:c + 9], st[:, m, 2 * P:3 * P], v[:, 1, h, :], start=False,
                                         stop=True).then_inc(o_ready, 1)

                    pe.wait_ge(kh_ready, 4)
                    pe.wait_ge(v_ready, 1)
                    for h in range(HEADS):
                        g, j, m = 32 * (h // 4), h % 4, h % 2
                        if h >= 2:
                            pe.wait_ge(masked, h - 1)
                        nc.tensor.matmul(bank[2 + m][:, 0:SEQ], kh[g:g + 32, j, 0:P], qk[g:g + 32, 0, :],
                                         start=True, stop=True)
                        nc.tensor.matmul(bank[2 + m][:, SEQ:SEQ + P], kh[g:g + 32, j, P:SEQ], qk[g:g + 32, 0, P:SEQ],
                                         start=True, stop=True).then_inc(scored, 1)
                        if h >= 1:
                            values(h - 1)
                    values(HEADS - 1)
                    pe.wait_ge(on_ready, 1)
                    for t in range(TPB):
                        last = nc.tensor.transpose(bank[5][:, t * P:(t + 1) * P], on[:, t, :], core.ident[:, :])
                    last.then_inc(ot_done, 1)
                    pe.wait_ge(ot_ready, 1)
                    for t in range(TPB):
                        last = nc.tensor.matmul(bank[6][:, t * P:(t + 1) * P], ot[:, t * P:(t + 1) * P], w["wo"][:, :],
                                                start=True, stop=True)
                    last.then_inc(y_done, 1)

                @block.vector
                def _(dve):
                    after = chain(dve, dve_step)
                    dve.wait_ge(qk_proj, 1)
                    for n, bias in enumerate((bq, bk)):
                        pre = bank[0][:, n * SEQ:(n + 1) * SEQ]
                        nc.vector.tensor_scalar(low[:, n, :], pre, bias[:, 0:1], 0.0, ALU.add, ALU.min).then_inc(low_ready, 1)
                    for n, bias in enumerate((bq, bk)):
                        pre = bank[0][:, n * SEQ:(n + 1) * SEQ]
                        after(nc.vector.tensor_scalar(qk[:, n, :], pre, bias[:, 0:1], 0.0, ALU.add, ALU.max))
                    dve.wait_ge(exp_ready, 1)
                    nc.vector.tensor_tensor(qk[:, :, :], qk[:, :, :], low[:, :, :], ALU.add).then_inc(qk_ready, 1)
                    dve.wait_ge(v_proj, 1)
                    nc.vector.tensor_tensor(
                        v[:, :, :, 0:8], bank[1][:, 0:SEQ].rearrange("p (t h d) -> p t h d", t=TPB, d=8),
                        bv[:, :].rearrange("p (h d) -> p h d", d=8)[:, None, :, :].to_broadcast([P, TPB, HEADS, 8]),
                        ALU.add).then_inc(v_ready, 1)
                    dve.wait_ge(qk_ready, 1)
                    for j in range(4):
                        nc.vector.tensor_scalar(kh[:, j, :], qk[:, 1, :], head4[:, j:j + 1], None, ALU.mult).then_inc(kh_ready, 1)
                    for h in range(HEADS):
                        dve.wait_ge(scored, h + 1)
                        if h >= 2:
                            dve.wait_ge(o_ready, h - 1)
                        nc.vector.tensor_tensor(st[:, h % 2, :], bank[2 + h % 2][:, 0:3 * P],
                                                keep[:, :, :].rearrange("p a b -> p (a b)"), ALU.mult).then_inc(masked, 1)
                    dve.wait_ge(o_ready, HEADS)
                    o = bank[4][:, 0:512].rearrange("p (t c) -> p t c", t=2)[:, :, 0:HEADS * 9].rearrange(
                        "p t (h d) -> p t h d", d=9)
                    after(nc.vector.tensor_scalar(rec[:, :, :], o[:, :, :, 8], 1e-6, None, ALU.add))
                    after(nc.vector.reciprocal(rec[:, :, :], rec[:, :, :]))
                    nc.vector.tensor_tensor(
                        on[:, :, :].rearrange("p t (h d) -> p t h d", d=8), o[:, :, :, 0:8],
                        rec[:, :, :].rearrange("p t (h a) -> p t h a", a=1).to_broadcast([P, TPB, HEADS, 8]),
                        ALU.mult).then_inc(on_ready, 1)
                    dve.wait_ge(y_done, 1)
                    nc.vector.tensor_tensor(
                        core.s[:, bass.ds(b * TPB, TPB), :], bank[6][:, 0:SEQ].rearrange("p (t c) -> p t c", t=TPB),
                        bo[:, :].rearrange("p (a c) -> p a c", a=1).to_broadcast([P, TPB, P]),
                        ALU.add).then_inc(stored, 1)
            zero()


class Softmax:

    NAMES = ( "scored", "max_ready", "bias_ready", "p_ready", "pt_done", "pt_ready",
             "o_ready", "on_ready", "ot_done", "ot_ready", "y_done", "rec_ready", "masked")

    def __init__(self, core, sb, dh, local, sem, mask_name, scale):
        self.core, self.dh, self.local, self.sem, self.scale = core, dh, local, sem, scale
        self.cols = HEADS * dh
        self.chunks = self.cols // P
        groups = HEADS // 2 if dh == 64 else 4
        self.qt = sb("qt", [P, groups, SEQ])
        self.kt = sb("kt", [P, groups if dh == 64 else 1, SEQ])
        self.v = sb("v", [P, TPB, self.cols])
        self.wo = sb("wo", [P, self.chunks, P])
        self.mask = sb("mask", [P, TPB, SEQ])
        self.sm = sb("sm", [P, 2, 2, SEQ])
        self.p = sb("p", [P, 2, 2, SEQ])
        self.pt = sb("pt", [P, 2, 4, P])
        self.mx = sb("mx", [P, TPB * HEADS])
        self.nb = sb("nb", [P, TPB * HEADS])
        self.sums = sb("sums", [P, TPB * HEADS])
        self.rec = sb("rec", [P, TPB * HEADS])
        self.on = sb("on", [P, TPB, self.cols])
        self.ot = sb("ot", [P, self.chunks, SEQ])
        self.factor = self.nfactor = None
        self.mask_src = core.dram[mask_name]

    def first(self, t):
        return local_first_key(t) if self.local else 0

    def width(self, t):
        return local_width(t) if self.local else (t + 1) * P

    def key_chunks(self, t):
        if t == 0:
            return [(0, P, 0, 0)]
        if self.local:
            return [(0, WINDOW, 0, P - WINDOW), (WINDOW, P, 1, 0)]
        return [(0, P, 0, 0), (P, P, 1, 0)]

    def units(self):
        return [(t, hp) for t in range(TPB) for hp in range(HEADS // 2)]

    def o_place(self, t, h):
        if self.dh == 64:
            return 6 + h // 8, (h % 8) * 64
        return 6 + t, h * 8

    def tensor(self, pe, heads_waits, v_waits):
        nc, core, sem, bank = self.core.nc, self.core, self.sem, self.core.bank
        for ready, n in heads_waits:
            pe.wait_ge(ready, n)
        units = self.units()

        def scores(u):
            t, hp = units[u]
            if u >= 2:
                pe.wait_ge(sem["masked"], 2 * (u - 1))
            w, k0 = self.width(t), self.first(t)
            for i in range(2):
                h = 2 * hp + i
                if self.dh == 64:
                    q = self.qt[64 * i:64 * i + 64, hp, t * P:(t + 1) * P]
                    k = self.kt[64 * i:64 * i + 64, hp, k0:k0 + w]
                else:
                    g = 32 * (h // 4)
                    q = self.qt[g:g + 32, h % 4, t * P:(t + 1) * P]
                    k = self.kt[g:g + 32, 0, k0:k0 + w]
                last = nc.tensor.matmul(bank[2 * (u % 2) + i][:, 0:w], q, k, start=True, stop=True)
            last.then_inc(sem["scored"], 1)

        def turn(u):
            t, hp = units[u]
            pe.wait_ge(sem["p_ready"], 2 * (u + 1))
            if u >= 2:
                pe.wait_ge(sem["pt_ready"], u - 1)
            kc = self.key_chunks(t)
            for c, (c0, n, _, _) in enumerate(kc):
                for i in range(2):
                    last = nc.tensor.transpose(bank[4 + u % 2][0:n, (2 * c + i) * P:(2 * c + i + 1) * P],
                                               self.p[:, u % 2, i, c0:c0 + n], core.ident[:, :])
            last.then_inc(sem["pt_done"], 1)

        def values(u):
            t, hp = units[u]
            pe.wait_ge(sem["pt_ready"], u + 1)
            if self.dh == 64 and t == 1 and hp in (0, 4):
                pe.wait_ge(sem["on_ready"], 1 + hp // 4)
            kc = self.key_chunks(t)
            for i in range(2):
                h = 2 * hp + i
                b, col = self.o_place(t, h)
                for c, (_, n, vt, p0) in enumerate(kc):
                    last = nc.tensor.matmul(bank[b][:, col:col + self.dh], self.pt[p0:p0 + n, u % 2, 2 * c + i, :],
                                            self.v[p0:p0 + n, vt, h * self.dh:(h + 1) * self.dh],
                                            start=(c == 0), stop=(c == len(kc) - 1))
            last.then_inc(sem["o_ready"], 1)

        n = len(units)
        scores(0)
        for u in range(n + 1):
            if u + 1 < n:
                scores(u + 1)
            if u == 0:
                for ready, n_v in v_waits:
                    pe.wait_ge(ready, n_v)
            if u < n:
                turn(u)
            if u >= 1:
                values(u - 1)
        pe.wait_ge(sem["on_ready"], TPB * self.on_parts())
        per = min(4, self.chunks)
        for t in range(TPB):
            for c in range(self.chunks):
                last = nc.tensor.transpose(bank[2 * t + c // 4][:, (c % 4) * P:(c % 4 + 1) * P],
                                           self.on[:, t, c * P:(c + 1) * P], core.ident[:, :])
                if c % per == per - 1:
                    last.then_inc(sem["ot_done"], 1)
        for t in range(TPB):
            pe.wait_ge(sem["ot_ready"], (t + 1) * self.chunks // per)
            for c in range(self.chunks):
                last = nc.tensor.matmul(bank[4][:, t * P:(t + 1) * P], self.ot[:, c, t * P:(t + 1) * P], self.wo[:, c, :],
                                        start=(c == 0), stop=(c == self.chunks - 1))
        last.then_inc(sem["y_done"], 1)

    def on_parts(self):
        return 2 if self.dh == 64 else 1

    def vector(self, dve, after):
        nc, sem, bank = self.core.nc, self.sem, self.core.bank
        units = self.units()

        def normalise(t, part):
            nh = HEADS // self.on_parts()
            h0 = part * nh
            last_unit = t * (HEADS // 2) + (h0 + nh) // 2
            dve.wait_ge(sem["o_ready"], last_unit)
            s = slice(t * HEADS + h0, t * HEADS + h0 + nh)
            nc.vector.reciprocal(self.rec[:, s], self.sums[:, s]).then_inc(sem["rec_ready"], 1)
            dve.wait_ge(sem["rec_ready"], t * self.on_parts() + part + 1)
            b, col = self.o_place(t, h0)
            nc.vector.tensor_tensor(
                self.on[:, t, h0 * self.dh:(h0 + nh) * self.dh].rearrange("p (h d) -> p h d", d=self.dh),
                bank[b][:, col:col + nh * self.dh].rearrange("p (h d) -> p h d", d=self.dh),
                self.rec[:, s].rearrange("p (h a) -> p h a", a=1).to_broadcast([P, nh, self.dh]),
                ALU.mult).then_inc(sem["on_ready"], 1)

        for u, (t, hp) in enumerate(units):
            w = self.width(t)
            dve.wait_ge(sem["scored"], u + 1)
            if u >= 2:
                dve.wait_ge(sem["p_ready"], 2 * (u - 1))
            for i in range(2):
                col = t * HEADS + 2 * hp + i
                nc.vector.tensor_tensor_reduce(self.sm[:, u % 2, i, 0:w], bank[2 * (u % 2) + i][:, 0:w],
                                               self.mask[:, t, 0:w], 1.0, LOWEST, ALU.add, ALU.max,
                                               self.mx[:, col:col + 1]).then_inc(sem["masked"], 1)
            dve.wait_ge(sem["masked"], 2 * (u + 1))
            c = slice(t * HEADS + 2 * hp, t * HEADS + 2 * hp + 2)
            if self.nfactor is not None:
                nc.vector.tensor_tensor(self.nb[:, c], self.mx[:, c], self.nfactor[:, c], ALU.mult).then_inc(sem["bias_ready"], 1)
            else:
                nc.vector.tensor_scalar(self.nb[:, c], self.mx[:, c], -self.scale, None, ALU.mult).then_inc(sem["bias_ready"], 1)
            if t == 1 and hp == 1:
                for part in range(self.on_parts()):
                    normalise(0, part)
        for part in range(self.on_parts()):
            normalise(1, part)
        per = min(4, self.chunks)
        k = 0
        for t in range(TPB):
            for c in range(0, self.chunks, per):
                k += 1
                dve.wait_ge(sem["ot_done"], k)
                nc.vector.tensor_copy(self.ot[:, c:c + per, t * P:(t + 1) * P],
                                      bank[2 * t + c // 4][:, 0:per * P].rearrange("p (c q) -> p c q", c=per)).then_inc(sem["ot_ready"], 1)

    def scalar(self, act):
        nc, sem, bank = self.core.nc, self.sem, self.core.bank
        units = self.units()

        def exps(u):
            t, hp = units[u]
            w = self.width(t)
            act.wait_ge(sem["bias_ready"], u + 1)
            if u >= 2:
                act.wait_ge(sem["pt_done"], u - 1)
            for i in range(2):
                col = t * HEADS + 2 * hp + i
                scale = self.factor[:, col:col + 1] if self.factor is not None else self.scale
                nc.scalar.activation(self.p[:, u % 2, i, 0:w], self.sm[:, u % 2, i, 0:w], ACT.Exp,
                                     bias=self.nb[:, col:col + 1], scale=scale,
                                     accum_out=self.sums[:, col:col + 1]).then_inc(sem["p_ready"], 1)

        def copy_back(u):
            t, hp = units[u]
            act.wait_ge(sem["pt_done"], u + 1)
            if u >= 2:
                act.wait_ge(sem["o_ready"], u - 1)
            kc = self.key_chunks(t)
            if all(n == P for _, n, _, _ in kc):
                m = 2 * len(kc)
                nc.scalar.copy(self.pt[:, u % 2, 0:m, :],
                               bank[4 + u % 2][:, 0:m * P].rearrange("p (m q) -> p m q", m=m)).then_inc(sem["pt_ready"], 1)
            else:
                for c, (_, n, _, p0) in enumerate(kc):
                    last = nc.scalar.copy(self.pt[p0:p0 + n, u % 2, 2 * c:2 * c + 2, :],
                                          bank[4 + u % 2][0:n, 2 * c * P:(2 * c + 2) * P].rearrange("p (m q) -> p m q", m=2))
                last.then_inc(sem["pt_ready"], 1)

        for u in range(len(units) + 1):
            if u < len(units):
                exps(u)
            if u >= 1:
                copy_back(u - 1)


def local_attention_stage(core, l):
    nc, dram, bank = core.nc, core.dram, core.bank
    NCH = 3 * INNER // 512
    with ExitStack() as ctx:
        def sb(name, shape, dt=F32):
            return ctx.enter_context(nc.sbuf_tensor("loc_" + name, shape, dt))

        own = ("heads_ready", "v_ready", "yb_ready", "xt_done", "xb_ready", "proj_done", "squared", "turned", "summed", "rk_ready",
               "added", "final", "qkt_done", "dve_step", "pool_step", "stored")
        names = own + Softmax.NAMES
        sems, zero = ctx.enter_context(signals(nc, ["loc_" + n for n in names]))
        sem = dict(zip(names, sems))
        att = Softmax(core, sb, DH, True, sem, "mask_local", None)
        wqkv = sb("wqkv", [P, 3 * INNER])
        rope, qks = sb("rope", [P, TPB, 4, DH]), sb("qks", [P, 2, DH])
        yb, xb = sb("yb", [P, TPB, P]), sb("xb", [P, SEQ])
        a, b_ = sb("a", [P, TPB, 4, 512]), sb("b", [P, 4, 512])
        sq = sb("sq", [P, 2, 512])
        n2, rn, tmp = sb("n2", [P, TPB, 32]), sb("rn", [P, TPB, 32]), sb("tmp", [P, 32])
        att.factor, att.nfactor = sb("f", [P, TPB * HEADS]), sb("nf", [P, TPB * HEADS])
        load(core, [
            (wqkv[:, :], dram["L0_ffn_Wqkv"][bass.ds(l, 1), :, :].rearrange("a p n -> p (a n)")),
            (att.wo[:, :, :], dram["L0_ffn_Wo"][bass.ds(l, 1), :, :].rearrange("a (c p) n -> p (a c) n", p=P)),
            (att.mask[:, :, :], att.mask_src), (rope[:, :, :, :], dram["rope_local"]),
            (qks[:, 0, :], dram["L0_ffn_q_scale"][bass.ds(l, 1), :].to_broadcast([P, DH])),
            (qks[:, 1, :], dram["L0_ffn_k_scale"][bass.ds(l, 1), :].to_broadcast([P, DH]))])
        with nc.Block() as block:
            @block.vector
            def _(dve):
                after = chain(dve, sem["dve_step"])
                for n in range(2):
                    wide = qks[:, n, :].rearrange("p (a d) -> p a d", a=1).to_broadcast([P, TPB, DH])
                    after(nc.vector.tensor_tensor(rope[:, :, 2 * n, :], rope[:, :, 2 * n, :], wide, ALU.mult))
                    for half in range(2):
                        d, s = half * 32, 32 - half * 32
                        wide = qks[:, n, s:s + 32].rearrange("p (a d) -> p a d", a=1).to_broadcast([P, TPB, 32])
                        after(nc.vector.tensor_tensor(rope[:, :, 2 * n + 1, d:d + 32], rope[:, :, 2 * n + 1, d:d + 32],
                                                      wide, ALU.mult))
                after(nc.vector.memset(xb[64:128, 0:1], 0.0))
        zero()
        with nc.Fori(0, NB) as b:
            with nc.Block() as block:
                @block.gpsimd
                def _(pool):
                    nc.gpsimd.tensor_copy(yb[:, :, :], core.y[:, bass.ds(b * TPB, TPB), :]).then_inc(sem["yb_ready"], 1)
                    for t in range(TPB):
                        for c in range(4):
                            i = t * 4 + c
                            pool.wait_ge(sem["turned"], i + 1)
                            ins = nc.gpsimd.tensor_tensor(a[:, t, c, :], a[:, t, c, :], b_[:, c, :], ALU.add)
                            ins.then_inc(sem["added"], 1)
                            if c >= 2:
                                pool.wait_ge(sem["added"], i + 1)
                                pool.wait_ge(sem["rk_ready"], 2 * t + 1)
                                k0 = 16 + (c - 2) * 8
                                nc.gpsimd.tensor_tensor(
                                    a[:, t, c, :].rearrange("p (h d) -> p h d", d=DH),
                                    a[:, t, c, :].rearrange("p (h d) -> p h d", d=DH),
                                    rn[:, t, k0:k0 + 8].rearrange("p (h a) -> p h a", a=1).to_broadcast([P, 8, DH]),
                                    ALU.mult).then_inc(sem["final"], 1)

                @block.tensor
                def _(pe):
                    pe.wait_ge(sem["yb_ready"], 1)
                    for t in range(TPB):
                        last = nc.tensor.transpose(bank[7][:, t * P:(t + 1) * P], yb[:, t, :], core.ident[:, :])
                    last.then_inc(sem["xt_done"], 1)
                    pe.wait_ge(sem["xb_ready"], 2)
                    for t in range(TPB):
                        for c in range(NCH):
                            if t == 1 and c < 4:
                                pe.wait_ge(sem["squared"], c + 1)
                                pe.wait_ge(sem["turned"], c + 1)
                            elif t == 1:
                                pe.wait_ge(sem["v_ready"], c - 3)
                            nc.tensor.matmul(bank[c][:, :], xb[:, t * P:(t + 1) * P], wqkv[:, c * 512:(c + 1) * 512],
                                             start=True, stop=True).then_inc(sem["proj_done"], 1)
                    k = 0
                    for t in range(TPB):
                        for c in range(4):
                            if c < 2:
                                pe.wait_ge(sem["added"], t * 4 + c + 1)
                            else:
                                pe.wait_ge(sem["final"], t * 2 + c - 1)
                            if k >= 2:
                                pe.wait_ge(sem["heads_ready"], k - 1)
                            for j in range(4):
                                last = nc.tensor.transpose(bank[6 + k % 2][:, j * P:(j + 1) * P],
                                                           a[:, t, c, j * P:(j + 1) * P], core.ident[:, :])
                            last.then_inc(sem["qkt_done"], 1)
                            k += 1
                    att.tensor(pe, [(sem["heads_ready"], 8)], [(sem["v_ready"], 4)])

                @block.scalar
                def _(act):
                    act.wait_ge(sem["xt_done"], 1)
                    nc.scalar.copy(xb[0:64, :], bank[7][0:64, 0:SEQ]).then_inc(sem["xb_ready"], 1)
                    nc.scalar.copy(xb[64:128, 1:SEQ], bank[7][64:128, 0:SEQ - 1]).then_inc(sem["xb_ready"], 1)
                    for t in range(TPB):
                        for c in range(NCH):
                            act.wait_ge(sem["proj_done"], t * NCH + c + 1)
                            if c < 4:
                                i = t * 4 + c
                                if i >= 2:
                                    act.wait_ge(sem["summed"], i - 1)
                                nc.scalar.activation(sq[:, i % 2, :], bank[c][:, :], ACT.Square).then_inc(sem["squared"], 1)
                            else:
                                nc.scalar.copy(att.v[:, t, (c - 4) * 512:(c - 3) * 512], bank[c][:, :]).then_inc(sem["v_ready"], 1)
                    k = 0
                    for t in range(TPB):
                        for c in range(4):
                            k += 1
                            act.wait_ge(sem["qkt_done"], k)
                            dst = att.qt if c < 2 else att.kt
                            nc.scalar.copy(dst[:, (c % 2) * 4:(c % 2) * 4 + 4, t * P:(t + 1) * P],
                                           bank[6 + (k - 1) % 2][:, :].rearrange("p (j q) -> p j q", j=4)).then_inc(sem["heads_ready"], 1)
                    att.scalar(act)

                @block.vector
                def _(dve):
                    after = chain(dve, sem["dve_step"])
                    for t in range(TPB):
                        for c in range(4):
                            i, n = t * 4 + c, c // 2
                            dve.wait_ge(sem["proj_done"], t * NCH + c + 1)
                            dve.wait_ge(sem["squared"], i + 1)
                            if t == 1:
                                dve.wait_ge(sem["added"], c + 1)
                            src = bank[c][:, :].rearrange("p (h d) -> p h d", d=DH)
                            cos = rope[:, t, 2 * n, :].rearrange("p (a d) -> p a d", a=1).to_broadcast([P, 8, DH])
                            nc.vector.tensor_tensor(a[:, t, c, :].rearrange("p (h d) -> p h d", d=DH), src, cos, ALU.mult)
                            halves = bank[c][:, :].rearrange("p (h s d) -> p h s d", s=2, d=32)[:, :, ::-1, :]
                            sin = rope[:, t, 2 * n + 1, :].rearrange("p (a s d) -> p a s d", a=1, s=2).to_broadcast([P, 8, 2, 32])
                            nc.vector.tensor_tensor(b_[:, c, :].rearrange("p (h s d) -> p h s d", s=2, d=32), halves, sin,
                                                    ALU.mult).then_inc(sem["turned"], 1)
                            nc.vector.tensor_reduce(n2[:, t, c * 8:(c + 1) * 8],
                                                    sq[:, i % 2, :].rearrange("p (h d) -> p h d", d=DH), AX.X,
                                                    ALU.add).then_inc(sem["summed"], 1)
                        dve.wait_ge(sem["summed"], 4 * (t + 1))
                        after(nc.vector.tensor_scalar(n2[:, t, :], n2[:, t, :], 1e-24, None, ALU.max))
                        rsqrt(nc, after, rn[:, t, :], n2[:, t, :], tmp[:, :])
                        for f, scale in ((att.factor, QK_SCALE), (att.nfactor, -QK_SCALE)):
                            nc.vector.tensor_scalar(f[:, t * HEADS:(t + 1) * HEADS], rn[:, t, 0:16], scale, None,
                                                    ALU.mult).then_inc(sem["rk_ready"], 1)
                    dve.wait_ge(sem["rk_ready"], 2 * TPB)
                    att.vector(dve, after)
                    dve.wait_ge(sem["y_done"], 1)
                    nc.vector.tensor_tensor(core.y[:, bass.ds(b * TPB, TPB), :],
                                            bank[4][:, 0:SEQ].rearrange("p (t c) -> p t c", t=TPB), yb[:, :, :],
                                            ALU.add).then_inc(sem["stored"], 1)
            zero()


def glu_stage(core, l):
    nc, dram, bank = core.nc, core.dram, core.bank
    with ExitStack() as ctx:
        def sb(name, shape, dt=F32):
            return ctx.enter_context(nc.sbuf_tensor("glu_" + name, shape, dt))

        names = ("yb_ready", "cols_done", "shifted", "rows_done", "xh_ready", "xh_done", "xn_ready", "hid_done",
                 "gelu_ready", "h_ready", "y_done", "yb2_ready", "stored", "dve_step")
        sems, zero = ctx.enter_context(signals(nc, ["glu_" + n for n in names]))
        sem = dict(zip(names, sems))
        w1, w2 = sb("w1", [P, 2 * DIM_INNER]), sb("w2", [P, 3, P])
        b1, b2, gain, shift = sb("b1", [P, 2, 3]), sb("b2", [P, P]), sb("gain", [P, 1]), sb("shift", [P, 1])
        yb, yb2, xs, xh, xn = sb("yb", [P, TPB, P]), sb("yb2", [P, TPB, P]), sb("xs", [P, SEQ]), sb("xh", [P, TPB, P]), sb("xn", [P, SEQ])
        gel, h = sb("gel", [P, 3, SEQ]), sb("h", [P, 3, SEQ])
        stats, mv, rstd, tmp = sb("stats", [P, TPB, 6]), sb("mv", [P, TPB, 2]), sb("rstd", [P, TPB]), sb("tmp", [P, TPB])
        row = lambda name: dram["L0_ffn_" + name][bass.ds(l, 1), :]
        load(core, [(w1[:, :], dram["L0_ffn_W1"][bass.ds(l, 1), :, :].rearrange("a p n -> p (a n)")),
                    (b2[:, :], row("b2").to_broadcast([P, P])),
                    (gain[:, :], row("ln_g").rearrange("a p -> p a")), (shift[:, :], row("ln_b").rearrange("a p -> p a"))] +
             [(w2[0:n, c, :], dram["L0_ffn_W2"][bass.ds(l, 1), c0:c0 + n, :].rearrange("a p n -> p (a n)"))
              for c, (c0, n) in enumerate(HID_CHUNKS)] +
             [(b1[0:n, g, c:c + 1], dram["L0_ffn_b1"][bass.ds(l, 1), g * DIM_INNER + c0:g * DIM_INNER + c0 + n].rearrange("a p -> p a"))
              for c, (c0, n) in enumerate(HID_CHUNKS) for g in range(2)])
        with nc.Block() as block:
            @block.vector
            def _(dve):
                nc.vector.memset(xs[64:128, 0:1], 0.0).then_inc(sem["dve_step"], 1)
        zero()
        with nc.Fori(0, NB) as b:
            with nc.Block() as block:
                @block.gpsimd
                def _(pool):
                    nc.gpsimd.tensor_copy(yb[:, :, :], core.y[:, bass.ds(b * TPB, TPB), :]).then_inc(sem["yb_ready"], 1)
                    pool.wait_ge(sem["yb_ready"], 1)
                    nc.gpsimd.tensor_tensor(yb2[:, :, :], yb[:, :, :],
                                            b2[:, :].rearrange("p (a c) -> p a c", a=1).to_broadcast([P, TPB, P]),
                                            ALU.add).then_inc(sem["yb2_ready"], 1)

                @block.tensor
                def _(pe):
                    pe.wait_ge(sem["yb_ready"], 1)
                    for t in range(TPB):
                        last = nc.tensor.transpose(bank[3][:, t * P:(t + 1) * P], yb[:, t, :], core.ident[:, :])
                    last.then_inc(sem["cols_done"], 1)
                    pe.wait_ge(sem["shifted"], 2)
                    for t in range(TPB):
                        last = nc.tensor.transpose(bank[4][:, t * P:(t + 1) * P], xs[:, t * P:(t + 1) * P], core.ident[:, :])
                    last.then_inc(sem["rows_done"], 1)
                    pe.wait_ge(sem["xh_ready"], 1)
                    for t in range(TPB):
                        last = nc.tensor.transpose(bank[5][:, t * P:(t + 1) * P], xh[:, t, :], core.ident[:, :])
                    last.then_inc(sem["xh_done"], 1)
                    pe.wait_ge(sem["xn_ready"], 1)
                    for c, (c0, n) in enumerate(HID_CHUNKS):
                        for g in (1, 0):
                            last = nc.tensor.matmul(bank[c][0:n, g * SEQ:(g + 1) * SEQ],
                                                    w1[:, g * DIM_INNER + c0:g * DIM_INNER + c0 + n], xn[:, :],
                                                    start=True, stop=True)
                        last.then_inc(sem["hid_done"], 1)
                    pe.wait_ge(sem["h_ready"], 3)
                    for t in range(TPB):
                        for c, (c0, n) in enumerate(HID_CHUNKS):
                            last = nc.tensor.matmul(bank[6][:, t * P:(t + 1) * P], h[0:n, c, t * P:(t + 1) * P], w2[0:n, c, :],
                                                    start=(c == 0), stop=(c == 2))
                    last.then_inc(sem["y_done"], 1)

                @block.scalar
                def _(act):
                    act.wait_ge(sem["cols_done"], 1)
                    nc.scalar.copy(xs[0:64, :], bank[3][0:64, 0:SEQ]).then_inc(sem["shifted"], 1)
                    nc.scalar.copy(xs[64:128, 1:SEQ], bank[3][64:128, 0:SEQ - 1]).then_inc(sem["shifted"], 1)
                    act.wait_ge(sem["xh_done"], 1)
                    nc.scalar.activation(xn[:, :], bank[5][:, 0:SEQ], ACT.Identity, bias=shift[:, 0:1],
                                         scale=gain[:, 0:1]).then_inc(sem["xn_ready"], 1)
                    for c, (c0, n) in enumerate(HID_CHUNKS):
                        act.wait_ge(sem["hid_done"], c + 1)
                        nc.scalar.activation(gel[0:n, c, :], bank[c][0:n, SEQ:2 * SEQ], ACT.Gelu,
                                             bias=b1[0:n, 1, c:c + 1]).then_inc(sem["gelu_ready"], 1)

                @block.vector
                def _(dve):
                    after = chain(dve, sem["dve_step"])
                    dve.wait_ge(sem["rows_done"], 1)
                    normalise_rows(nc, after, [bank[4][:, t * P:(t + 1) * P] for t in range(TPB)],
                                   [xh[:, t, :] for t in range(TPB)], stats, mv, rstd, tmp, 1e-5).then_inc(sem["xh_ready"], 1)
                    for c, (c0, n) in enumerate(HID_CHUNKS):
                        dve.wait_ge(sem["gelu_ready"], c + 1)
                        nc.vector.scalar_tensor_tensor(out=h[0:n, c, :], in0=bank[c][0:n, 0:SEQ], scalar=b1[0:n, 0, c:c + 1],
                                                       in1=gel[0:n, c, :], op0=ALU.add, op1=ALU.mult).then_inc(sem["h_ready"], 1)
                    dve.wait_ge(sem["y_done"], 1)
                    dve.wait_ge(sem["yb2_ready"], 1)
                    nc.vector.tensor_tensor(core.y[:, bass.ds(b * TPB, TPB), :],
                                            bank[6][:, 0:SEQ].rearrange("p (t c) -> p t c", t=TPB), yb2[:, :, :],
                                            ALU.add).then_inc(sem["stored"], 1)
            zero()


def local_transformer_stage(core):
    nc = core.nc
    with signals(nc, ["y_started"]) as ((started,), zero):
        with nc.Block() as block:
            @block.vector
            def _(dve):
                nc.vector.tensor_copy(core.y[:, :, :], core.xn[:, :, :]).then_inc(started, 1)
        zero()
    with nc.Fori(0, LAYERS_RUN) as l:
        local_attention_stage(core, l)
        glu_stage(core, l)


def affine_rows(nc, after, rows, gain, shift):
    n = rows.shape[1]
    wide = lambda v: v.rearrange("p (a c) -> p a c", a=1).to_broadcast([P, n, P])
    after(nc.vector.tensor_tensor(rows, rows, wide(gain), ALU.mult))
    return lambda out: nc.vector.tensor_tensor(out, rows, wide(shift), ALU.add)


def gelu_linear_attention_stage(core):
    nc, dram, bank = core.nc, core.dram, core.bank
    with ExitStack() as ctx:
        def sb(name, shape, dt=F32):
            return ctx.enter_context(nc.sbuf_tensor("l1a_" + name, shape, dt))

        names = ("turned", "w_ready", "x_ready", "qk_proj", "v_proj", "gelu_ready", "qk_ready", "rot_done", "qkr_ready",
                 "v_ready", "krt_done", "krt_ready", "kv_done", "kv_ready", "mean_ready", "o_done", "stored", "dve_step")
        sems, zero = ctx.enter_context(signals(nc, ["l1a_" + n for n in names]))
        sem = dict(zip(names, sems))
        w, wt = sb("w", [P, 3, P]), sb("wt", [P, 3, P])
        bq, bk, bv = sb("bq", [P, 1]), sb("bk", [P, 1]), sb("bv", [P, P])
        gamma, beta = sb("gamma", [P, P]), sb("beta", [P, P])
        rope, swap, block_ = sb("rope", [P, 2, SEQ]), sb("swap", [P, P]), sb("block", [P, P])
        xb, qk, part, qkr = sb("xb", [P, SEQ]), sb("qk", [P, 2, SEQ]), sb("part", [P, 2, SEQ]), sb("qkr", [P, 2, SEQ])
        v, krt = sb("v", [P, TPB, P]), sb("krt", [P, TPB, P])
        mean, kmean, kv = sb("mean", [P, 1]), sb("kmean", [P, P]), sb("kv", [P, P])
        rec, res = sb("rec", [P, TPB, P]), sb("res", [P, TPB, P])
        stats, mv, rstd, tmp = sb("stats", [P, TPB, 6]), sb("mv", [P, TPB, 2]), sb("rstd", [P, TPB]), sb("tmp", [P, TPB])
        load(core, [(w[:, i, :], dram["L1_attn_W" + n]) for i, n in enumerate("qkv")] +
             [(bq[:, :], column(dram["L1_attn_bq"])), (bk[:, :], column(dram["L1_attn_bk"])),
              (bv[:, :], spread(dram["L1_attn_bv"])), (gamma[:, :], spread(dram["L1_attn_gamma"])),
              (beta[:, :], spread(dram["L1_attn_beta"])), (rope[:, :, :], dram["rope_l1"]),
              (swap[:, :], dram["swap"]), (block_[:, :], dram["head_block"])])
        with nc.Block() as block:
            @block.tensor
            def _(pe):
                for i in range(3):
                    last = nc.tensor.transpose(bank[0][:, i * P:(i + 1) * P], w[:, i, :], core.ident[:, :])
                last.then_inc(sem["turned"], 1)

            @block.vector
            def _(dve):
                dve.wait_ge(sem["turned"], 1)
                nc.vector.tensor_copy(wt[:, :, :].rearrange("p a b -> p (a b)"), bank[0][:, 0:3 * P]).then_inc(sem["w_ready"], 1)
        zero()
        with nc.Fori(0, NB) as b:
            with nc.Block() as block:
                @block.scalar
                def _(act):
                    nc.scalar.copy(xb[:, :], core.xnt[:, bass.ds(b * SEQ, SEQ)]).then_inc(sem["x_ready"], 1)
                    act.wait_ge(sem["qk_proj"], 1)
                    for n, bias in enumerate((bq, bk)):
                        nc.scalar.activation(part[:, n, :], bank[0][:, n * SEQ:(n + 1) * SEQ], ACT.Gelu,
                                             bias=bias[:, 0:1]).then_inc(sem["gelu_ready"], 1)
                    act.wait_ge(sem["krt_done"], 1)
                    nc.scalar.copy(krt[:, :, :], bank[3][:, 0:SEQ].rearrange("p (t c) -> p t c", t=TPB)).then_inc(sem["krt_ready"], 1)

                @block.tensor
                def _(pe):
                    pe.wait_ge(sem["x_ready"], 1)
                    for n in range(2):
                        last = nc.tensor.matmul(bank[0][:, n * SEQ:(n + 1) * SEQ], wt[:, n, :], xb[:, :], start=True, stop=True)
                    last.then_inc(sem["qk_proj"], 1)
                    for t in range(TPB):
                        last = nc.tensor.matmul(bank[2][:, t * P:(t + 1) * P], xb[:, t * P:(t + 1) * P], wt[:, 2, :],
                                                start=True, stop=True)
                    last.then_inc(sem["v_proj"], 1)
                    pe.wait_ge(sem["qk_ready"], 1)
                    nc.tensor.matmul(bank[1][:, :], swap[:, :], qk[:, :, :].rearrange("p n q -> p (n q)"), start=True,
                                     stop=True).then_inc(sem["rot_done"], 1)
                    pe.wait_ge(sem["qkr_ready"], 1)
                    for t in range(TPB):
                        last = nc.tensor.transpose(bank[3][:, t * P:(t + 1) * P], qkr[:, 1, t * P:(t + 1) * P], core.ident[:, :])
                    last.then_inc(sem["krt_done"], 1)
                    pe.wait_ge(sem["krt_ready"], 1)
                    pe.wait_ge(sem["v_ready"], 1)
                    for t in range(TPB):
                        last = nc.tensor.matmul(bank[4][:, 0:P], krt[:, t, :], v[:, t, :], start=(t == 0), stop=(t == TPB - 1))
                    last.then_inc(sem["kv_done"], 1)
                    pe.wait_ge(sem["mean_ready"], 2)
                    for t in range(TPB):
                        nc.tensor.matmul(bank[6][:, t * P:(t + 1) * P], qk[:, 0, t * P:(t + 1) * P], kmean[:, :],
                                         start=True, stop=True)
                    pe.wait_ge(sem["kv_ready"], 1)
                    for t in range(TPB):
                        last = nc.tensor.matmul(bank[5][:, t * P:(t + 1) * P], qkr[:, 0, t * P:(t + 1) * P], kv[:, :],
                                                start=True, stop=True)
                    last.then_inc(sem["o_done"], 1)

                @block.vector
                def _(dve):
                    after = chain(dve, sem["dve_step"])
                    table = lambda n: rope[:, n, :].rearrange("p (a q) -> p a q", a=1).to_broadcast([P, 2, SEQ])
                    dve.wait_ge(sem["gelu_ready"], 2)
                    nc.vector.tensor_scalar(qk[:, :, :], part[:, :, :], 0.21, None, ALU.add).then_inc(sem["qk_ready"], 1)
                    dve.wait_ge(sem["qk_ready"], 1)
                    nc.vector.tensor_reduce(mean[:, :], qk[:, 1, :], AX.X, ALU.add).then_inc(sem["mean_ready"], 1)
                    after(nc.vector.tensor_tensor(part[:, :, :], qk[:, :, :], table(0), ALU.mult))
                    dve.wait_ge(sem["mean_ready"], 1)
                    nc.vector.tensor_scalar(kmean[:, :], block_[:, :], mean[:, 0:1], 1.0 / SEQ, ALU.mult, ALU.mult).then_inc(sem["mean_ready"], 1)
                    dve.wait_ge(sem["v_proj"], 1)
                    nc.vector.tensor_tensor(v[:, :, :], bank[2][:, 0:SEQ].rearrange("p (t c) -> p t c", t=TPB),
                                            bv[:, :].rearrange("p (a c) -> p a c", a=1).to_broadcast([P, TPB, P]),
                                            ALU.add).then_inc(sem["v_ready"], 1)
                    dve.wait_ge(sem["rot_done"], 1)
                    after(nc.vector.tensor_tensor(qkr[:, :, :], bank[1][:, :].rearrange("p (n q) -> p n q", n=2), table(1), ALU.mult))
                    nc.vector.tensor_tensor(qkr[:, :, :], qkr[:, :, :], part[:, :, :], ALU.add).then_inc(sem["qkr_ready"], 1)
                    dve.wait_ge(sem["kv_done"], 1)
                    nc.vector.scalar_tensor_tensor(out=kv[:, :], in0=bank[4][:, 0:P], scalar=1.0 / SEQ, in1=block_[:, :],
                                                   op0=ALU.mult, op1=ALU.mult).then_inc(sem["kv_ready"], 1)
                    dve.wait_ge(sem["o_done"], 1)
                    tiles = lambda i: bank[i][:, 0:SEQ].rearrange("p (t c) -> p t c", t=TPB)
                    after(nc.vector.tensor_scalar(rec[:, :, :], tiles(6), 1e-6, None, ALU.add))
                    after(nc.vector.reciprocal(rec[:, :, :], rec[:, :, :]))
                    after(nc.vector.tensor_tensor(res[:, :, :], tiles(5), rec[:, :, :], ALU.mult))
                    after(nc.vector.tensor_tensor(res[:, :, :], res[:, :, :], core.xn[:, bass.ds(b * TPB, TPB), :], ALU.add))
                    after(normalise_rows(nc, after, [res[:, t, :] for t in range(TPB)], [res[:, t, :] for t in range(TPB)],
                                         stats, mv, rstd, tmp, 1e-12))
                    affine_rows(nc, after, res[:, :, :], gamma[:, :], beta[:, :])(
                        core.s[:, bass.ds(b * TPB, TPB), :]).then_inc(sem["stored"], 1)
            zero()


def experts_stage(core):
    nc, dram, bank = core.nc, core.dram, core.bank
    with ExitStack() as ctx:
        def sb(name, shape, dt=F32):
            return ctx.enter_context(nc.sbuf_tensor("moe_" + name, shape, dt))

        chosen = sb("chosen", [P, NT, NE])
        with ExitStack() as ctx2:
            def sb2(name, shape, dt=F32):
                return ctx2.enter_context(nc.sbuf_tensor("route_" + name, shape, dt))

            names = ("turned", "router_ready", "logits_done", "exp_ready", "shifted", "top_ready", "top_stored", "top_spread",
                     "onehot_ready", "compared", "counted", "dve_step")
            sems, zero = ctx2.enter_context(signals(nc, ["route_" + n for n in names]))
            sem = dict(zip(names, sems))
            router, router_t = sb2("router", [NE, P]), sb2("router_t", [P, NE])
            expert_no, earlier = sb2("expert_no", [P, NT, NE]), sb2("earlier", [P, P])
            prob, onehot, cand = sb2("prob", [P, NT, NE]), sb2("onehot", [P, NT, NE]), sb2("cand", [P, NT, NE])
            onehot_b = sb2("onehot_b", [P, NT, NE], BF16)
            red, top, keep, count = sb2("red", [P, NT]), sb2("top", [P, NT]), sb2("keep", [P, NT]), sb2("count", [P, NT])
            row = sb2("row", [P, TOK])
            above, tie = sb2("above", [P, 2, TOK], BF16), sb2("tie", [P, P], BF16)
            top_dram = nc.dram_tensor("top_prob", (NT, P), F32, kind="Internal").ap()
            load(core, [(router[:, :], dram["L1_ffn_router_w"]), (expert_no[:, :, :], dram["expert_no"]),
                        (earlier[:, :], dram["strictly_before"])])
            wide = lambda v: v.rearrange("p (t a) -> p t a", a=1).to_broadcast([P, NT, NE])
            with nc.Block() as block:
                @block.tensor
                def _(pe):
                    nc.tensor.transpose(bank[0][:, 0:NE], router[:, :], core.ident[0:NE, 0:NE]).then_inc(sem["turned"], 1)
                    pe.wait_ge(sem["router_ready"], 1)
                    for i in range(NT):
                        last = nc.tensor.matmul(bank[1][:, i * NE:(i + 1) * NE], core.xnt[:, i * P:(i + 1) * P], router_t[:, :],
                                                start=True, stop=True)
                    last.then_inc(sem["logits_done"], 1)
                    pe.wait_ge(sem["onehot_ready"], 1)
                    for j in range(NT):
                        pe.wait_ge(sem["compared"], j + 1)
                        for i in range(NT):
                            last = nc.tensor.matmul(bank[2][:, i * NE:(i + 1) * NE], above[:, j % 2, i * P:(i + 1) * P],
                                                    onehot_b[:, j, :], start=(i == 0 and j == 0), stop=(j == NT - 1),
                                                    skip_group_check=True)
                        last.then_inc(sem["counted"], 1)

                @block.scalar
                def _(act):
                    act.wait_ge(sem["shifted"], 1)
                    nc.scalar.activation(prob[:, :, :], prob[:, :, :], ACT.Exp).then_inc(sem["exp_ready"], 1)

                @block.sync
                def _(sp):
                    sp.wait_ge(sem["top_ready"], 1)
                    sp.dma_start(top_dram.rearrange("t p -> p t"), top[:, :]).then_inc(sem["top_stored"], 16)
                    sp.wait_ge(sem["top_stored"], 16)
                    sp.dma_start(row[:, :], top_dram.rearrange("(a t) p -> a (t p)", a=1).to_broadcast([P, TOK])).then_inc(sem["top_spread"], 16)

                @block.vector
                def _(dve):
                    after = chain(dve, sem["dve_step"])
                    dve.wait_ge(sem["turned"], 1)
                    nc.vector.tensor_copy(router_t[:, :], bank[0][:, 0:NE]).then_inc(sem["router_ready"], 1)
                    dve.wait_ge(sem["logits_done"], 1)
                    logits = bank[1][:, 0:NT * NE].rearrange("p (t e) -> p t e", e=NE)
                    after(nc.vector.tensor_reduce(red[:, :], logits, AX.X, ALU.max))
                    nc.vector.tensor_tensor(prob[:, :, :], logits, wide(red[:, :]), ALU.subtract).then_inc(sem["shifted"], 1)
                    dve.wait_ge(sem["exp_ready"], 1)
                    after(nc.vector.tensor_reduce(red[:, :], prob[:, :, :], AX.X, ALU.add))
                    after(nc.vector.reciprocal(red[:, :], red[:, :]))
                    after(nc.vector.tensor_tensor(prob[:, :, :], prob[:, :, :], wide(red[:, :]), ALU.mult))
                    nc.vector.tensor_reduce(top[:, :], prob[:, :, :], AX.X, ALU.max).then_inc(sem["top_ready"], 1)
                    dve.wait_ge(sem["top_ready"], 1)
                    after(nc.vector.tensor_tensor(cand[:, :, :], prob[:, :, :], wide(top[:, :]), ALU.is_equal))
                    after(nc.vector.scalar_tensor_tensor(out=cand[:, :, :].rearrange("p t e -> p (t e)"),
                                                         in0=cand[:, :, :].rearrange("p t e -> p (t e)"), scalar=-100.0,
                                                         in1=expert_no[:, :, :].rearrange("p t e -> p (t e)"),
                                                         op0=ALU.mult, op1=ALU.add))
                    after(nc.vector.tensor_reduce(red[:, :], cand[:, :, :], AX.X, ALU.min))
                    after(nc.vector.tensor_tensor(onehot[:, :, :], cand[:, :, :], wide(red[:, :]), ALU.is_equal))
                    nc.vector.tensor_copy(onehot_b[:, :, :], onehot[:, :, :]).then_inc(sem["onehot_ready"], 1)
                    dve.wait_ge(sem["top_spread"], 16)
                    for j in range(NT):
                        if j >= 2:
                            dve.wait_ge(sem["counted"], j - 1)
                        m, mine = j % 2, top[:, j:j + 1]
                        d0, d1 = j * P, (j + 1) * P
                        after(nc.vector.tensor_scalar(above[:, m, 0:d1], row[:, 0:d1], mine, None, ALU.is_lt))
                        after(nc.vector.scalar_tensor_tensor(out=tie[:, :], in0=row[:, d0:d1], scalar=mine, in1=earlier[:, :],
                                                             op0=ALU.is_equal, op1=ALU.mult))
                        if j < NT - 1:
                            nc.vector.tensor_scalar(above[:, m, d1:TOK], row[:, d1:TOK], mine, None, ALU.is_le)
                        nc.vector.tensor_tensor(above[:, m, d0:d1], above[:, m, d0:d1], tie[:, :], ALU.add).then_inc(sem["compared"], 1)
                    dve.wait_ge(sem["counted"], NT)
                    counts = bank[2][:, 0:NT * NE].rearrange("p (t e) -> p t e", e=NE)
                    after(nc.vector.tensor_tensor(cand[:, :, :], counts, onehot[:, :, :], ALU.mult))
                    after(nc.vector.tensor_reduce(count[:, :], cand[:, :, :], AX.X, ALU.add))
                    after(nc.vector.tensor_scalar(keep[:, :], count[:, :], float(CAPACITY), None, ALU.is_lt))
                    after(nc.vector.tensor_tensor(chosen[:, :, :], onehot[:, :, :], wide(keep[:, :]), ALU.mult))
                    after(nc.vector.tensor_scalar(keep[:, :], keep[:, :], -1.0, 1.0, ALU.mult, ALU.add))
                    after(nc.vector.tensor_tensor(chosen[:, :, 0], chosen[:, :, 0], keep[:, :], ALU.add))
            zero()
        names = ("turned", "copied", "b2_done", "y_started", "hid_done", "h_act", "h_dve", "out_done", "added")
        sems, zero = ctx.enter_context(signals(nc, ["moe_" + n for n in names]))
        sem = dict(zip(names, sems))
        w1, w2, b1, b2 = sb("w1", [P, DFF]), sb("w2", [P, 4, P]), sb("b1", [P, 4]), sb("b2", [NE, P])
        sel_t = sb("sel_t", [NE, NT, P])
        h = sb("h", [P, 2, 4, 512])
        load(core, [(b2[:, :], dram["L1_ffn_b2"])])
        with nc.Block() as block:
            @block.tensor
            def _(pe):
                for g in range(NT // 4):
                    if g >= 2:
                        pe.wait_ge(sem["copied"], g - 1)
                    for i in range(4):
                        last = nc.tensor.transpose(bank[g % 2][0:NE, i * P:(i + 1) * P], chosen[:, 4 * g + i, :], core.ident[:, :])
                    last.then_inc(sem["turned"], 1)
                for g in range(NT // 4):
                    pe.wait_ge(sem["copied"], g + 1)
                    if g >= 2:
                        pe.wait_ge(sem["y_started"], g - 1)
                    for i in range(4):
                        last = nc.tensor.matmul(bank[2 + g % 2][:, i * P:(i + 1) * P], sel_t[:, 4 * g + i, :], b2[:, :],
                                                start=True, stop=True)
                    last.then_inc(sem["b2_done"], 1)

            @block.scalar
            def _(act):
                for g in range(NT // 4):
                    act.wait_ge(sem["turned"], g + 1)
                    nc.scalar.copy(sel_t[:, 4 * g:4 * g + 4, :], bank[g % 2][0:NE, :].rearrange("p (i q) -> p i q", i=4)).then_inc(sem["copied"], 1)

            @block.vector
            def _(dve):
                for g in range(NT // 4):
                    dve.wait_ge(sem["b2_done"], g + 1)
                    nc.vector.tensor_copy(core.y[:, 4 * g:4 * g + 4, :],
                                          bank[2 + g % 2][:, :].rearrange("p (i c) -> p i c", i=4)).then_inc(sem["y_started"], 1)
        zero()
        NBLK = TOK // 512
        with nc.Fori(0, NE) as e:
            load(core, [(w1[:, :], dram["L1_ffn_W1"][bass.ds(e, 1), :, :].rearrange("a p n -> p (a n)")),
                        (w2[:, :, :], dram["L1_ffn_W2"][bass.ds(e, 1), :, :].rearrange("a (c p) n -> p (a c) n", p=P)),
                        (b1[:, :], dram["L1_ffn_b1"][bass.ds(e, 1), :].rearrange("a (c p) -> p (a c)", p=P))])
            with nc.Block() as block:
                @block.tensor
                def _(pe):
                    def hidden(k):
                        for c in range(4):
                            if k >= 1:
                                pe.wait_ge(sem["h_act"] if c % 2 == 0 else sem["h_dve"], 2 * (k - 1) + c // 2 + 1)
                            nc.tensor.matmul(bank[c][:, :], w1[:, c * P:(c + 1) * P], core.xnt[:, k * 512:(k + 1) * 512],
                                             start=True, stop=True).then_inc(sem["hid_done"], 1)

                    def outputs(k):
                        pe.wait_ge(sem["h_act"], 2 * (k + 1))
                        pe.wait_ge(sem["h_dve"], 2 * (k + 1))
                        for i in range(4):
                            if k >= 1:
                                pe.wait_ge(sem["added"], 4 * (k - 1) + i + 1)
                            for c in range(4):
                                last = nc.tensor.matmul(bank[4 + i][:, 0:P], h[:, k % 2, c, i * P:(i + 1) * P], w2[:, c, :],
                                                        start=(c == 0), stop=(c == 3))
                            last.then_inc(sem["out_done"], 1)

                    for k in range(NBLK + 1):
                        if k < NBLK:
                            hidden(k)
                        if k >= 1:
                            outputs(k - 1)

                @block.scalar
                def _(act):
                    for k in range(NBLK):
                        if k >= 2:
                            act.wait_ge(sem["out_done"], 4 * (k - 1))
                        for c in (0, 2):
                            act.wait_ge(sem["hid_done"], 4 * k + c + 1)
                            nc.scalar.activation(h[:, k % 2, c, :], bank[c][:, :], ACT.Relu, bias=b1[:, c:c + 1]).then_inc(sem["h_act"], 1)

                @block.vector
                def _(dve):
                    for k in range(NBLK + 1):
                        if k < NBLK:
                            if k >= 2:
                                dve.wait_ge(sem["out_done"], 4 * (k - 1))
                            for c in (1, 3):
                                dve.wait_ge(sem["hid_done"], 4 * k + c + 1)
                                nc.vector.tensor_scalar(h[:, k % 2, c, :], bank[c][:, :], b1[:, c:c + 1], 0.0, ALU.add,
                                                        ALU.max).then_inc(sem["h_dve"], 1)
                        if k >= 1:
                            for i in range(4):
                                tile = 4 * (k - 1) + i
                                dve.wait_ge(sem["out_done"], tile + 1)
                                nc.vector.scalar_tensor_tensor(out=core.y[:, tile, :], in0=bank[4 + i][:, 0:P],
                                                               scalar=chosen[:, tile, bass.ds(e, 1)], in1=core.y[:, tile, :],
                                                               op0=ALU.mult, op1=ALU.add).then_inc(sem["added"], 1)
            zero()


def causal_attention_stage(core):
    nc, dram, bank = core.nc, core.dram, core.bank
    with ExitStack() as ctx:
        def sb(name, shape, dt=F32):
            return ctx.enter_context(nc.sbuf_tensor("l2a_" + name, shape, dt))

        own = ("x_ready", "qk_proj", "v_proj", "qk_act", "qk_dve", "v_act", "v_dve", "dve_step", "stored")
        names = own + Softmax.NAMES
        sems, zero = ctx.enter_context(signals(nc, ["l2a_" + n for n in names]))
        sem = dict(zip(names, sems))
        att = Softmax(core, sb, 64, False, sem, "mask_causal", 1.0 / 8.0)
        w = {n: sb("w" + n, [P, HEADS, 64]) for n in "qkv"}
        gamma, beta = sb("gamma", [P, P]), sb("beta", [P, P])
        xb, res = sb("xb", [P, SEQ]), sb("res", [P, TPB, P])
        stats, mv, rstd, tmp = sb("stats", [P, TPB, 6]), sb("mv", [P, TPB, 2]), sb("rstd", [P, TPB]), sb("tmp", [P, TPB])
        load(core, [(w[n][:, :, :], dram["L2_attn_W" + n].rearrange("h d e -> d h e")) for n in w] +
             [(att.wo[:, :, :], dram["L2_attn_Wo"].rearrange("(c p) n -> p c n", p=P)), (att.mask[:, :, :], att.mask_src),
              (gamma[:, :], spread(dram["L2_attn_gamma"])), (beta[:, :], spread(dram["L2_attn_beta"]))])
        with nc.Fori(0, NB) as b:
            with nc.Block() as block:
                def pair(n, hp):
                    return w[n][:, 2 * hp:2 * hp + 2, :].rearrange("p h e -> p (h e)")

                def copies(eng, copy, odd, qk_sem, v_sem):
                    for hp in range(odd, 8, 2):
                        eng.wait_ge(sem["qk_proj"], hp + 1)
                        copy(att.qt[:, hp, :], bank[hp % 4][:, 0:SEQ])
                        copy(att.kt[:, hp, :], bank[hp % 4][:, SEQ:2 * SEQ]).then_inc(qk_sem, 1)
                    for half in range(2):
                        eng.wait_ge(sem["v_proj"], 2 * odd + half + 1)
                        copy(att.v[:, odd, half * 512:(half + 1) * 512], bank[4 + 2 * odd + half][:, :]).then_inc(v_sem, 1)

                @block.scalar
                def _(act):
                    nc.scalar.copy(xb[:, :], core.xnt[:, bass.ds(b * SEQ, SEQ)]).then_inc(sem["x_ready"], 1)
                    copies(act, nc.scalar.copy, 0, sem["qk_act"], sem["v_act"])
                    att.scalar(act)

                @block.tensor
                def _(pe):
                    pe.wait_ge(sem["x_ready"], 1)
                    for hp in range(8):
                        if hp >= 4:
                            pe.wait_ge(sem["qk_act"] if hp % 2 == 0 else sem["qk_dve"], (hp - 4) // 2 + 1)
                        nc.tensor.matmul(bank[hp % 4][:, 0:SEQ], pair("q", hp), xb[:, :], start=True, stop=True)
                        nc.tensor.matmul(bank[hp % 4][:, SEQ:2 * SEQ], pair("k", hp), xb[:, :], start=True,
                                         stop=True).then_inc(sem["qk_proj"], 1)
                    for t in range(TPB):
                        for half in range(2):
                            nc.tensor.matmul(bank[4 + 2 * t + half][:, :], xb[:, t * P:(t + 1) * P],
                                             w["v"][:, 8 * half:8 * half + 8, :].rearrange("p h e -> p (h e)"),
                                             start=True, stop=True).then_inc(sem["v_proj"], 1)
                    att.tensor(pe, [(sem["qk_act"], 4), (sem["qk_dve"], 4)], [(sem["v_act"], 2), (sem["v_dve"], 2)])

                @block.vector
                def _(dve):
                    after = chain(dve, sem["dve_step"])
                    copies(dve, nc.vector.tensor_copy, 1, sem["qk_dve"], sem["v_dve"])
                    att.vector(dve, after)
                    dve.wait_ge(sem["y_done"], 1)
                    after(nc.vector.tensor_tensor(res[:, :, :], bank[4][:, 0:SEQ].rearrange("p (t c) -> p t c", t=TPB),
                                                  core.xn[:, bass.ds(b * TPB, TPB), :], ALU.add))
                    after(normalise_rows(nc, after, [res[:, t, :] for t in range(TPB)], [res[:, t, :] for t in range(TPB)],
                                         stats, mv, rstd, tmp, 1e-3))
                    affine_rows(nc, after, res[:, :, :], gamma[:, :], beta[:, :])(
                        core.s[:, bass.ds(b * TPB, TPB), :]).then_inc(sem["stored"], 1)
            zero()


def routed_ffn_stage(core):
    nc, dram, bank = core.nc, core.dram, core.bank
    with ExitStack() as ctx:
        def sb(name, shape, dt=F32):
            return ctx.enter_context(nc.sbuf_tensor("cd_" + name, shape, dt))

        weight = sb("weight", [P, NT])
        with ExitStack() as ctx2:
            def sb2(name, shape, dt=F32):
                return ctx2.enter_context(nc.sbuf_tensor("cd_" + name, shape, dt))

            names = ("rt_ready", "s_done", "dve_step", "max_ready", "sum_ready", "log_ready", "z_ready", "score_ready",
                     "stored", "spread_")
            sems, zero = ctx2.enter_context(signals(nc, ["cd_" + n for n in names]))
            sem = dict(zip(names, sems))
            rt, rtm = sb2("rt", [P, 1]), sb2("rtm", [P, NB, NB])
            s, r, u, e = sb2("s", [NB, SEQ]), sb2("r", [NB, SEQ]), sb2("u", [NB, SEQ]), sb2("e", [NB, SEQ])
            m, nm, total, log, a = (sb2(n, [NB, 1]) for n in ("m", "nm", "total", "log", "a"))
            row, mine, before = sb2("row", [P, NB, SEQ]), sb2("mine", [P, NT]), sb2("before", [P, TPB, SEQ])
            junk, more, same = sb2("junk", [P, 2, SEQ]), sb2("more", [P, NT]), sb2("same", [P, NT])
            score_dram = nc.dram_tensor("route_score", (NB, SEQ), F32, kind="Internal").ap()
            load(core, [(rt[:, :], column(dram["L2_ffn_routing_token"])), (before[:, :, :], dram["before"])])
            with nc.Block() as block:
                @block.vector
                def _(dve):
                    after = chain(dve, sem["dve_step"])
                    after(nc.vector.memset(rtm[:, :, :], 0.0))
                    for b in range(NB):
                        last = nc.vector.tensor_copy(rtm[:, b, b:b + 1], rt[:, :])
                    last.then_inc(sem["rt_ready"], 1)
                    dve.wait_ge(sem["s_done"], 1)
                    after(nc.vector.tensor_copy(s[:, :], bank[0][0:NB, 0:SEQ]))
                    after(nc.vector.tensor_scalar(r[:, :], s[:, :], 0.0, None, ALU.max))

                @block.tensor
                def _(pe):
                    pe.wait_ge(sem["rt_ready"], 1)
                    for b in range(NB):
                        last = nc.tensor.matmul(bank[0][0:NB, 0:SEQ], rtm[:, b, :], core.xnt[:, b * SEQ:(b + 1) * SEQ],
                                                start=(b == 0), stop=(b == NB - 1))
                    last.then_inc(sem["s_done"], 1)
            zero()
            UNROLL = 10
            with nc.Fori(0, ROUTE_ITERS // UNROLL) as _i:
                with nc.Block() as block:
                    @block.vector
                    def _(dve):
                        after = chain(dve, sem["dve_step"])
                        for k in range(UNROLL):
                            after(nc.vector.tensor_tensor_reduce(u[:, :], s[:, :], r[:, :], 1.0 / EPS_ROUTE, LOWEST,
                                                                 ALU.subtract, ALU.max, m[:, :]))
                            nc.vector.tensor_scalar(nm[:, :], m[:, :], -1.0, None, ALU.mult).then_inc(sem["max_ready"], 1)
                            dve.wait_ge(sem["log_ready"], k + 1)
                            after(nc.vector.tensor_tensor(a[:, :], log[:, :], m[:, :], ALU.add))
                            after(nc.vector.tensor_scalar(a[:, :], a[:, :], -EPS_ROUTE, float(np.float32(EPS_ROUTE) * np.log(np.float32(K_ROUTE))),
                                                          ALU.mult, ALU.add))
                            after(nc.vector.tensor_scalar(r[:, :], s[:, :], a[:, 0:1], 0.0, ALU.add, ALU.max))

                    @block.scalar
                    def _(act):
                        for k in range(UNROLL):
                            act.wait_ge(sem["max_ready"], k + 1)
                            nc.scalar.activation(e[:, :], u[:, :], ACT.Exp, bias=nm[:, 0:1], accum_out=total[:, :]).then_inc(sem["sum_ready"], 1)
                            act.wait_ge(sem["sum_ready"], k + 1)
                            nc.scalar.activation(log[:, :], total[:, :], ACT.Ln).then_inc(sem["log_ready"], 1)
                zero()
            with nc.Block() as block:
                @block.vector
                def _(dve):
                    after = chain(dve, sem["dve_step"])
                    after(nc.vector.scalar_tensor_tensor(out=u[:, :], in0=s[:, :], scalar=a[:, 0:1], in1=r[:, :],
                                                         op0=ALU.add, op1=ALU.subtract))
                    nc.vector.tensor_scalar(u[:, :], u[:, :], 1.0 / EPS_ROUTE, -87.336545, ALU.mult, ALU.max).then_inc(sem["z_ready"], 1)
                    dve.wait_ge(sem["spread_"], 32)
                    for b in range(NB):
                        for t in range(TPB):
                            i = b * TPB + t
                            after(nc.vector.tensor_scalar(junk[:, 0, :], row[:, b, :], mine[:, i:i + 1], 0.0, ALU.is_gt, ALU.add,
                                                          accum_out=more[:, i:i + 1]))
                            after(nc.vector.scalar_tensor_tensor(out=junk[:, 1, :], in0=row[:, b, :], scalar=mine[:, i:i + 1],
                                                                 in1=before[:, t, :], op0=ALU.is_equal, op1=ALU.mult,
                                                                 accum_out=same[:, i:i + 1]))
                    after(nc.vector.tensor_tensor(more[:, :], more[:, :], same[:, :], ALU.add))
                    after(nc.vector.tensor_scalar(more[:, :], more[:, :], float(NUM_HEAVY), None, ALU.is_lt))
                    after(nc.vector.tensor_scalar(same[:, :], mine[:, :], -1.0, 1.0, ALU.mult, ALU.add))
                    after(nc.vector.tensor_tensor(same[:, :], same[:, :], mine[:, :], ALU.add))
                    after(nc.vector.tensor_tensor(weight[:, :], same[:, :], more[:, :], ALU.mult))

                @block.scalar
                def _(act):
                    act.wait_ge(sem["z_ready"], 1)
                    nc.scalar.activation(e[:, :], u[:, :], ACT.Exp).then_inc(sem["score_ready"], 1)

                @block.sync
                def _(sp):
                    sp.wait_ge(sem["score_ready"], 1)
                    sp.dma_start(score_dram, e[:, :]).then_inc(sem["stored"], 16)
                    sp.wait_ge(sem["stored"], 16)
                    sp.dma_start(row[:, :, :].rearrange("p b q -> p (b q)"),
                                 score_dram.rearrange("(a b) q -> a (b q)", a=1).to_broadcast([P, TOK])).then_inc(sem["spread_"], 16)
                    sp.dma_start(mine[:, :], score_dram.rearrange("b (t p) -> p (b t)", p=P)).then_inc(sem["spread_"], 16)
            zero()
        names = ("dve_step", "xr_ready", "cols_done", "xg_ready", "hid_done", "h_ready", "out_done", "sum_ready", "light_added", "stored")
        sems, zero = ctx.enter_context(signals(nc, ["lh_" + n for n in names]))
        sem = dict(zip(names, sems))
        w1l, w2l = sb("w1l", [P, LIGHT]), sb("w2l", [LIGHT, P])
        w1h, w2h = sb("w1h", [P, HEAVY]), sb("w2h", [P, 4, P])
        b1l, b2l, b1h, b2h = sb("b1l", [LIGHT, 1]), sb("b2l", [P, P]), sb("b1h", [P, 4]), sb("b2h", [P, P])
        gl, gh = sb("gl", [P, 1]), sb("gh", [P, 1])
        xr, n2, rn, tmp = sb("xr", [P, 4, P]), sb("n2", [P, 4]), sb("rn", [P, 4]), sb("tmp", [P, 4])
        xl, xh = sb("xl", [P, 512]), sb("xh", [P, 512])
        hl, hh = sb("hl", [LIGHT, 512]), sb("hh", [P, 4, 512])
        heavy, both = sb("heavy", [P, 4, P]), sb("both", [P, 4, P])
        load(core, [(w1l[:, :], dram["L2_ffn_w1_light"]), (w2l[:, :], dram["L2_ffn_w2_light"]),
                    (w1h[:, :], dram["L2_ffn_w1_heavy"]), (w2h[:, :, :], dram["L2_ffn_w2_heavy"].rearrange("(c p) n -> p c n", p=P)),
                    (b1l[:, :], column(dram["L2_ffn_b1_light"])), (b2l[:, :], spread(dram["L2_ffn_b2_light"])),
                    (b1h[:, :], dram["L2_ffn_b1_heavy"].rearrange("(c p) -> p c", p=P)), (b2h[:, :], spread(dram["L2_ffn_b2_heavy"])),
                    (gl[:, :], column(dram["L2_ffn_gamma_light"])), (gh[:, :], column(dram["L2_ffn_gamma_heavy"]))])
        with nc.Fori(0, NT // 4) as i:
            with nc.Block() as block:
                @block.vector
                def _(dve):
                    after = chain(dve, sem["dve_step"])
                    for j in range(4):
                        x = core.xn[:, bass.ds(i * 4 + j, 1), :]
                        last = nc.vector.tensor_tensor(xr[:, j:j + 1, :], x, x, ALU.mult)
                    after(last)
                    after(nc.vector.tensor_reduce(n2[:, :], xr[:, :, :], AX.X, ALU.add))
                    after(nc.vector.tensor_scalar(n2[:, :], n2[:, :], 1e-24, None, ALU.max))
                    rsqrt(nc, after, rn[:, :], n2[:, :], tmp[:, :])
                    after(nc.vector.tensor_scalar(rn[:, :], rn[:, :], float(np.sqrt(P)), None, ALU.mult))
                    for j in range(4):
                        last = nc.vector.tensor_scalar(xr[:, j:j + 1, :], core.xn[:, bass.ds(i * 4 + j, 1), :], rn[:, j:j + 1], None,
                                                       ALU.mult)
                    last.then_inc(sem["xr_ready"], 1)
                    dve.wait_ge(sem["out_done"], 2)
                    after(nc.vector.tensor_tensor(heavy[:, :, :], bank[7][:, :].rearrange("p (j c) -> p j c", j=4),
                                                  b2h[:, :].rearrange("p (a c) -> p a c", a=1).to_broadcast([P, 4, P]), ALU.add))
                    for j in range(4):
                        last = nc.vector.scalar_tensor_tensor(out=both[:, j, :], in0=heavy[:, j, :],
                                                              scalar=weight[:, bass.ds(i * 4 + j, 1)],
                                                              in1=bank[6][:, j * P:(j + 1) * P], op0=ALU.mult, op1=ALU.add)
                    after(last)
                    nc.vector.tensor_tensor(core.y[:, bass.ds(i * 4, 4), :], both[:, :, :],
                                            b2l[:, :].rearrange("p (a c) -> p a c", a=1).to_broadcast([P, 4, P]),
                                            ALU.add).then_inc(sem["stored"], 1)

                @block.tensor
                def _(pe):
                    pe.wait_ge(sem["xr_ready"], 1)
                    for j in range(4):
                        last = nc.tensor.transpose(bank[0][:, j * P:(j + 1) * P], xr[:, j, :], core.ident[:, :])
                    last.then_inc(sem["cols_done"], 1)
                    pe.wait_ge(sem["xg_ready"], 2)
                    nc.tensor.matmul(bank[1][0:LIGHT, :], w1l[:, :], xl[:, :], start=True, stop=True).then_inc(sem["hid_done"], 1)
                    for c in range(4):
                        nc.tensor.matmul(bank[2 + c][:, :], w1h[:, c * P:(c + 1) * P], xh[:, :], start=True,
                                         stop=True).then_inc(sem["hid_done"], 1)
                    pe.wait_ge(sem["h_ready"], 1)
                    for j in range(4):
                        last = nc.tensor.matmul(bank[6][:, j * P:(j + 1) * P], hl[:, j * P:(j + 1) * P], w2l[:, :],
                                                start=True, stop=True)
                    last.then_inc(sem["out_done"], 1)
                    pe.wait_ge(sem["h_ready"], 5)
                    for j in range(4):
                        for c in range(4):
                            last = nc.tensor.matmul(bank[7][:, j * P:(j + 1) * P], hh[:, c, j * P:(j + 1) * P], w2h[:, c, :],
                                                    start=(c == 0), stop=(c == 3))
                    last.then_inc(sem["out_done"], 1)

                @block.scalar
                def _(act):
                    act.wait_ge(sem["cols_done"], 1)
                    nc.scalar.activation(xl[:, :], bank[0][:, :], ACT.Copy, scale=gl[:, 0:1]).then_inc(sem["xg_ready"], 1)
                    nc.scalar.activation(xh[:, :], bank[0][:, :], ACT.Copy, scale=gh[:, 0:1]).then_inc(sem["xg_ready"], 1)
                    act.wait_ge(sem["hid_done"], 1)
                    nc.scalar.activation(hl[:, :], bank[1][0:LIGHT, :], ACT.Gelu, bias=b1l[:, 0:1]).then_inc(sem["h_ready"], 1)
                    for c in range(4):
                        act.wait_ge(sem["hid_done"], c + 2)
                        nc.scalar.activation(hh[:, c, :], bank[2 + c][:, :], ACT.Gelu, bias=b1h[:, c:c + 1]).then_inc(sem["h_ready"], 1)
            zero()


def small_head_attention_stage(core):
    nc, dram, bank = core.nc, core.dram, core.bank
    with ExitStack() as ctx:
        def sb(name, shape, dt=F32):
            return ctx.enter_context(nc.sbuf_tensor("l3a_" + name, shape, dt))

        own = ("w_ready", "x_ready", "proj_done", "rot_done", "v_proj", "cos_ready", "roped", "heads_ready", "v_ready", "dve_step", "stored")
        names = own + Softmax.NAMES
        sems, zero = ctx.enter_context(signals(nc, ["l3a_" + n for n in names]))
        sem = dict(zip(names, sems))
        att = Softmax(core, sb, 8, False, sem, "mask_causal", float(1.0 / np.sqrt(np.float32(8.0))))
        w, wr = {n: sb("w" + n, [P, P]) for n in "qkv"}, {n: sb("wr" + n, [P, P]) for n in "qk"}
        rope, head4 = sb("rope", [P, 2, SEQ]), sb("head4", [P, 4])
        xb, part, q = sb("xb", [P, SEQ]), sb("part", [P, 2, SEQ]), sb("q", [P, SEQ])
        load(core, [(w[n][:, :], dram["L3_attn_W" + n]) for n in w] +
             [(att.wo[:, 0, :], dram["L3_attn_Wo"]), (att.mask[:, :, :], att.mask_src), (rope[:, :, :], dram["rope_l3"]),
              (head4[:, :], dram["head_of_4"])])
        with nc.Block() as block:
            @block.vector
            def _(dve):
                for n in "qk":
                    src, dst = (z[n][:, :].rearrange("p (c s) -> p c s", s=2) for z in (w, wr))
                    nc.vector.tensor_scalar(dst[:, :, 0], src[:, :, 1], -1.0, None, ALU.mult)
                    last = nc.vector.tensor_copy(dst[:, :, 1], src[:, :, 0])
                last.then_inc(sem["w_ready"], 1)
        zero()
        with nc.Fori(0, NB) as b:
            with nc.Block() as block:
                @block.scalar
                def _(act):
                    nc.scalar.copy(xb[:, :], core.xnt[:, bass.ds(b * SEQ, SEQ)]).then_inc(sem["x_ready"], 1)
                    act.wait_ge(sem["v_proj"], 1)
                    nc.scalar.copy(att.v[:, :, :], bank[2][:, 0:SEQ].rearrange("p (t c) -> p t c", t=TPB)).then_inc(sem["v_ready"], 1)
                    att.scalar(act)

                @block.tensor
                def _(pe):
                    pe.wait_ge(sem["x_ready"], 1)
                    for i, n in enumerate("qk"):
                        last = nc.tensor.matmul(bank[0][:, i * SEQ:(i + 1) * SEQ], w[n][:, :], xb[:, :], start=True, stop=True)
                    last.then_inc(sem["proj_done"], 1)
                    for i, n in enumerate("qk"):
                        last = nc.tensor.matmul(bank[1][:, i * SEQ:(i + 1) * SEQ], wr[n][:, :], xb[:, :], start=True, stop=True)
                    last.then_inc(sem["rot_done"], 1)
                    for t in range(TPB):
                        last = nc.tensor.matmul(bank[2][:, t * P:(t + 1) * P], xb[:, t * P:(t + 1) * P], w["v"][:, :],
                                                start=True, stop=True)
                    last.then_inc(sem["v_proj"], 1)
                    pe.wait_ge(sem["v_ready"], 1)
                    att.tensor(pe, [(sem["heads_ready"], 4), (sem["roped"], 2)], [])

                @block.vector
                def _(dve):
                    after = chain(dve, sem["dve_step"])
                    table = lambda n: rope[:, n, :].rearrange("p (a q) -> p a q", a=1).to_broadcast([P, 2, SEQ])
                    both = lambda i: bank[i][:, :].rearrange("p (n q) -> p n q", n=2)
                    dve.wait_ge(sem["proj_done"], 1)
                    after(nc.vector.tensor_tensor(part[:, :, :], both(0), table(0), ALU.mult))
                    dve.wait_ge(sem["rot_done"], 1)
                    for i, dst in enumerate((q[:, :], att.kt[:, 0, :])):
                        after(nc.vector.tensor_tensor(dst, bank[1][:, i * SEQ:(i + 1) * SEQ], rope[:, 1, :], ALU.mult))
                        nc.vector.tensor_tensor(dst, dst, part[:, i, :], ALU.add).then_inc(sem["roped"], 1)
                    dve.wait_ge(sem["roped"], 1)
                    for j in range(4):
                        nc.vector.tensor_scalar(att.qt[:, j, :], q[:, :], head4[:, j:j + 1], None, ALU.mult).then_inc(sem["heads_ready"], 1)
                    att.vector(dve, after)
                    dve.wait_ge(sem["y_done"], 1)
                    nc.vector.tensor_copy(core.s[:, bass.ds(b * TPB, TPB), :],
                                          bank[4][:, 0:SEQ].rearrange("p (t c) -> p t c", t=TPB)).then_inc(sem["stored"], 1)
            zero()


def grouped_ffn_stage(core):
    nc, dram, bank = core.nc, core.dram, core.bank
    with ExitStack() as ctx:
        def sb(name, shape, dt=F32):
            return ctx.enter_context(nc.sbuf_tensor("grp_" + name, shape, dt))

        names = ("loaded", "turned", "w_ready", "hid_done", "h_ready", "out_done", "stored")
        sems, zero = ctx.enter_context(signals(nc, ["grp_" + n for n in names]))
        sem = dict(zip(names, sems))
        w1, w2, w1t, w2t = (sb(n, [P, 4, P]) for n in ("w1", "w2", "w1t", "w2t"))
        b1, b2, h = sb("b1", [P, 4]), sb("b2", [P, P]), sb("h", [P, 4, GTOK])
        with nc.Fori(0, NG) as g:
            with nc.Block() as block:
                @block.sync
                def _(sp):
                    one = bass.ds(g, 1)
                    sp.dma_start(w1[:, :, :], dram["L3_ffn_W1"][one, :, :].rearrange("a (c p) h -> p (a c) h", p=P)).then_inc(sem["loaded"], 16)
                    sp.dma_start(w2[:, :, :], dram["L3_ffn_W2"][one, :, :].rearrange("a p (c o) -> p (a c) o", o=P)).then_inc(sem["loaded"], 16)
                    sp.dma_start(b1[:, :], dram["L3_ffn_b1"][one, :].rearrange("a (c p) -> p (a c)", p=P)).then_inc(sem["loaded"], 16)
                    sp.dma_start(b2[:, :], dram["L3_ffn_b2"][one, :].to_broadcast([P, P])).then_inc(sem["loaded"], 16)
                    sp.wait_ge(sem["loaded"], 64)

                @block.tensor
                def _(pe):
                    pe.wait_ge(sem["loaded"], 64)
                    for i, w in enumerate((w1, w2)):
                        for c in range(4):
                            last = nc.tensor.transpose(bank[i][:, c * P:(c + 1) * P], w[:, c, :], core.ident[:, :])
                        last.then_inc(sem["turned"], 1)
                    pe.wait_ge(sem["w_ready"], 1)
                    for c in range(4):
                        nc.tensor.matmul(bank[2 + c][:, :], w1t[:, c, :], core.xnt[:, bass.ds(g * GTOK, GTOK)], start=True,
                                         stop=True).then_inc(sem["hid_done"], 1)
                    pe.wait_ge(sem["w_ready"], 2)
                    pe.wait_ge(sem["h_ready"], 4)
                    for j in range(4):
                        for c in range(4):
                            last = nc.tensor.matmul(bank[6][:, j * P:(j + 1) * P], h[:, c, j * P:(j + 1) * P], w2t[:, c, :],
                                                    start=(c == 0), stop=(c == 3))
                    last.then_inc(sem["out_done"], 1)

                @block.scalar
                def _(act):
                    for c in range(4):
                        act.wait_ge(sem["hid_done"], c + 1)
                        nc.scalar.activation(h[:, c, :], bank[2 + c][:, :], ACT.Identity, bias=b1[:, c:c + 1]).then_inc(sem["h_ready"], 1)

                @block.vector
                def _(dve):
                    for i, wt in enumerate((w1t, w2t)):
                        dve.wait_ge(sem["turned"], i + 1)
                        nc.vector.tensor_copy(wt[:, :, :], bank[i][:, :].rearrange("p (c q) -> p c q", c=4)).then_inc(sem["w_ready"], 1)
                    dve.wait_ge(sem["out_done"], 1)
                    nc.vector.tensor_tensor(core.y[:, bass.ds(g * 4, 4), :], bank[6][:, :].rearrange("p (j c) -> p j c", j=4),
                                            b2[:, :].rearrange("p (a c) -> p a c", a=1).to_broadcast([P, 4, P]),
                                            ALU.add).then_inc(sem["stored"], 1)
            zero()


LAYERS_RUN = DEPTH


def program(nc, dram, out, stop=None):
    with ExitStack() as ctx:
        ctx.enter_context(nc.allow_non_contiguous_dma(reason="vectors of a few hundred elements laid over partitions"))
        core = Core(nc, dram, ctx)
        load(core, [(core.x[:, :, :], dram["L0_attn_x"].rearrange("b (t p) c -> p (b t) c", p=P)),
                    (core.ident[:, :], dram["ident"])])

        def store(rows):
            with signals(nc, ["out_stored"]) as ((out_stored,), zero):
                with nc.Block() as block:
                    @block.sync
                    def _(sp):
                        sp.dma_start(out.rearrange("b (t p) c -> p (b t) c", p=P), rows[:, :, :]).then_inc(out_stored, 16)
                        sp.wait_ge(out_stored, 16)

        for name, stage, shown in stages():
            stage(core)
            core.stage += 1
            if stop == name:
                return store(shown(core))
        store(core.x)


def stages():
    return [
        ("ln0", layer_norm_stage, lambda c: c.xn),
        ("s0", linear_attention_stage, lambda c: c.s),
        ("g0", local_transformer_stage, lambda c: c.y),
        ("x0", combine_stage, lambda c: c.x),
        ("ln1", layer_norm_stage, lambda c: c.xn),
        ("s1", gelu_linear_attention_stage, lambda c: c.s),
        ("g1", experts_stage, lambda c: c.y),
        ("x1", combine_stage, lambda c: c.x),
        ("ln2", layer_norm_stage, lambda c: c.xn),
        ("s2", causal_attention_stage, lambda c: c.s),
        ("g2", routed_ffn_stage, lambda c: c.y),
        ("x2", combine_stage, lambda c: c.x),
        ("ln3", layer_norm_stage, lambda c: c.xn),
        ("s3", small_head_attention_stage, lambda c: c.s),
        ("g3", grouped_ffn_stage, lambda c: c.y),
        ("x3", combine_stage, lambda c: c.x),
    ]


def kernel(**inputs):
    import concourse.bacc as bacc
    from concourse.bass_utils import run_bass_kernel_spmd

    arrays = {f"in_{k}": np.ascontiguousarray(v) for k, v in inputs.items()}
    arrays.update({f"table_{k}": v for k, v in shape_constants().items()})
    nc = bacc.Bacc("TRN2", target_bir_lowering=False, num_devices=1)
    dram = {n.split("_", 1)[1]: nc.dram_tensor(n, a.shape, F32, kind="ExternalInput").ap() for n, a in arrays.items()}
    out = nc.dram_tensor("out", (NB, SEQ, P), F32, kind="ExternalOutput").ap()
    program(nc, dram, out)
    r = run_bass_kernel_spmd(nc, [arrays], core_ids=[0])
    return r.results[0]["out"]
```

```python
from contextlib import ExitStack, contextmanager

import numpy as np

import concourse.bass as bass
from concourse import mybir

F32 = mybir.dt.float32
I32 = mybir.dt.int32
BF16 = mybir.dt.bfloat16
ALU = mybir.AluOpType
ACT = mybir.ActivationFunctionType
AX = mybir.AxisListType

P = 128
NB, SEQ = 16, 256
TPB = SEQ // P
NT = NB * TPB
TOK = NB * SEQ
HEADS = 16
NEG = -1.0e20
LOWEST = -3.0e38

DEPTH, DH, WINDOW = 6, 64, 32
LOOP_WINDOWS = 6
INNER = HEADS * DH
DIM_INNER = int(P * 4 * 2 / 3)
HID_CHUNKS = [(0, 128), (128, 128), (256, DIM_INNER - 256)]
QK_SCALE = 8.0
NE, DFF = 8, 512
CAPACITY = int(np.ceil(TOK / NE * 1.25))
ROUTE_ITERS, EPS_ROUTE, K_ROUTE, NUM_HEAVY = 50, 0.1, 8.0, 128
LIGHT, HEAVY = 64, 512
NG, INTER = 8, 512
GTOK = TOK // NG


def shape_constants():
    c = {}
    i = np.arange(P)
    c["ident"] = np.eye(P, dtype=np.float32)
    c["upto"] = (i[:, None] <= i[None, :]).astype(np.float32)
    causal = np.full((P, TPB, SEQ), NEG, np.float32)
    local = np.full((P, TPB, SEQ), NEG, np.float32)
    for t in range(TPB):
        q = t * P + i
        k = np.arange(SEQ)
        causal[:, t][k[None, :] <= q[:, None]] = 0.0
        first = local_first_key(t)
        w = local_width(t)
        kk = first + np.arange(w)
        ok = (kk[None, :] <= q[:, None]) & (q[:, None] <= kk[None, :] + WINDOW)
        ok &= (kk[None, :] // WINDOW) >= (q[:, None] // WINDOW - 1)
        local[:, t, :w][ok] = 0.0
    c["mask_causal"], c["mask_local"] = causal, local
    half = np.arange(0, DH, 2, dtype=np.float32)
    inv_freq = (np.float32(1.0) / np.float32(10000.0) ** (half / np.float32(DH))).astype(np.float32)
    t = np.arange(SEQ, dtype=np.float32)
    freqs = (t[:, None] * inv_freq[None, :]).astype(np.float32)
    freqs = np.concatenate([freqs, freqs], -1)
    base = ((half + np.float32(0.4 * DH)) / np.float32(1.4 * DH)).astype(np.float32)
    power = ((t - SEQ // 2) / np.float32(WINDOW // 2)).astype(np.float32)
    scale = (base[None, :] ** power[:, None]).astype(np.float32)
    scale = np.concatenate([scale, scale], -1)
    sign = np.where(np.arange(DH) < DH // 2, -1.0, 1.0).astype(np.float32)
    cos, sin = np.cos(freqs), np.sin(freqs) * sign
    inv = (np.float32(1.0) / scale).astype(np.float32)
    tab = np.stack([cos * scale, sin * scale, cos * inv, sin * inv], 1)
    c["rope_local"] = np.ascontiguousarray(tab.reshape(TPB, P, 4, DH).transpose(1, 0, 2, 3)).astype(np.float32)
    for name, d in (("rope_l1", P), ("rope_l3", 8)):
        f = (np.float32(1.0) / np.float32(10000.0) ** (np.arange(0, d, 2, dtype=np.float32) / np.float32(d))).astype(np.float32)
        ang = (t[:, None] * f[None, :]).astype(np.float32)
        both = np.stack([np.repeat(np.cos(ang), 2, 1), np.repeat(np.sin(ang), 2, 1)], 0)
        c[name] = np.ascontiguousarray(np.tile(both, (1, 1, P // d)).transpose(2, 0, 1)).astype(np.float32)
    swap = np.zeros((P, P), np.float32)
    swap[np.arange(1, P, 2), np.arange(0, P, 2)] = -1.0
    swap[np.arange(0, P, 2), np.arange(1, P, 2)] = 1.0
    c["swap"] = swap
    c["strictly_before"] = (i[:, None] < i[None, :]).astype(np.float32)
    c["head_block"] = (i[:, None] // 8 == i[None, :] // 8).astype(np.float32)
    c["head_of_4"] = (((i[:, None] // 8) % 4) == np.arange(4)[None, :]).astype(np.float32)
    before = np.arange(SEQ)[None, None, :] < (np.arange(TPB)[None, :, None] * P + i[:, None, None])
    c["before"] = before.astype(np.float32)
    c["expert_no"] = np.tile(np.arange(NE, dtype=np.float32), (P, NT, 1))
    return c


def local_first_key(t):
    return 0 if t == 0 else t * P - WINDOW


def local_width(t):
    return (t + 1) * P - local_first_key(t)


@contextmanager
def signals(nc, names):
    with ExitStack() as c:
        s = [c.enter_context(nc.semaphore(n)) for n in names]

        def zero():
            numbers = sorted(x.num for x in s)
            starts = [n for n in numbers if n - 1 not in numbers]
            for first in starts:
                end = first
                while end in numbers:
                    end += 1
                nc.sync.sem_clear(range(first, end))
            nc.all_engine_barrier(sem_only=True)

        zero()
        yield s, zero


def chain(eng, sem):
    n = [0]

    def after(ins):
        n[0] += 1
        ins.then_inc(sem, 1)
        eng.wait_ge(sem, n[0])

    return after


def slots_before(slots, slot):
    low, high = 0, len(slots)
    while low < high:
        middle = (low + high) // 2
        low, high = (middle + 1, high) if slots[middle] < slot else (low, middle)
    return low


class Signals:

    def __init__(self, sem, when):
        self.sem, self.when, self.start, self.sent = sem, {n: sorted(w) for n, w in when.items()}, 0, {}

    def begin(self, start):
        self.start, self.sent = start, {}

    def end(self, stop):
        for n, slots in self.when.items():
            due = slots_before(slots, stop) - slots_before(slots, self.start)
            assert self.sent.get(n, 0) == due, (n, self.start, self.sent.get(n, 0), due)

    def wait(self, eng, name, count):
        here = count - slots_before(self.when[name], self.start)
        if here > 0:
            eng.wait_ge(self.sem[name], here)

    def done(self, ins, name):
        self.sent[name] = self.sent.get(name, 0) + 1
        ins.then_inc(self.sem[name], 1)


def run_windows(nc, sig, zero, emit, last_slot):
    first = 3 * 16
    span = LOOP_WINDOWS * 16
    turns = (NB - 1 - 3) // LOOP_WINDOWS
    rest = first + turns * span

    def part(start, stop, shift):
        sig.begin(start)
        with nc.Block() as block:
            emit(block, range(start, stop), shift)
        sig.end(stop)
        zero()

    part(0, first, 0)
    with nc.Fori(0, turns) as turn:
        part(first, first + span, turn * LOOP_WINDOWS)
    part(rest, last_slot, 0)


def rsqrt(nc, after, out, x, tmp):
    after(nc.vector.tensor_scalar(tmp.bitcast(I32), x.bitcast(I32), 1, None, ALU.logical_shift_right))
    after(nc.vector.tensor_scalar(out.bitcast(I32), tmp.bitcast(I32), -1.0, float(0x5F3759DF), ALU.mult, ALU.add))
    after(nc.vector.tensor_scalar(x, x, -0.5, None, ALU.mult))
    for _ in range(3):
        after(nc.vector.tensor_tensor(tmp, out, out, ALU.mult))
        after(nc.vector.tensor_tensor(tmp, tmp, x, ALU.mult))
        after(nc.vector.scalar_tensor_tensor(out=out, in0=tmp, scalar=1.5, in1=out, op0=ALU.add, op1=ALU.mult))


class Core:

    def __init__(self, nc, dram, ctx):
        self.nc, self.dram, self.stage = nc, dram, 0

        def sb(name, shape, dt=F32):
            return ctx.enter_context(nc.sbuf_tensor(name, shape, dt))

        self.x = sb("x_rows", [P, NT, P])
        self.xn = sb("xn_rows", [P, NT, P])
        self.xnt = sb("xn_cols", [P, TOK])
        self.s = sb("s_rows", [P, NT, P])
        self.y = sb("y_rows", [P, NT, P])
        self.ident = sb("ident", [P, P])
        self.bank = [ctx.enter_context(nc.psum_tensor(f"bank{i}", [P, 512], F32)) for i in range(8)]

    def name(self, base):
        return f"{base}_{self.stage}"


def load(core, pairs):
    nc = core.nc
    with signals(nc, ["loaded"]) as ((loaded,), zero):
        with nc.Block() as block:
            @block.sync
            def _(sp):
                for dst, src in pairs:
                    sp.dma_start(dst, src).then_inc(loaded, 16)
                sp.wait_ge(loaded, 16 * len(pairs))
        zero()


def column(ap):
    return ap.rearrange("(p a) -> p a", a=1)


def spread(ap):
    return ap.rearrange("(a n) -> a n", a=1).to_broadcast([P, ap.shape[0]])


def normalise_rows(nc, after, x_tiles, out_tiles, stats, mv, rstd, tmp, eps):
    n = len(x_tiles)
    for j in range(n):
        last = nc.vector.bn_stats(stats[:, j, :], x_tiles[j])
    after(last)
    return normalise_by(nc, after, x_tiles, out_tiles, stats, mv, rstd, tmp, eps)


def normalise_by(nc, after, x_tiles, out_tiles, stats, mv, rstd, tmp, eps):
    n = len(x_tiles)
    for j in range(n):
        last = nc.vector.bn_aggr(mv[:, j, :], stats[:, j, :])
    after(last)
    after(nc.vector.tensor_scalar(mv[:, 0:n, 1], mv[:, 0:n, 1], eps, None, ALU.add))
    rsqrt(nc, after, rstd[:, 0:n], mv[:, 0:n, 1], tmp[:, 0:n])
    return [nc.vector.tensor_scalar(out_tiles[j], x_tiles[j], mv[:, j, 0:1], rstd[:, j:j + 1], ALU.subtract, ALU.mult)
            for j in range(n)]


def layer_norm_stage(core):
    nc, bank, G = core.nc, core.bank, 4
    with ExitStack() as ctx:
        stats = ctx.enter_context(nc.sbuf_tensor(core.name("ln_stats"), [P, NT, 6], F32))
        mv = ctx.enter_context(nc.sbuf_tensor(core.name("ln_mv"), [P, NT, 2], F32))
        rstd = ctx.enter_context(nc.sbuf_tensor(core.name("ln_rstd"), [P, NT], F32))
        tmp = ctx.enter_context(nc.sbuf_tensor(core.name("ln_tmp"), [P, NT], F32))
        (dve_step, rows_ready, turned, copied), zero = ctx.enter_context(
            signals(nc, [core.name(n) for n in ("ln_dve_step", "ln_rows_ready", "ln_turned", "ln_copied")]))
        with nc.Block() as block:
            @block.vector
            def _(dve):
                after = chain(dve, dve_step)
                tiles = [core.x[:, j, :] for j in range(NT)]
                for ins in normalise_rows(nc, after, tiles, [core.xn[:, j, :] for j in range(NT)], stats, mv, rstd, tmp, 1e-5):
                    ins.then_inc(rows_ready, 1)

            @block.tensor
            def _(pe):
                for j in range(NT):
                    pe.wait_ge(rows_ready, j + 1)
                    if j % G == 0 and j >= 2 * G:
                        pe.wait_ge(copied, j // G - 1)
                    ins = nc.tensor.transpose(bank[j // G % 2][:, (j % G) * P:(j % G + 1) * P], core.xn[:, j, :], core.ident[:, :])
                    if j % G == G - 1:
                        ins.then_inc(turned, 1)

            @block.scalar
            def _(act):
                for g in range(NT // G):
                    act.wait_ge(turned, g + 1)
                    nc.scalar.copy(core.xnt[:, g * G * P:(g + 1) * G * P], bank[g % 2][:, :]).then_inc(copied, 1)
        zero()


def layer_norm_of_branch(core, eps, gamma, beta):
    nc = core.nc
    with ExitStack() as ctx:
        stats = ctx.enter_context(nc.sbuf_tensor(core.name("bn_stats"), [P, NT, 6], F32))
        mv = ctx.enter_context(nc.sbuf_tensor(core.name("bn_mv"), [P, NT, 2], F32))
        rstd = ctx.enter_context(nc.sbuf_tensor(core.name("bn_rstd"), [P, NT], F32))
        tmp = ctx.enter_context(nc.sbuf_tensor(core.name("bn_tmp"), [P, NT], F32))
        (dve_step, rows_ready, scaled, pool_step, stored), zero = ctx.enter_context(
            signals(nc, [core.name(n) for n in ("bn_dve_step", "bn_rows_ready", "bn_scaled", "bn_pool_step", "bn_stored")]))
        half = NT // 2
        wide = lambda v: v.rearrange("p (a c) -> p a c", a=1).to_broadcast([P, half, P])
        with nc.Block() as block:
            @block.vector
            def _(dve):
                after = chain(dve, dve_step)
                tiles = [core.s[:, j, :] for j in range(NT)]
                for ins in normalise_rows(nc, after, tiles, tiles, stats, mv, rstd, tmp, eps):
                    ins.then_inc(rows_ready, 1)
                dve.wait_ge(rows_ready, NT)
                nc.vector.tensor_tensor(core.s[:, half:NT, :], core.s[:, half:NT, :], wide(gamma), ALU.mult).then_inc(scaled, 1)
                dve.wait_ge(scaled, 1)
                nc.vector.tensor_tensor(core.s[:, half:NT, :], core.s[:, half:NT, :], wide(beta), ALU.add).then_inc(stored, 1)

            @block.gpsimd
            def _(pool):
                n = half // 2
                wide = lambda v: v.rearrange("p (a c) -> p a c", a=1).to_broadcast([P, n, P])
                for g in range(2):
                    rows = core.s[:, g * n:(g + 1) * n, :]
                    pool.wait_ge(rows_ready, (g + 1) * n)
                    nc.gpsimd.tensor_tensor(rows, rows, wide(gamma), ALU.mult).then_inc(pool_step, 1)
                    pool.wait_ge(pool_step, g + 1)
                    nc.gpsimd.tensor_tensor(rows, rows, wide(beta), ALU.add).then_inc(stored, 1)
        zero()


def combine_stage(core):
    nc, G = core.nc, 8
    with ExitStack() as ctx:
        (gated, multiplied, added), zero = ctx.enter_context(signals(nc, [core.name(n) for n in ("cb_gated", "cb_multiplied", "cb_added")]))
        groups = [slice(i * G, (i + 1) * G) for i in range(NT // G)]
        with nc.Block() as block:
            @block.scalar
            def _(act):
                for g in groups:
                    nc.scalar.activation(core.y[:, g, :], core.y[:, g, :], ACT.Silu).then_inc(gated, 1)

            @block.vector
            def _(dve):
                for i, g in enumerate(groups):
                    dve.wait_ge(gated, i + 1)
                    nc.vector.tensor_tensor(core.y[:, g, :], core.y[:, g, :], core.s[:, g, :], ALU.mult).then_inc(multiplied, 1)
                    dve.wait_ge(multiplied, i + 1)
                    nc.vector.tensor_tensor(core.x[:, g, :], core.y[:, g, :], core.x[:, g, :], ALU.add).then_inc(added, 1)
        zero()


def linear_attention_stage(core):
    nc, dram, bank = core.nc, core.dram, core.bank
    TURN, SLOTS, DIAG = 4, 8, P + 8
    with ExitStack() as ctx:
        def sb(name, shape, dt=F32):
            return ctx.enter_context(nc.sbuf_tensor("l0a_" + name, shape, dt))

        names = ("set_up", "x_ready", "qk_proj", "v_proj", "low_ready", "high_ready", "exp_ready", "qk_ready", "v_ready",
                 "kh_ready", "kr_done", "kr_ready", "kv_done", "state_ready", "kc_ready", "den_done", "den_added", "rec_ready",
                 "scored", "masked", "o_done", "ot_ready", "y_done", "stored")
        sems, zero = ctx.enter_context(signals(nc, ["l0a_" + n for n in names]))
        sem = dict(zip(names, sems))
        w = {n: sb(n, [P, P]) for n in ("wq", "wk", "wv", "wo")}
        bq, bk = sb("bq", [P, 1]), sb("bk", [P, 1])
        bv, bo = sb("bv", [P, P]), sb("bo", [P, P])
        upto, ones, block_, head4 = sb("upto", [P, P]), sb("ones", [P, P]), sb("block", [P, P]), sb("head4", [P, 4])
        xb, low, qk = sb("xb", [P, 2, SEQ]), sb("low", [P, 2, SEQ]), sb("qk", [P, 2, 2, SEQ])
        kh, kr = sb("kh", [P, 2, 4, SEQ]), sb("kr", [P, TPB, P])
        vz = sb("vz", [P, 2, TPB, HEADS * DIAG])
        state, kc, rec = sb("state", [P, 2, P]), sb("kc", [P, SEQ]), sb("rec", [P, 2, SEQ])
        st, ot = sb("st", [P, 2, 4, P]), sb("ot", [P, 2, SEQ])
        load(core, [(w[n][:, :], dram["L0_attn_" + n]) for n in w] +
             [(bq[:, :], column(dram["L0_attn_bq"])), (bk[:, :], column(dram["L0_attn_bk"])),
              (bv[:, :], spread(dram["L0_attn_bv"])), (bo[:, :], spread(dram["L0_attn_bo"])),
              (upto[:, :], dram["upto"]), (block_[:, :], dram["head_block"]), (head4[:, :], dram["head_of_4"])])
        with nc.Block() as block:
            @block.vector
            def _(dve):
                nc.vector.memset(vz[:, :, :, :], 0.0).then_inc(sem["set_up"], 1)
                nc.vector.memset(ones[:, :], 1.0).then_inc(sem["set_up"], 1)
        zero()
        by_head = lambda m, t: vz[:, m, t, :].rearrange("p (h c) -> p h c", c=DIAG)[:, :, 0:8]
        slots = range(SLOTS * (TURN + 1) + 5)

        def batch(slot, step):
            j, s = divmod(slot - step, SLOTS)
            return j if s == 0 and 0 <= j < TURN else None

        def unit(n):
            return n // SLOTS, n % SLOTS // 4, n % 4

        with nc.Fori(0, NB // TURN) as turn:
            with nc.Block() as block:
                @block.scalar
                def _(act):
                    for slot in slots:
                        if (j := batch(slot, 0)) is not None:
                            if j >= 2:
                                act.wait_ge(sem["v_proj"], j - 1)
                            nc.scalar.copy(xb[:, j % 2, :], core.xnt[:, bass.ds((turn * TURN + j) * SEQ, SEQ)]).then_inc(sem["x_ready"], 1)
                        if (j := batch(slot, 3)) is not None:
                            act.wait_ge(sem["low_ready"], 2 * (j + 1))
                            nc.scalar.activation(low[:, :, :], low[:, :, :], ACT.Exp).then_inc(sem["exp_ready"], 1)
                        if (j := batch(slot, 6)) is not None:
                            act.wait_ge(sem["kr_done"], j + 1)
                            if j >= 1:
                                act.wait_ge(sem["kv_done"], j)
                            nc.scalar.copy(kr[:, :, :], bank[1][:, SEQ:2 * SEQ].rearrange("p (t c) -> p t c", t=TPB)).then_inc(sem["kr_ready"], 1)

                @block.gpsimd
                def _(pool):
                    for j in range(TURN):
                        pool.wait_ge(sem["qk_ready"], j + 1)
                        if j >= 2:
                            pool.wait_ge(sem["scored"], SLOTS * (j - 1))
                        for i in range(4):
                            nc.gpsimd.tensor_scalar(kh[:, j % 2, i, :], qk[:, j % 2, 1, :], head4[:, i:i + 1], None,
                                                    ALU.mult).then_inc(sem["kh_ready"], 1)

                @block.tensor
                def _(pe):
                    for slot in slots:
                        if 0 <= (n := slot - 10) < SLOTS * TURN:
                            (j, t, g), to = unit(n), bank[6 + n // SLOTS % 2]
                            if n % SLOTS == 0 and j >= 2:
                                pe.wait_ge(sem["stored"], j - 1)
                            if t == 1 and g == 0:
                                pe.wait_ge(sem["state_ready"], j + 1)
                                nc.tensor.matmul(to[:, P:2 * P], state[:, j % 2, :], qk[:, j % 2, 0, P:SEQ], start=True, stop=False)
                            pe.wait_ge(sem["masked"], n + 1)
                            for i in range(4):
                                h = 4 * g + i
                                last = nc.tensor.matmul(to[:, t * P:(t + 1) * P], vz[:, j % 2, t, h * P:(h + 1) * P], st[:, n % 2, i, :],
                                                        start=(t == 0 and h == 0), stop=(h == HEADS - 1))
                            last.then_inc(sem["o_done"], 1)
                        if (j := batch(slot, 1)) is not None:
                            pe.wait_ge(sem["x_ready"], j + 1)
                            if j >= 1:
                                pe.wait_ge(sem["high_ready"], 2 * j)
                                pe.wait_ge(sem["kr_ready"], j)
                            for i, n in enumerate(("wq", "wk")):
                                last = nc.tensor.matmul(bank[0][:, i * SEQ:(i + 1) * SEQ], w[n][:, :], xb[:, j % 2, :], start=True, stop=True)
                            last.then_inc(sem["qk_proj"], 1)
                            for t in range(TPB):
                                last = nc.tensor.matmul(bank[1][:, t * P:(t + 1) * P], xb[:, j % 2, t * P:(t + 1) * P], w["wv"][:, :],
                                                        start=True, stop=True)
                            last.then_inc(sem["v_proj"], 1)
                        if (j := batch(slot, 5)) is not None:
                            pe.wait_ge(sem["qk_ready"], j + 1)
                            pe.wait_ge(sem["v_ready"], j + 1)
                            for t in range(TPB):
                                last = nc.tensor.transpose(bank[1][:, SEQ + t * P:SEQ + (t + 1) * P], qk[:, j % 2, 1, t * P:(t + 1) * P],
                                                           core.ident[:, :])
                            last.then_inc(sem["kr_done"], 1)
                        if (j := batch(slot, 7)) is not None:
                            pe.wait_ge(sem["kr_ready"], j + 1)
                            if j >= 1:
                                pe.wait_ge(sem["kc_ready"], j)
                            nc.tensor.matmul(bank[2][:, 0:P], kr[:, 0, :], by_head(j % 2, 0), start=True, stop=True)
                            nc.tensor.matmul(bank[2][:, P:2 * P], kr[:, 0, :], upto[:, :], start=True, stop=True)
                            nc.tensor.matmul(bank[2][:, 2 * P:3 * P], kr[:, 0, :], ones[:, :], start=True, stop=False)
                            nc.tensor.matmul(bank[2][:, 2 * P:3 * P], kr[:, 1, :], upto[:, :], start=False,
                                             stop=True).then_inc(sem["kv_done"], 1)
                        if (j := batch(slot, 8)) is not None:
                            pe.wait_ge(sem["kc_ready"], j + 1)
                            if j >= 1:
                                pe.wait_ge(sem["den_added"], j)
                            nc.tensor.matmul(bank[3][:, 0:SEQ], block_[:, :], kc[:, :], start=True, stop=True).then_inc(sem["den_done"], 1)
                            pe.wait_ge(sem["kh_ready"], 4 * (j + 1))
                        if (j := batch(slot, 19)) is not None:
                            pe.wait_ge(sem["ot_ready"], j + 1)
                            for t in range(TPB):
                                last = nc.tensor.matmul(bank[6 + j % 2][:, SEQ + t * P:SEQ + (t + 1) * P], ot[:, j % 2, t * P:(t + 1) * P],
                                                        w["wo"][:, :], start=True, stop=True)
                            last.then_inc(sem["y_done"], 1)
                        if 0 <= (n := slot - 8) < SLOTS * TURN:
                            j, t, g = unit(n)
                            if n >= 2:
                                pe.wait_ge(sem["masked"], n - 1)
                            for i in range(4):
                                last = nc.tensor.matmul(bank[4 + n % 2][:, i * P:(i + 1) * P],
                                                        kh[32 * g:32 * g + 32, j % 2, i, t * P:(t + 1) * P],
                                                        qk[32 * g:32 * g + 32, j % 2, 0, t * P:(t + 1) * P], start=True, stop=True)
                            last.then_inc(sem["scored"], 1)

                @block.vector
                def _(dve):
                    for slot in slots:
                        if 0 <= (n := slot - 9) < SLOTS * TURN:
                            dve.wait_ge(sem["scored"], n + 1)
                            if n >= 2:
                                dve.wait_ge(sem["o_done"], n - 1)
                            nc.vector.tensor_tensor(st[:, n % 2, :, :], bank[4 + n % 2][:, :].rearrange("p (i q) -> p i q", i=4),
                                                    upto[:, None, :].to_broadcast([P, 4, P]), ALU.mult).then_inc(sem["masked"], 1)
                        if (j := batch(slot, 2)) is not None:
                            dve.wait_ge(sem["qk_proj"], j + 1)
                            if j >= 1:
                                dve.wait_ge(sem["qk_ready"], j)
                            if j >= 2:
                                dve.wait_ge(sem["o_done"], SLOTS * (j - 1))
                                dve.wait_ge(sem["kh_ready"], 4 * (j - 1))
                            for n, bias in enumerate((bq, bk)):
                                pre = bank[0][:, n * SEQ:(n + 1) * SEQ]
                                nc.vector.tensor_scalar(low[:, n, :], pre, bias[:, 0:1], 0.0, ALU.add, ALU.min).then_inc(sem["low_ready"], 1)
                            for n, bias in enumerate((bq, bk)):
                                pre = bank[0][:, n * SEQ:(n + 1) * SEQ]
                                nc.vector.tensor_scalar(qk[:, j % 2, n, :], pre, bias[:, 0:1], 0.0, ALU.add, ALU.max).then_inc(sem["high_ready"], 1)
                        if (j := batch(slot, 3)) is not None:
                            dve.wait_ge(sem["v_proj"], j + 1)
                            for t in range(TPB):
                                last = nc.vector.tensor_tensor(
                                    by_head(j % 2, t), bank[1][:, t * P:(t + 1) * P].rearrange("p (h d) -> p h d", d=8),
                                    bv[:, :].rearrange("p (h d) -> p h d", d=8), ALU.add)
                            last.then_inc(sem["v_ready"], 1)
                        if (j := batch(slot, 4)) is not None:
                            dve.wait_ge(sem["exp_ready"], j + 1)
                            dve.wait_ge(sem["high_ready"], 2 * (j + 1))
                            nc.vector.tensor_tensor(qk[:, j % 2, :, :], qk[:, j % 2, :, :], low[:, :, :], ALU.add).then_inc(sem["qk_ready"], 1)
                        if (j := batch(slot, 7)) is not None:
                            dve.wait_ge(sem["kv_done"], j + 1)
                            dve.wait_ge(sem["qk_ready"], j + 1)
                            if j >= 1:
                                dve.wait_ge(sem["den_done"], j)
                            nc.vector.tensor_tensor(state[:, j % 2, :], bank[2][:, 0:P], block_[:, :], ALU.mult).then_inc(sem["state_ready"], 1)
                            nc.vector.tensor_tensor(kc[:, :], bank[2][:, P:3 * P], qk[:, j % 2, 0, :], ALU.mult).then_inc(sem["kc_ready"], 1)
                        if (j := batch(slot, 9)) is not None:
                            dve.wait_ge(sem["den_done"], j + 1)
                            if j >= 2:
                                dve.wait_ge(sem["ot_ready"], j - 1)
                            nc.vector.tensor_scalar(rec[:, j % 2, :], bank[3][:, 0:SEQ], 1e-6, None, ALU.add).then_inc(sem["den_added"], 1)
                            dve.wait_ge(sem["den_added"], j + 1)
                            nc.vector.reciprocal(rec[:, j % 2, :], rec[:, j % 2, :]).then_inc(sem["rec_ready"], 1)
                        if (j := batch(slot, 18)) is not None:
                            dve.wait_ge(sem["o_done"], SLOTS * (j + 1))
                            dve.wait_ge(sem["rec_ready"], j + 1)
                            if j >= 2:
                                dve.wait_ge(sem["y_done"], j - 1)
                            nc.vector.tensor_tensor(ot[:, j % 2, :], bank[6 + j % 2][:, 0:SEQ], rec[:, j % 2, :], ALU.mult).then_inc(sem["ot_ready"], 1)
                        if (j := batch(slot, 20)) is not None:
                            dve.wait_ge(sem["y_done"], j + 1)
                            nc.vector.tensor_tensor(
                                core.s[:, bass.ds((turn * TURN + j) * TPB, TPB), :],
                                bank[6 + j % 2][:, SEQ:2 * SEQ].rearrange("p (t c) -> p t c", t=TPB),
                                bo[:, None, :].to_broadcast([P, TPB, P]), ALU.add).then_inc(sem["stored"], 1)
            zero()


class Softmax:

    NAMES = ("scored", "masked", "bias_ready", "p_ready", "pt_done", "pt_ready", "o_ready", "rec_ready", "on_ready",
             "bank7_full", "bank7_free")
    UNITS = TPB * HEADS // 2

    def __init__(self, core, sb, dh, local, mask_name, scale, stage_turns, qt=None, v=None):
        self.core, self.dh, self.local, self.scale = core, dh, local, scale
        self.parts = TPB * HEADS * dh // 512 if dh == 64 else TPB
        self.part_units = self.UNITS // self.parts
        self.part_cols = TPB * HEADS * dh // self.parts
        self.part_chunks = self.part_cols // P
        self.chunks = HEADS * dh // P
        groups = HEADS // 2 if dh == 64 else 4
        self.qt = qt if qt is not None else sb("qt", [P, 2, groups, SEQ])
        self.kt = sb("kt", [P, 2, groups if dh == 64 else 1, SEQ])
        self.late = 0 if dh == 64 else 1
        if v is not None:
            self.v = v
        elif dh == 64:
            self.v = sb("v", [P, 2, TPB, HEADS * dh])
        else:
            self.v = sb("v", [P, 2, TPB, HEADS * (P + dh)])
        self.wo = sb("wo", [P, self.chunks, P])
        self.mask = sb("mask", [P, TPB, SEQ])
        self.sm = sb("sm", [P, 2, 2, SEQ])
        self.p = sb("p", [P, 2 + self.late, 2, SEQ])
        self.pt = sb("pt", [P, 2, 4, P])
        self.mx, self.nb, self.sums, self.rec = (sb(n, [P, 2, TPB * HEADS]) for n in ("mx", "nb", "sums", "rec"))
        self.on = sb("on", [P, 2, self.part_cols])
        self.ot = sb("ot", [P, 2, self.chunks, P])
        self.factor = self.nfactor = None
        self.mask_src = core.dram[mask_name]
        self.plan = [(16 * k + s, "stage", k, i) for k in range(NB) for i, s in enumerate(stage_turns)]
        for k in range(NB):
            for part in range(self.parts):
                last = 16 * (k + 1) + (part + 1) * self.part_units - 1
                if dh == 64:
                    self.plan.append((last + 6, "part", k, part))
                if (part + 1) % (self.parts // TPB) == 0:
                    self.plan.append((last + 8 - self.late, "y", k, (part + 1) // (self.parts // TPB) - 1))
        self.plan.sort()
        slots = [use[0] for use in self.plan]
        assert len(set(slots)) == len(slots)
        self.number = {use[1:]: n for n, use in enumerate(self.plan)}
        self.at = {use[0]: use[1:] for use in self.plan}
        self.last_slot = slots[-1] + 2
        ends = [16 + g for g in range(NB * self.UNITS) if (g + 1) % self.part_units == 0]
        units = range(16, 16 + NB * self.UNITS)
        after = lambda lag, n=1: [u + lag for u in units for _ in range(n)]
        self.when = {"scored": after(0), "masked": after(1, 2), "bias_ready": after(1), "p_ready": after(1, 2),
                     "pt_done": after(2 + self.late), "pt_ready": after(3 + self.late), "o_ready": after(4 + self.late),
                     "rec_ready": [u + 5 for u in ends] if dh == 64 else after(2),
                     "on_ready": [u + 5 + self.late for u in ends],
                     "bank7_full": slots, "bank7_free": [u + 1 for u in slots]}
        if dh == 8:
            self.when["p_divided"] = after(2, 2)

    def full(self, eng, kind, k, i):
        self.sig.wait(eng, "bank7_full", self.number[kind, k, i] + 1)

    def free(self, eng, kind, k, i):
        self.sig.wait(eng, "bank7_free", self.number[kind, k, i] + 1)

    def take_bank7(self, pe, kind, k, i):
        self.sig.wait(pe, "bank7_free", self.number[kind, k, i])

    def first(self, t):
        return local_first_key(t) if self.local else 0

    def width(self, t):
        return local_width(t) if self.local else (t + 1) * P

    def key_chunks(self, t):
        if t == 0:
            return [(0, P, 0, 0)]
        if self.local:
            return [(WINDOW, P, 1, 0), (0, WINDOW, 0, P - WINDOW)]
        return [(0, P, 0, 0), (P, P, 1, 0)]

    def unit(self, g):
        if not 0 <= g < NB * self.UNITS:
            return None
        u = g % self.UNITS
        return g // self.UNITS, u // (HEADS // 2), u % (HEADS // 2)

    def scores(self, pe, g):
        if not self.unit(g):
            return
        nc, sig, bank = self.core.nc, self.sig, self.core.bank
        k, t, hp = self.unit(g)
        sig.wait(pe, "masked", 2 * g)
        w, k0 = self.width(t), self.first(t)
        for i in range(2):
            h = 2 * hp + i
            if self.dh == 64:
                rows, group, key_group = slice(64 * i, 64 * i + 64), hp, hp
            else:
                rows, group, key_group = slice(32 * (h // 4), 32 * (h // 4) + 32), h % 4, 0
            last = nc.tensor.matmul(bank[i][:, 0:w], self.qt[rows, k % 2, group, t * P:(t + 1) * P],
                                    self.kt[rows, k % 2, key_group, k0:k0 + w], start=True, stop=True)
        sig.done(last, "scored")

    def turn(self, pe, g):
        if not self.unit(g):
            return
        nc, core, sig = self.core.nc, self.core, self.sig
        k, t, hp = self.unit(g)
        sig.wait(pe, "p_divided" if self.late else "p_ready", 2 * (g + 1))
        sig.wait(pe, "pt_ready", g)
        for c, (c0, n, _, _) in enumerate(self.key_chunks(t)):
            for i in range(2):
                last = nc.tensor.transpose(core.bank[2][0:n, (2 * c + i) * P:(2 * c + i) * P + n],
                                           self.p[0:n, g % self.p.shape[1], i, c0:c0 + n], core.ident[0:n, 0:n])
        sig.done(last, "pt_done")

    def values(self, pe, g):
        if not self.unit(g):
            return
        nc, sig, bank = self.core.nc, self.sig, self.core.bank
        k, t, hp = self.unit(g)
        sig.wait(pe, "pt_ready", g + 1)
        part = g // self.part_units
        if g % self.part_units == 0:
            sig.wait(pe, "on_ready", part - 1)
        kc = self.key_chunks(t)
        for i in range(2):
            h = 2 * hp + i
            col = (h * self.dh) % self.part_cols
            for c, (_, n, vt, p0) in enumerate(kc):
                last = nc.tensor.matmul(bank[3 + part % 2][:, col:col + self.dh], self.pt[p0:p0 + n, g % 2, 2 * c + i, :],
                                        self.v[p0:p0 + n, k % 2, vt, h * self.dh:(h + 1) * self.dh],
                                        start=(c == 0), stop=(c == len(kc) - 1))
        sig.done(last, "o_ready")

    def values_to_columns(self, pe, g):
        if not self.unit(g):
            return
        nc, sig, bank = self.core.nc, self.sig, self.core.bank
        k, t, hp = self.unit(g)
        part = g // self.part_units
        sig.wait(pe, "pt_ready", g + 1)
        if hp == 0:
            sig.wait(pe, "on_ready", part - 1)
        for i in range(2):
            h = 2 * hp + i
            for c in range(t + 1):
                last = nc.tensor.matmul(bank[3 + part % 2][:, 0:P], self.v[:, k % 2, c, h * P:(h + 1) * P],
                                        self.pt[:, g % 2, 2 * c + i, :], start=(h == 0 and c == 0), stop=(h == HEADS - 1 and c == t))
        sig.done(last, "o_ready")

    def turn_part(self, pe, k, part):
        nc, core, sig = self.core.nc, self.core, self.sig
        self.take_bank7(pe, "part", k, part)
        n = k * self.parts + part
        sig.wait(pe, "on_ready", n + 1)
        for c in range(self.part_chunks):
            last = nc.tensor.transpose(core.bank[7][:, c * P:(c + 1) * P], self.on[:, n % 2, c * P:(c + 1) * P],
                                       core.ident[:, :])
        sig.done(last, "bank7_full")

    def project_out(self, pe, k, t):
        nc, core, sig = self.core.nc, self.core, self.sig
        self.take_bank7(pe, "y", k, t)
        if self.late:
            sig.wait(pe, "on_ready", k * TPB + t + 1)
        else:
            for part in range(t * self.parts // TPB, (t + 1) * self.parts // TPB):
                self.free(pe, "part", k, part)
        for c in range(self.chunks):
            last = nc.tensor.matmul(core.bank[7][:, 0:P], self.ot[:, t, c, :], self.wo[:, c, :],
                                    start=(c == 0), stop=(c == self.chunks - 1))
        sig.done(last, "bank7_full")

    def mask_and_max(self, dve, g):
        if not self.unit(g):
            return
        nc, sig, bank = self.core.nc, self.sig, self.core.bank
        k, t, hp = self.unit(g)
        w = self.width(t)
        sig.wait(dve, "scored", g + 1)
        sig.wait(dve, "p_ready", 2 * (g - 1))
        for i in range(2):
            col = t * HEADS + 2 * hp + i
            ins = nc.vector.tensor_tensor_reduce(self.sm[:, g % 2, i, 0:w], bank[i][:, 0:w], self.mask[:, t, 0:w], 1.0,
                                                 LOWEST, ALU.add, ALU.max, self.mx[:, k % 2, col:col + 1])
            sig.done(ins, "masked")
        sig.wait(dve, "masked", 2 * (g + 1))
        c = slice(t * HEADS + 2 * hp, t * HEADS + 2 * hp + 2)
        if self.nfactor is not None:
            ins = nc.vector.tensor_tensor(self.nb[:, k % 2, c], self.mx[:, k % 2, c], self.nfactor[:, k % 2, c], ALU.mult)
        else:
            ins = nc.vector.tensor_scalar(self.nb[:, k % 2, c], self.mx[:, k % 2, c], -self.scale, None, ALU.mult)
        sig.done(ins, "bias_ready")

    def normalise(self, dve, g):
        if not self.unit(g) or (g + 1) % self.part_units:
            return
        nc, sig, bank = self.core.nc, self.sig, self.core.bank
        k, n = g // self.UNITS, g // self.part_units
        part = n % self.parts
        if n >= 2:
            self.full(dve, "part", (n - 2) // self.parts, (n - 2) % self.parts)
        nh = self.part_cols // self.dh
        s = slice(part * nh, (part + 1) * nh)
        sig.wait(dve, "o_ready", g + 1)
        sig.done(nc.vector.reciprocal(self.rec[:, k % 2, s], self.sums[:, k % 2, s]), "rec_ready")
        sig.wait(dve, "rec_ready", n + 1)
        ins = nc.vector.tensor_tensor(
            self.on[:, n % 2, :].rearrange("p (h d) -> p h d", d=self.dh),
            bank[3 + n % 2][:, 0:self.part_cols].rearrange("p (h d) -> p h d", d=self.dh),
            self.rec[:, k % 2, s].rearrange("p (h a) -> p h a", a=1).to_broadcast([P, nh, self.dh]), ALU.mult)
        sig.done(ins, "on_ready")

    def divide(self, dve, g):
        if not self.unit(g):
            return
        nc, sig = self.core.nc, self.sig
        k, t, hp = self.unit(g)
        c = t * HEADS + 2 * hp
        sig.wait(dve, "p_ready", 2 * (g + 1))
        sig.done(nc.vector.reciprocal(self.rec[:, k % 2, c:c + 2], self.sums[:, k % 2, c:c + 2]), "rec_ready")
        sig.wait(dve, "rec_ready", g + 1)
        for i in range(2):
            p = self.p[:, g % 3, i, 0:self.width(t)]
            sig.done(nc.vector.tensor_scalar(p, p, self.rec[:, k % 2, c + i:c + i + 1], None, ALU.mult), "p_divided")

    def copy_columns(self, dve, g):
        if not self.unit(g) or (g + 1) % self.part_units:
            return
        nc, sig = self.core.nc, self.sig
        k, t = g // self.UNITS, g // self.part_units % TPB
        sig.wait(dve, "o_ready", g + 1)
        if k >= 1:
            self.full(dve, "y", k - 1, t)
        sig.done(nc.vector.tensor_copy(self.ot[:, t, 0, :], self.core.bank[3 + g // self.part_units % 2][:, 0:P]), "on_ready")

    def copy_part(self, eng, copy, k, part):
        t = part // (self.parts // TPB)
        if k >= 1:
            self.full(eng, "y", k - 1, t)
        self.full(eng, "part", k, part)
        c0 = (part * self.part_chunks) % self.chunks
        n = self.part_chunks
        self.sig.done(copy(self.ot[:, t, c0:c0 + n, :], self.core.bank[7][:, 0:n * P].rearrange("p (c q) -> p c q", c=n)),
                      "bank7_free")

    def exps(self, act, g):
        if not self.unit(g):
            return
        nc, sig = self.core.nc, self.sig
        k, t, hp = self.unit(g)
        w = self.width(t)
        sig.wait(act, "bias_ready", g + 1)
        n = self.p.shape[1]
        sig.wait(act, "pt_done", g + 1 - n)
        for i in range(2):
            col = t * HEADS + 2 * hp + i
            scale = self.factor[:, k % 2, col:col + 1] if self.factor is not None else self.scale
            ins = nc.scalar.activation(self.p[:, g % n, i, 0:w], self.sm[:, g % 2, i, 0:w], ACT.Exp,
                                       bias=self.nb[:, k % 2, col:col + 1], scale=scale,
                                       accum_out=self.sums[:, k % 2, col:col + 1])
            sig.done(ins, "p_ready")

    def copy_turned(self, act, g):
        if not self.unit(g):
            return
        nc, sig, bank = self.core.nc, self.sig, self.core.bank
        k, t, hp = self.unit(g)
        sig.wait(act, "pt_done", g + 1)
        sig.wait(act, "o_ready", g - 1)
        kc = self.key_chunks(t)
        if all(n == P for _, n, _, _ in kc):
            m = 2 * len(kc)
            last = nc.scalar.copy(self.pt[:, g % 2, 0:m, :], bank[2][:, 0:m * P].rearrange("p (m q) -> p m q", m=m))
        else:
            for c, (_, n, _, p0) in enumerate(kc):
                last = nc.scalar.copy(self.pt[p0:p0 + n, g % 2, 2 * c:2 * c + 2, 0:n],
                                      bank[2][0:n, 2 * c * P:(2 * c + 2) * P].rearrange("p (m q) -> p m q", m=2)[:, :, 0:n])
        sig.done(last, "pt_ready")


def local_attention_stage(core, l):
    nc, dram, bank = core.nc, core.dram, core.bank
    NCH = 3 * INNER // 512
    CH = TPB * NCH
    CHUNKS = [(8 * t + s, t, c) for t in range(TPB) for s, c in ((2, 0), (3, 4), (4, 1), (6, 2), (7, 5), (8, 3))]
    TURNS = (0, 8, 10, 12, 14, 18, 19, 20, 22)
    with ExitStack() as ctx:
        def sb(name, shape, dt=F32):
            return ctx.enter_context(nc.sbuf_tensor("loc_" + name, shape, dt))

        att = Softmax(core, sb, DH, True, "mask_local", None, TURNS,
                      qt=core.xn[:, :, :].rearrange("p t c -> p (t c)").rearrange("p (k g q) -> p k g q", k=2, g=HEADS // 2),
                      v=core.xnt[:, :].rearrange("p (k t c) -> p k t c", k=2, t=TPB))
        proj = [16 * k + slot for k in range(NB) for slot, _, _ in CHUNKS]
        chunk = lambda i: (i // CH,) + CHUNKS[i % CH][1:]
        qk = [i for i in range(NB * CH) if chunk(i)[2] < 4]
        qk_number = {i: n for n, i in enumerate(qk)}
        number_at = {slot: i for i, slot in enumerate(proj)}
        lasts = [proj[i] for i in qk if chunk(i)[2] == 3]
        yb_slot = [max(0, 16 * k - 3) for k in range(NB)]
        when = dict(att.when)
        when.update({
            "yb_ready": yb_slot,
            "xb_ready": [16 * k + 1 for k in range(NB) for _ in range(2)],
            "proj_done": proj,
            "squared": [proj[i] + 1 for i in qk],
            "turned": [proj[i] + 1 for i in qk],
            "summed": [proj[i] + 1 for i in qk],
            "rk_ready": [s + 2 for s in lasts for _ in range(2)],
            "v_act": [proj[i] + 1 for i in range(NB * CH) if chunk(i)[2] == 4],
            "v_dve": [proj[i] + 1 for i in range(NB * CH) if chunk(i)[2] == 5],
            "added": [proj[i] + 2 for i in qk],
            "final": [s + 3 for s in lasts for _ in range(2)],
            "stored": [use[0] + 1 for use in att.plan if use[1] == "y"],
        })
        names = tuple(when) + ("dve_step",)
        sems, zero = ctx.enter_context(signals(nc, ["loc_" + n for n in names]))
        sem = dict(zip(names, sems))
        sig = att.sig = Signals(sem, when)
        wqkv = sb("wqkv", [P, 3 * INNER])
        rope, qks = sb("rope", [P, TPB, 4, DH]), sb("qks", [P, 2, DH])
        yb, xb = sb("yb", [P, 2, TPB, P]), sb("xb", [P, 2, SEQ])
        a, b_ = sb("a", [P, TPB, 4, 512]), sb("b", [P, 2, 512])
        sq = sb("sq", [P, 2, 512])
        n2, rn, tmp = sb("n2", [P, TPB, 32]), sb("rn", [P, TPB, 32]), sb("tmp", [P, 32])
        att.factor, att.nfactor = sb("f", [P, 2, TPB * HEADS]), sb("nf", [P, 2, TPB * HEADS])
        load(core, [
            (wqkv[:, :], dram["L0_ffn_Wqkv"][bass.ds(l, 1), :, :].rearrange("a p n -> p (a n)")),
            (att.wo[:, :, :], dram["L0_ffn_Wo"][bass.ds(l, 1), :, :].rearrange("a (c p) n -> p (a c) n", p=P)),
            (att.mask[:, :, :], att.mask_src), (rope[:, :, :, :], dram["rope_local"]),
            (qks[:, 0, :], dram["L0_ffn_q_scale"][bass.ds(l, 1), :].to_broadcast([P, DH])),
            (qks[:, 1, :], dram["L0_ffn_k_scale"][bass.ds(l, 1), :].to_broadcast([P, DH]))])
        with nc.Block() as block:
            @block.vector
            def _(dve):
                after = chain(dve, sem["dve_step"])
                for n in range(2):
                    wide = qks[:, n, :].rearrange("p (a d) -> p a d", a=1).to_broadcast([P, TPB, DH])
                    after(nc.vector.tensor_tensor(rope[:, :, 2 * n, :], rope[:, :, 2 * n, :], wide, ALU.mult))
                    for half in range(2):
                        d, s = half * 32, 32 - half * 32
                        wide = qks[:, n, s:s + 32].rearrange("p (a d) -> p a d", a=1).to_broadcast([P, TPB, 32])
                        after(nc.vector.tensor_tensor(rope[:, :, 2 * n + 1, d:d + 32], rope[:, :, 2 * n + 1, d:d + 32],
                                                      wide, ALU.mult))
                after(nc.vector.memset(xb[64:128, :, 0:1], 0.0))
                after(nc.vector.memset(att.pt[:, :, 2:4, :], 0.0))
        zero()

        def left_bank(pe, i):
            if i < 0:
                return
            k, t, c = chunk(i)
            if c < 4:
                sig.wait(pe, "turned", qk_number[i] + 1)
            else:
                sig.wait(pe, "v_act" if c == 4 else "v_dve", k * TPB + t + 1)

        def copy_heads(copy, k, t, c):
            dst = att.qt if c < 2 else att.kt
            sig.done(copy(dst[:, k % 2, (c % 2) * 4:(c % 2) * 4 + 4, t * P:(t + 1) * P],
                          bank[7][:, :].rearrange("p (j q) -> p j q", j=4)), "bank7_free")

        def emit(block, slots, shift):
            @block.gpsimd
            def _(pool):
                for slot in slots:
                    i = number_at.get(slot - 2)
                    if i is not None and chunk(i)[2] < 4:
                        (k, t, c), n = chunk(i), qk_number[i]
                        sig.wait(pool, "turned", n + 1)
                        sig.done(nc.gpsimd.tensor_tensor(a[:, t, c, :], a[:, t, c, :], b_[:, n % 2, :], ALU.add), "added")
                    i = number_at.get(slot - 3)
                    if i is not None and chunk(i)[2] == 3:
                        (k, t, _), n = chunk(i), qk_number[i]
                        sig.wait(pool, "added", n + 1)
                        sig.wait(pool, "rk_ready", (k * TPB + t) * 2 + 1)
                        for c in (2, 3):
                            k0 = 16 + (c - 2) * 8
                            ins = nc.gpsimd.tensor_tensor(
                                a[:, t, c, :].rearrange("p (h d) -> p h d", d=DH),
                                a[:, t, c, :].rearrange("p (h d) -> p h d", d=DH),
                                rn[:, t, k0:k0 + 8].rearrange("p (h a) -> p h a", a=1).to_broadcast([P, 8, DH]), ALU.mult)
                            sig.done(ins, "final")
                    if slot in yb_slot:
                        k = yb_slot.index(slot)
                        if k >= 2:
                            att.full(pool, "stage", k - 2, 0)
                        sig.done(nc.gpsimd.tensor_copy(yb[:, k % 2, :, :], core.y[:, bass.ds((shift + k) * TPB, TPB), :]),
                                 "yb_ready")

            @block.tensor
            def _(pe):
                for slot in slots:
                    i = number_at.get(slot)
                    if i is not None:
                        k, t, c = chunk(i)
                        if i % CH == 0:
                            sig.wait(pe, "xb_ready", 2 * (k + 1))
                        left_bank(pe, i - 2)
                        ins = nc.tensor.matmul(bank[5 + i % 2][:, :], xb[:, k % 2, t * P:(t + 1) * P], wqkv[:, c * 512:(c + 1) * 512],
                                               start=True, stop=True)
                        sig.done(ins, "proj_done")
                    att.values(pe, slot - 20)
                    if slot in att.at:
                        kind, k, j = att.at[slot]
                        if kind == "part":
                            att.turn_part(pe, k, j)
                        elif kind == "y":
                            att.project_out(pe, k, j)
                        elif j == 0:
                            att.take_bank7(pe, kind, k, j)
                            sig.wait(pe, "yb_ready", k + 1)
                            for t in range(TPB):
                                last = nc.tensor.transpose(bank[7][:, t * P:(t + 1) * P], yb[:, k % 2, t, :], core.ident[:, :])
                            sig.done(last, "bank7_full")
                        else:
                            t, c = (j - 1) // 4, (j - 1) % 4
                            att.take_bank7(pe, kind, k, j)
                            if c < 2:
                                sig.wait(pe, "added", (k * TPB + t) * 4 + c + 1)
                            else:
                                sig.wait(pe, "final", (k * TPB + t) * 2 + c - 1)
                            for m in range(4):
                                last = nc.tensor.transpose(bank[7][:, m * P:(m + 1) * P], a[:, t, c, m * P:(m + 1) * P],
                                                           core.ident[:, :])
                            sig.done(last, "bank7_full")
                    att.turn(pe, slot - 18)
                    att.scores(pe, slot - 16)

            @block.scalar
            def _(act):
                for slot in slots:
                    i = number_at.get(slot - 1)
                    if i is not None and chunk(i)[2] < 4:
                        n = qk_number[i]
                        sig.wait(act, "proj_done", i + 1)
                        sig.wait(act, "summed", n - 1)
                        sig.done(nc.scalar.activation(sq[:, n % 2, :], bank[5 + i % 2][:, :], ACT.Square), "squared")
                    elif i is not None and chunk(i)[2] == 4:
                        k, t, _ = chunk(i)
                        sig.wait(act, "proj_done", i + 1)
                        sig.done(nc.scalar.copy(att.v[:, k % 2, t, 0:512], bank[5 + i % 2][:, :]), "v_act")
                    kind, k, j = att.at.get(slot - 1, (None, 0, 0))
                    if kind == "stage" and j == 0:
                        att.full(act, kind, k, j)
                        sig.wait(act, "proj_done", CH * (k - 1))
                        sig.done(nc.scalar.copy(xb[0:64, k % 2, :], bank[7][0:64, 0:SEQ]), "xb_ready")
                        sig.done(nc.scalar.copy(xb[64:128, k % 2, 1:SEQ], bank[7][64:128, 0:SEQ - 1]), "xb_ready")
                        sig.wait(act, "xb_ready", 2 * (k + 1))
                        sig.done(nc.scalar.copy(spare[0:1, 0:1], core.ident[0:1, 0:1]), "bank7_free")
                    elif kind == "stage":
                        att.full(act, kind, k, j)
                        copy_heads(nc.scalar.copy, k, (j - 1) // 4, (j - 1) % 4)
                    att.copy_turned(act, slot - 19)
                    att.exps(act, slot - 17)

            @block.vector
            def _(dve):
                after = chain(dve, sem["dve_step"])
                for slot in slots:
                    att.mask_and_max(dve, slot - 17)
                    kind, k, j = att.at.get(slot - 1, (None, 0, 0))
                    if kind == "part":
                        att.copy_part(dve, nc.vector.tensor_copy, k, j)
                    elif kind == "y":
                        att.full(dve, kind, k, j)
                        row = core.y[:, bass.ds((shift + k) * TPB + j, 1), :]
                        sig.done(nc.vector.tensor_tensor(row, bank[7][:, 0:P].rearrange("p (a c) -> p a c", a=1), row, ALU.add),
                                 "stored")
                        sig.wait(dve, "stored", k * TPB + j + 1)
                        sig.done(nc.vector.tensor_copy(spare[0:1, 1:2], core.ident[0:1, 0:1]), "bank7_free")
                    i = number_at.get(slot - 1)
                    if i is not None:
                        k, t, c = chunk(i)
                        src_bank = bank[5 + i % 2]
                        if c < 4:
                            n, which = qk_number[i], c // 2
                            sig.wait(dve, "squared", n + 1)
                            sig.wait(dve, "added", n - 1)
                            if k >= 1:
                                att.full(dve, "stage", k - 1, 1 + t * 4 + c)
                            src = src_bank[:, :].rearrange("p (h d) -> p h d", d=DH)
                            cos = rope[:, t, 2 * which, :].rearrange("p (a d) -> p a d", a=1).to_broadcast([P, 8, DH])
                            nc.vector.tensor_tensor(a[:, t, c, :].rearrange("p (h d) -> p h d", d=DH), src, cos, ALU.mult)
                            halves = src_bank[:, :].rearrange("p (h s d) -> p h s d", s=2, d=32)[:, :, ::-1, :]
                            sin = rope[:, t, 2 * which + 1, :].rearrange("p (a s d) -> p a s d", a=1, s=2).to_broadcast([P, 8, 2, 32])
                            ins = nc.vector.tensor_tensor(b_[:, n % 2, :].rearrange("p (h s d) -> p h s d", s=2, d=32), halves,
                                                          sin, ALU.mult)
                            sig.done(ins, "turned")
                            ins = nc.vector.tensor_reduce(n2[:, t, c * 8:(c + 1) * 8],
                                                          sq[:, n % 2, :].rearrange("p (h d) -> p h d", d=DH), AX.X, ALU.add)
                            sig.done(ins, "summed")
                        elif c == 5:
                            sig.wait(dve, "proj_done", i + 1)
                            sig.done(nc.vector.tensor_copy(att.v[:, k % 2, t, 512:1024], src_bank[:, :]), "v_dve")
                    i = number_at.get(slot - 2)
                    if i is not None and chunk(i)[2] == 3:
                        k, t, _ = chunk(i)
                        tile = k * TPB + t
                        sig.wait(dve, "summed", 4 * (tile + 1))
                        sig.wait(dve, "final", 2 * (tile - 1))
                        after(nc.vector.tensor_scalar(n2[:, t, :], n2[:, t, :], 1e-24, None, ALU.max))
                        rsqrt(nc, after, rn[:, t, :], n2[:, t, :], tmp[:, :])
                        for f, scale in ((att.factor, QK_SCALE), (att.nfactor, -QK_SCALE)):
                            ins = nc.vector.tensor_scalar(f[:, k % 2, t * HEADS:(t + 1) * HEADS], rn[:, t, 0:16], scale, None,
                                                          ALU.mult)
                            sig.done(ins, "rk_ready")
                        sig.wait(dve, "rk_ready", 2 * (tile + 1))
                    att.normalise(dve, slot - 21)

        spare = sb("spare", [1, 2])
        run_windows(nc, sig, zero, emit, att.last_slot)


def glu_stage(core, l):
    nc, dram, bank = core.nc, core.dram, core.bank
    rows, cols, G = core.xn, core.xnt, 4
    NGRP, GB = NT // G, G // TPB
    CH, TURN = len(HID_CHUNKS), 8
    with ExitStack() as ctx:
        def sb(name, shape, dt=F32):
            return ctx.enter_context(nc.sbuf_tensor("glu_" + name, shape, dt))

        names = ("zeroed", "cols_done", "shifted", "rows_done", "rows_ready", "normalised", "turned", "biased", "xn_ready",
                 "hid_done", "gelu_ready", "h_ready", "y_done", "stored", "dve_step")
        sems, zero = ctx.enter_context(signals(nc, ["glu_" + n for n in names]))
        sem = dict(zip(names, sems))
        w1, w2 = sb("w1", [P, 2 * DIM_INNER]), sb("w2", [P, CH, P])
        b1, b2, gain, shift = sb("b1", [P, 2, CH]), sb("b2", [P, P]), sb("gain", [P, 1]), sb("shift", [P, 1])
        xs = sb("xs", [P, 2, GB, SEQ])
        gel, h = sb("gel", [P, CH, SEQ]), sb("h", [P, 2, CH, SEQ])
        stats, mv, rstd, tmp = sb("stats", [P, NT, 6]), sb("mv", [P, NT, 2]), sb("rstd", [P, NT]), sb("tmp", [P, NT])
        row = lambda name: dram["L0_ffn_" + name][bass.ds(l, 1), :]
        load(core, [(w1[:, :], dram["L0_ffn_W1"][bass.ds(l, 1), :, :].rearrange("a p n -> p (a n)")),
                    (b2[:, :], row("b2").to_broadcast([P, P])),
                    (gain[:, :], row("ln_g").rearrange("a p -> p a")), (shift[:, :], row("ln_b").rearrange("a p -> p a"))] +
             [(w2[0:n, c, :], dram["L0_ffn_W2"][bass.ds(l, 1), c0:c0 + n, :].rearrange("a p n -> p (a n)"))
              for c, (c0, n) in enumerate(HID_CHUNKS)] +
             [(b1[0:n, g, c:c + 1], dram["L0_ffn_b1"][bass.ds(l, 1), g * DIM_INNER + c0:g * DIM_INNER + c0 + n].rearrange("a p -> p a"))
              for c, (c0, n) in enumerate(HID_CHUNKS) for g in range(2)])
        tiles = lambda ap: ap.rearrange("p (t c) -> p t c", c=P)
        with nc.Block() as block:
            @block.tensor
            def _(pe):
                for g in range(NGRP + 1):
                    if g < NGRP:
                        if g >= 2:
                            pe.wait_ge(sem["shifted"], 2 * (g - 1))
                        for i in range(G):
                            last = nc.tensor.transpose(bank[g % 2][:, i * P:(i + 1) * P], core.y[:, g * G + i, :], core.ident[:, :])
                        last.then_inc(sem["cols_done"], 1)
                    if g >= 1:
                        pe.wait_ge(sem["shifted"], 2 * g)
                        if g >= 3:
                            pe.wait_ge(sem["rows_ready"], g - 2)
                        for i in range(G):
                            b, t = i // TPB, i % TPB
                            last = nc.tensor.transpose(bank[2 + (g - 1) % 2][:, i * P:(i + 1) * P],
                                                       xs[:, (g - 1) % 2, b, t * P:(t + 1) * P], core.ident[:, :])
                        last.then_inc(sem["rows_done"], 1)
                for g in range(NGRP):
                    pe.wait_ge(sem["normalised"], G * (g + 1))
                    if g >= 2:
                        pe.wait_ge(sem["xn_ready"], g - 1)
                    for i in range(G):
                        last = nc.tensor.transpose(bank[4 + g % 2][:, i * P:(i + 1) * P], rows[:, g * G + i, :], core.ident[:, :])
                    last.then_inc(sem["turned"], 1)

            @block.scalar
            def _(act):
                act.wait_ge(sem["zeroed"], 1)
                for g in range(NGRP + 1):
                    if g < NGRP:
                        src = bank[g % 2][:, :].rearrange("p (b q) -> p b q", b=GB)
                        act.wait_ge(sem["cols_done"], g + 1)
                        if g >= 2:
                            act.wait_ge(sem["rows_done"], g - 1)
                        nc.scalar.copy(xs[0:64, g % 2, :, :], src[0:64, :, :]).then_inc(sem["shifted"], 1)
                        nc.scalar.copy(xs[64:128, g % 2, :, 1:SEQ], src[64:128, :, 0:SEQ - 1]).then_inc(sem["shifted"], 1)
                    if g >= 1:
                        act.wait_ge(sem["rows_done"], g)
                        nc.scalar.copy(rows[:, (g - 1) * G:g * G, :], tiles(bank[2 + (g - 1) % 2][:, :])).then_inc(sem["rows_ready"], 1)
                for g in range(NGRP):
                    act.wait_ge(sem["turned"], g + 1)
                    nc.scalar.activation(cols[:, g * G * P:(g + 1) * G * P], bank[4 + g % 2][:, :], ACT.Identity,
                                         bias=shift[:, 0:1], scale=gain[:, 0:1]).then_inc(sem["xn_ready"], 1)

            @block.vector
            def _(dve):
                after = chain(dve, sem["dve_step"])
                nc.vector.memset(xs[64:128, :, :, 0:1], 0.0).then_inc(sem["zeroed"], 1)
                for g in range(NGRP):
                    dve.wait_ge(sem["rows_ready"], g + 1)
                    for i in range(G):
                        last = nc.vector.bn_stats(stats[:, g * G + i, :], rows[:, g * G + i, :])
                after(last)
                for ins in normalise_by(nc, after, [rows[:, j, :] for j in range(NT)], [rows[:, j, :] for j in range(NT)],
                                        stats, mv, rstd, tmp, 1e-5):
                    ins.then_inc(sem["normalised"], 1)

            @block.gpsimd
            def _(pool):
                for g in range(NGRP):
                    pool.wait_ge(sem["cols_done"], g + 1)
                    y = core.y[:, g * G:(g + 1) * G, :]
                    nc.gpsimd.tensor_tensor(y, y, b2[:, :].rearrange("p (a c) -> p a c", a=1).to_broadcast([P, G, P]),
                                            ALU.add).then_inc(sem["biased"], 1)
        zero()
        with nc.Fori(0, NB // TURN) as turn:
            with nc.Block() as block:
                @block.tensor
                def _(pe):
                    for j in range(TURN + 1):
                        if j < TURN:
                            for c, (c0, n) in enumerate(HID_CHUNKS):
                                m = CH * j + c
                                if m >= 6:
                                    pe.wait_ge(sem["h_ready"], m - 5)
                                for g in (1, 0):
                                    last = nc.tensor.matmul(bank[m % 6][0:n, g * SEQ:(g + 1) * SEQ],
                                                            w1[:, g * DIM_INNER + c0:g * DIM_INNER + c0 + n],
                                                            cols[:, bass.ds((turn * TURN + j) * SEQ, SEQ)], start=True, stop=True)
                                last.then_inc(sem["hid_done"], 1)
                        if j >= 1:
                            i = j - 1
                            pe.wait_ge(sem["h_ready"], CH * (i + 1))
                            if i >= 2:
                                pe.wait_ge(sem["stored"], i - 1)
                            for t in range(TPB):
                                for c, (c0, n) in enumerate(HID_CHUNKS):
                                    last = nc.tensor.matmul(bank[6 + i % 2][:, t * P:(t + 1) * P], h[0:n, i % 2, c, t * P:(t + 1) * P],
                                                            w2[0:n, c, :], start=(c == 0), stop=(c == CH - 1))
                            last.then_inc(sem["y_done"], 1)

                @block.scalar
                def _(act):
                    for m in range(CH * TURN):
                        c, n = m % CH, HID_CHUNKS[m % CH][1]
                        act.wait_ge(sem["hid_done"], m + 1)
                        if m >= CH:
                            act.wait_ge(sem["h_ready"], m - CH + 1)
                        nc.scalar.activation(gel[0:n, c, :], bank[m % 6][0:n, SEQ:2 * SEQ], ACT.Gelu,
                                             bias=b1[0:n, 1, c:c + 1]).then_inc(sem["gelu_ready"], 1)

                @block.vector
                def _(dve):
                    for j in range(TURN + 1):
                        if j < TURN:
                            if j >= 2:
                                dve.wait_ge(sem["y_done"], j - 1)
                            for c, (c0, n) in enumerate(HID_CHUNKS):
                                m = CH * j + c
                                dve.wait_ge(sem["gelu_ready"], m + 1)
                                nc.vector.scalar_tensor_tensor(out=h[0:n, j % 2, c, :], in0=bank[m % 6][0:n, 0:SEQ],
                                                               scalar=b1[0:n, 0, c:c + 1], in1=gel[0:n, c, :],
                                                               op0=ALU.add, op1=ALU.mult).then_inc(sem["h_ready"], 1)
                        if j >= 1:
                            i = j - 1
                            dve.wait_ge(sem["y_done"], i + 1)
                            y = core.y[:, bass.ds((turn * TURN + i) * TPB, TPB), :]
                            nc.vector.tensor_tensor(y, tiles(bank[6 + i % 2][:, 0:SEQ]), y, ALU.add).then_inc(sem["stored"], 1)
            zero()


def local_transformer_stage(core):
    nc = core.nc
    with signals(nc, ["y_started"]) as ((started,), zero):
        with nc.Block() as block:
            @block.vector
            def _(dve):
                nc.vector.tensor_copy(core.y[:, :, :], core.xn[:, :, :]).then_inc(started, 1)
        zero()
    with nc.Fori(0, LAYERS_RUN) as l:
        local_attention_stage(core, l)
        glu_stage(core, l)


def gelu_linear_attention_stage(core):
    nc, dram, bank = core.nc, core.dram, core.bank
    with ExitStack() as ctx:
        def sb(name, shape, dt=F32):
            return ctx.enter_context(nc.sbuf_tensor("l1a_" + name, shape, dt))

        names = ("turned", "w_ready", "x_ready", "qk_proj", "v_proj", "gelu_ready", "qk_ready", "rot_done", "qkr_ready",
                 "v_ready", "krt_done", "krt_ready", "kv_done", "kv_ready", "mean_ready", "o_done", "stored", "dve_step")
        sems, zero = ctx.enter_context(signals(nc, ["l1a_" + n for n in names]))
        sem = dict(zip(names, sems))
        w, wt = sb("w", [P, 3, P]), sb("wt", [P, 3, P])
        bq, bk, bv = sb("bq", [P, 1]), sb("bk", [P, 1]), sb("bv", [P, P])
        gamma, beta = sb("gamma", [P, P]), sb("beta", [P, P])
        rope, swap, block_ = sb("rope", [P, 2, SEQ]), sb("swap", [P, P]), sb("block", [P, P])
        xb, qk, part, qkr = sb("xb", [P, SEQ]), sb("qk", [P, 2, SEQ]), sb("part", [P, 2, SEQ]), sb("qkr", [P, 2, SEQ])
        v, krt = sb("v", [P, TPB, P]), sb("krt", [P, TPB, P])
        mean, kmean, kv = sb("mean", [P, 1]), sb("kmean", [P, P]), sb("kv", [P, P])
        rec, res = sb("rec", [P, TPB, P]), sb("res", [P, TPB, P])
        load(core, [(w[:, i, :], dram["L1_attn_W" + n]) for i, n in enumerate("qkv")] +
             [(bq[:, :], column(dram["L1_attn_bq"])), (bk[:, :], column(dram["L1_attn_bk"])),
              (bv[:, :], spread(dram["L1_attn_bv"])), (gamma[:, :], spread(dram["L1_attn_gamma"])),
              (beta[:, :], spread(dram["L1_attn_beta"])), (rope[:, :, :], dram["rope_l1"]),
              (swap[:, :], dram["swap"]), (block_[:, :], dram["head_block"])])
        with nc.Block() as block:
            @block.tensor
            def _(pe):
                for i in range(3):
                    last = nc.tensor.transpose(bank[0][:, i * P:(i + 1) * P], w[:, i, :], core.ident[:, :])
                last.then_inc(sem["turned"], 1)

            @block.vector
            def _(dve):
                dve.wait_ge(sem["turned"], 1)
                nc.vector.tensor_copy(wt[:, :, :].rearrange("p a b -> p (a b)"), bank[0][:, 0:3 * P]).then_inc(sem["w_ready"], 1)
        zero()
        with nc.Fori(0, NB) as b:
            with nc.Block() as block:
                @block.scalar
                def _(act):
                    nc.scalar.copy(xb[:, :], core.xnt[:, bass.ds(b * SEQ, SEQ)]).then_inc(sem["x_ready"], 1)
                    act.wait_ge(sem["qk_proj"], 1)
                    for n, bias in enumerate((bq, bk)):
                        nc.scalar.activation(part[:, n, :], bank[0][:, n * SEQ:(n + 1) * SEQ], ACT.Gelu,
                                             bias=bias[:, 0:1]).then_inc(sem["gelu_ready"], 1)
                    act.wait_ge(sem["krt_done"], 1)
                    nc.scalar.copy(krt[:, :, :], bank[3][:, 0:SEQ].rearrange("p (t c) -> p t c", t=TPB)).then_inc(sem["krt_ready"], 1)

                @block.tensor
                def _(pe):
                    pe.wait_ge(sem["x_ready"], 1)
                    for n in range(2):
                        last = nc.tensor.matmul(bank[0][:, n * SEQ:(n + 1) * SEQ], wt[:, n, :], xb[:, :], start=True, stop=True)
                    last.then_inc(sem["qk_proj"], 1)
                    for t in range(TPB):
                        last = nc.tensor.matmul(bank[2][:, t * P:(t + 1) * P], xb[:, t * P:(t + 1) * P], wt[:, 2, :],
                                                start=True, stop=True)
                    last.then_inc(sem["v_proj"], 1)
                    pe.wait_ge(sem["qk_ready"], 1)
                    nc.tensor.matmul(bank[1][:, :], swap[:, :], qk[:, :, :].rearrange("p n q -> p (n q)"), start=True,
                                     stop=True).then_inc(sem["rot_done"], 1)
                    pe.wait_ge(sem["qkr_ready"], 1)
                    for t in range(TPB):
                        last = nc.tensor.transpose(bank[3][:, t * P:(t + 1) * P], qkr[:, 1, t * P:(t + 1) * P], core.ident[:, :])
                    last.then_inc(sem["krt_done"], 1)
                    pe.wait_ge(sem["krt_ready"], 1)
                    pe.wait_ge(sem["v_ready"], 1)
                    for t in range(TPB):
                        last = nc.tensor.matmul(bank[4][:, 0:P], krt[:, t, :], v[:, t, :], start=(t == 0), stop=(t == TPB - 1))
                    last.then_inc(sem["kv_done"], 1)
                    pe.wait_ge(sem["mean_ready"], 2)
                    for t in range(TPB):
                        nc.tensor.matmul(bank[6][:, t * P:(t + 1) * P], qk[:, 0, t * P:(t + 1) * P], kmean[:, :],
                                         start=True, stop=True)
                    pe.wait_ge(sem["kv_ready"], 1)
                    for t in range(TPB):
                        last = nc.tensor.matmul(bank[5][:, t * P:(t + 1) * P], qkr[:, 0, t * P:(t + 1) * P], kv[:, :],
                                                start=True, stop=True)
                    last.then_inc(sem["o_done"], 1)

                @block.vector
                def _(dve):
                    after = chain(dve, sem["dve_step"])
                    table = lambda n: rope[:, n, :].rearrange("p (a q) -> p a q", a=1).to_broadcast([P, 2, SEQ])
                    dve.wait_ge(sem["gelu_ready"], 2)
                    nc.vector.tensor_scalar(qk[:, :, :], part[:, :, :], 0.21, None, ALU.add).then_inc(sem["qk_ready"], 1)
                    dve.wait_ge(sem["qk_ready"], 1)
                    nc.vector.tensor_reduce(mean[:, :], qk[:, 1, :], AX.X, ALU.add).then_inc(sem["mean_ready"], 1)
                    after(nc.vector.tensor_tensor(part[:, :, :], qk[:, :, :], table(0), ALU.mult))
                    dve.wait_ge(sem["mean_ready"], 1)
                    nc.vector.tensor_scalar(kmean[:, :], block_[:, :], mean[:, 0:1], 1.0 / SEQ, ALU.mult, ALU.mult).then_inc(sem["mean_ready"], 1)
                    dve.wait_ge(sem["v_proj"], 1)
                    nc.vector.tensor_tensor(v[:, :, :], bank[2][:, 0:SEQ].rearrange("p (t c) -> p t c", t=TPB),
                                            bv[:, :].rearrange("p (a c) -> p a c", a=1).to_broadcast([P, TPB, P]),
                                            ALU.add).then_inc(sem["v_ready"], 1)
                    dve.wait_ge(sem["rot_done"], 1)
                    after(nc.vector.tensor_tensor(qkr[:, :, :], bank[1][:, :].rearrange("p (n q) -> p n q", n=2), table(1), ALU.mult))
                    nc.vector.tensor_tensor(qkr[:, :, :], qkr[:, :, :], part[:, :, :], ALU.add).then_inc(sem["qkr_ready"], 1)
                    dve.wait_ge(sem["kv_done"], 1)
                    nc.vector.scalar_tensor_tensor(out=kv[:, :], in0=bank[4][:, 0:P], scalar=1.0 / SEQ, in1=block_[:, :],
                                                   op0=ALU.mult, op1=ALU.mult).then_inc(sem["kv_ready"], 1)
                    dve.wait_ge(sem["o_done"], 1)
                    tiles = lambda i: bank[i][:, 0:SEQ].rearrange("p (t c) -> p t c", t=TPB)
                    after(nc.vector.tensor_scalar(rec[:, :, :], tiles(6), 1e-6, None, ALU.add))
                    after(nc.vector.reciprocal(rec[:, :, :], rec[:, :, :]))
                    after(nc.vector.tensor_tensor(res[:, :, :], tiles(5), rec[:, :, :], ALU.mult))
                    nc.vector.tensor_tensor(core.s[:, bass.ds(b * TPB, TPB), :], res[:, :, :],
                                            core.xn[:, bass.ds(b * TPB, TPB), :], ALU.add).then_inc(sem["stored"], 1)
            zero()
        layer_norm_of_branch(core, 1e-12, gamma[:, :], beta[:, :])


def experts_stage(core):
    nc, dram, bank = core.nc, core.dram, core.bank
    with ExitStack() as ctx:
        def sb(name, shape, dt=F32):
            return ctx.enter_context(nc.sbuf_tensor("moe_" + name, shape, dt))

        chosen = sb("chosen", [P, NT, NE])
        with ExitStack() as ctx2:
            def sb2(name, shape, dt=F32):
                return ctx2.enter_context(nc.sbuf_tensor("route_" + name, shape, dt))

            names = ("turned", "router_ready", "logits_done", "exp_ready", "shifted", "top_ready", "top_stored", "top_spread",
                     "onehot_ready", "compared", "counted", "dve_step")
            sems, zero = ctx2.enter_context(signals(nc, ["route_" + n for n in names]))
            sem = dict(zip(names, sems))
            router, router_t = sb2("router", [NE, P]), sb2("router_t", [P, NE])
            expert_no, earlier = sb2("expert_no", [P, NT, NE]), sb2("earlier", [P, P])
            prob, onehot, cand = sb2("prob", [P, NT, NE]), sb2("onehot", [P, NT, NE]), sb2("cand", [P, NT, NE])
            onehot_b = sb2("onehot_b", [P, NT, NE], BF16)
            red, top, keep, count = sb2("red", [P, NT]), sb2("top", [P, NT]), sb2("keep", [P, NT]), sb2("count", [P, NT])
            row = sb2("row", [P, TOK])
            above, tie = sb2("above", [P, 2, TOK], BF16), sb2("tie", [P, P], BF16)
            top_dram = nc.dram_tensor("top_prob", (NT, P), F32, kind="Internal").ap()
            load(core, [(router[:, :], dram["L1_ffn_router_w"]), (expert_no[:, :, :], dram["expert_no"]),
                        (earlier[:, :], dram["strictly_before"])])
            wide = lambda v: v.rearrange("p (t a) -> p t a", a=1).to_broadcast([P, NT, NE])
            with nc.Block() as block:
                @block.tensor
                def _(pe):
                    nc.tensor.transpose(bank[0][:, 0:NE], router[:, :], core.ident[0:NE, 0:NE]).then_inc(sem["turned"], 1)
                    pe.wait_ge(sem["router_ready"], 1)
                    for i in range(NT):
                        last = nc.tensor.matmul(bank[1][:, i * NE:(i + 1) * NE], core.xnt[:, i * P:(i + 1) * P], router_t[:, :],
                                                start=True, stop=True)
                    last.then_inc(sem["logits_done"], 1)
                    pe.wait_ge(sem["onehot_ready"], 1)
                    for j in range(NT):
                        pe.wait_ge(sem["compared"], j + 1)
                        for i in range(NT):
                            last = nc.tensor.matmul(bank[2][:, i * NE:(i + 1) * NE], above[:, j % 2, i * P:(i + 1) * P],
                                                    onehot_b[:, j, :], start=(i == 0 and j == 0), stop=(j == NT - 1),
                                                    skip_group_check=True)
                        last.then_inc(sem["counted"], 1)

                @block.scalar
                def _(act):
                    act.wait_ge(sem["shifted"], 1)
                    nc.scalar.activation(prob[:, :, :], prob[:, :, :], ACT.Exp).then_inc(sem["exp_ready"], 1)

                @block.sync
                def _(sp):
                    sp.wait_ge(sem["top_ready"], 1)
                    sp.dma_start(top_dram.rearrange("t p -> p t"), top[:, :]).then_inc(sem["top_stored"], 16)
                    sp.wait_ge(sem["top_stored"], 16)
                    sp.dma_start(row[:, :], top_dram.rearrange("(a t) p -> a (t p)", a=1).to_broadcast([P, TOK])).then_inc(sem["top_spread"], 16)

                @block.vector
                def _(dve):
                    after = chain(dve, sem["dve_step"])
                    dve.wait_ge(sem["turned"], 1)
                    nc.vector.tensor_copy(router_t[:, :], bank[0][:, 0:NE]).then_inc(sem["router_ready"], 1)
                    dve.wait_ge(sem["logits_done"], 1)
                    logits = bank[1][:, 0:NT * NE].rearrange("p (t e) -> p t e", e=NE)
                    after(nc.vector.tensor_reduce(red[:, :], logits, AX.X, ALU.max))
                    nc.vector.tensor_tensor(prob[:, :, :], logits, wide(red[:, :]), ALU.subtract).then_inc(sem["shifted"], 1)
                    dve.wait_ge(sem["exp_ready"], 1)
                    after(nc.vector.tensor_reduce(red[:, :], prob[:, :, :], AX.X, ALU.add))
                    after(nc.vector.reciprocal(red[:, :], red[:, :]))
                    after(nc.vector.tensor_tensor(prob[:, :, :], prob[:, :, :], wide(red[:, :]), ALU.mult))
                    nc.vector.tensor_reduce(top[:, :], prob[:, :, :], AX.X, ALU.max).then_inc(sem["top_ready"], 1)
                    dve.wait_ge(sem["top_ready"], 1)
                    after(nc.vector.tensor_tensor(cand[:, :, :], prob[:, :, :], wide(top[:, :]), ALU.is_equal))
                    after(nc.vector.scalar_tensor_tensor(out=cand[:, :, :].rearrange("p t e -> p (t e)"),
                                                         in0=cand[:, :, :].rearrange("p t e -> p (t e)"), scalar=-100.0,
                                                         in1=expert_no[:, :, :].rearrange("p t e -> p (t e)"),
                                                         op0=ALU.mult, op1=ALU.add))
                    after(nc.vector.tensor_reduce(red[:, :], cand[:, :, :], AX.X, ALU.min))
                    after(nc.vector.tensor_tensor(onehot[:, :, :], cand[:, :, :], wide(red[:, :]), ALU.is_equal))
                    nc.vector.tensor_copy(onehot_b[:, :, :], onehot[:, :, :]).then_inc(sem["onehot_ready"], 1)
                    dve.wait_ge(sem["top_spread"], 16)
                    for j in range(NT):
                        if j >= 2:
                            dve.wait_ge(sem["counted"], j - 1)
                        m, mine = j % 2, top[:, j:j + 1]
                        d0, d1 = j * P, (j + 1) * P
                        after(nc.vector.tensor_scalar(above[:, m, 0:d1], row[:, 0:d1], mine, None, ALU.is_lt))
                        after(nc.vector.scalar_tensor_tensor(out=tie[:, :], in0=row[:, d0:d1], scalar=mine, in1=earlier[:, :],
                                                             op0=ALU.is_equal, op1=ALU.mult))
                        if j < NT - 1:
                            nc.vector.tensor_scalar(above[:, m, d1:TOK], row[:, d1:TOK], mine, None, ALU.is_le)
                        nc.vector.tensor_tensor(above[:, m, d0:d1], above[:, m, d0:d1], tie[:, :], ALU.add).then_inc(sem["compared"], 1)
                    dve.wait_ge(sem["counted"], NT)
                    counts = bank[2][:, 0:NT * NE].rearrange("p (t e) -> p t e", e=NE)
                    after(nc.vector.tensor_tensor(cand[:, :, :], counts, onehot[:, :, :], ALU.mult))
                    after(nc.vector.tensor_reduce(count[:, :], cand[:, :, :], AX.X, ALU.add))
                    after(nc.vector.tensor_scalar(keep[:, :], count[:, :], float(CAPACITY), None, ALU.is_lt))
                    after(nc.vector.tensor_tensor(chosen[:, :, :], onehot[:, :, :], wide(keep[:, :]), ALU.mult))
                    after(nc.vector.tensor_scalar(keep[:, :], keep[:, :], -1.0, 1.0, ALU.mult, ALU.add))
                    after(nc.vector.tensor_tensor(chosen[:, :, 0], chosen[:, :, 0], keep[:, :], ALU.add))
            zero()
        names = ("turned", "copied", "b2_done", "y_started", "hid_done", "h_act", "h_dve", "out_done", "added")
        sems, zero = ctx.enter_context(signals(nc, ["moe_" + n for n in names]))
        sem = dict(zip(names, sems))
        w1, w2, b1, b2 = sb("w1", [P, DFF]), sb("w2", [P, 4, P]), sb("b1", [P, 4]), sb("b2", [NE, P])
        sel_t = sb("sel_t", [NE, NT, P])
        h = sb("h", [P, 2, 4, 512])
        load(core, [(b2[:, :], dram["L1_ffn_b2"])])
        with nc.Block() as block:
            @block.tensor
            def _(pe):
                for g in range(NT // 4):
                    if g >= 2:
                        pe.wait_ge(sem["copied"], g - 1)
                    for i in range(4):
                        last = nc.tensor.transpose(bank[g % 2][0:NE, i * P:(i + 1) * P], chosen[:, 4 * g + i, :], core.ident[:, :])
                    last.then_inc(sem["turned"], 1)
                for g in range(NT // 4):
                    pe.wait_ge(sem["copied"], g + 1)
                    if g >= 2:
                        pe.wait_ge(sem["y_started"], g - 1)
                    for i in range(4):
                        last = nc.tensor.matmul(bank[2 + g % 2][:, i * P:(i + 1) * P], sel_t[:, 4 * g + i, :], b2[:, :],
                                                start=True, stop=True)
                    last.then_inc(sem["b2_done"], 1)

            @block.scalar
            def _(act):
                for g in range(NT // 4):
                    act.wait_ge(sem["turned"], g + 1)
                    nc.scalar.copy(sel_t[:, 4 * g:4 * g + 4, :], bank[g % 2][0:NE, :].rearrange("p (i q) -> p i q", i=4)).then_inc(sem["copied"], 1)

            @block.vector
            def _(dve):
                for g in range(NT // 4):
                    dve.wait_ge(sem["b2_done"], g + 1)
                    nc.vector.tensor_copy(core.y[:, 4 * g:4 * g + 4, :],
                                          bank[2 + g % 2][:, :].rearrange("p (i c) -> p i c", i=4)).then_inc(sem["y_started"], 1)
        zero()
        NBLK = TOK // 512
        with nc.Fori(0, NE) as e:
            load(core, [(w1[:, :], dram["L1_ffn_W1"][bass.ds(e, 1), :, :].rearrange("a p n -> p (a n)")),
                        (w2[:, :, :], dram["L1_ffn_W2"][bass.ds(e, 1), :, :].rearrange("a (c p) n -> p (a c) n", p=P)),
                        (b1[:, :], dram["L1_ffn_b1"][bass.ds(e, 1), :].rearrange("a (c p) -> p (a c)", p=P))])
            with nc.Block() as block:
                @block.tensor
                def _(pe):
                    def hidden(k):
                        for c in range(4):
                            if k >= 1:
                                pe.wait_ge(sem["h_act"] if c % 2 == 0 else sem["h_dve"], 2 * (k - 1) + c // 2 + 1)
                            nc.tensor.matmul(bank[c][:, :], w1[:, c * P:(c + 1) * P], core.xnt[:, k * 512:(k + 1) * 512],
                                             start=True, stop=True).then_inc(sem["hid_done"], 1)

                    def outputs(k):
                        pe.wait_ge(sem["h_act"], 2 * (k + 1))
                        pe.wait_ge(sem["h_dve"], 2 * (k + 1))
                        for i in range(4):
                            if k >= 1:
                                pe.wait_ge(sem["added"], 4 * (k - 1) + i + 1)
                            for c in range(4):
                                last = nc.tensor.matmul(bank[4 + i][:, 0:P], h[:, k % 2, c, i * P:(i + 1) * P], w2[:, c, :],
                                                        start=(c == 0), stop=(c == 3))
                            last.then_inc(sem["out_done"], 1)

                    for k in range(NBLK + 1):
                        if k < NBLK:
                            hidden(k)
                        if k >= 1:
                            outputs(k - 1)

                @block.scalar
                def _(act):
                    for k in range(NBLK):
                        if k >= 2:
                            act.wait_ge(sem["out_done"], 4 * (k - 1))
                        for c in (0, 2):
                            act.wait_ge(sem["hid_done"], 4 * k + c + 1)
                            nc.scalar.activation(h[:, k % 2, c, :], bank[c][:, :], ACT.Relu, bias=b1[:, c:c + 1]).then_inc(sem["h_act"], 1)

                @block.vector
                def _(dve):
                    for k in range(NBLK + 1):
                        if k < NBLK:
                            if k >= 2:
                                dve.wait_ge(sem["out_done"], 4 * (k - 1))
                            for c in (1, 3):
                                dve.wait_ge(sem["hid_done"], 4 * k + c + 1)
                                nc.vector.tensor_scalar(h[:, k % 2, c, :], bank[c][:, :], b1[:, c:c + 1], 0.0, ALU.add,
                                                        ALU.max).then_inc(sem["h_dve"], 1)
                        if k >= 1:
                            for i in range(4):
                                tile = 4 * (k - 1) + i
                                dve.wait_ge(sem["out_done"], tile + 1)
                                nc.vector.scalar_tensor_tensor(out=core.y[:, tile, :], in0=bank[4 + i][:, 0:P],
                                                               scalar=chosen[:, tile, bass.ds(e, 1)], in1=core.y[:, tile, :],
                                                               op0=ALU.mult, op1=ALU.add).then_inc(sem["added"], 1)
            zero()


def store_tile(core, sig, dve, att, shift, k, t, residual):
    nc = core.nc
    att.full(dve, "y", k, t)
    tile = bass.ds((shift + k) * TPB + t, 1)
    src = core.bank[7][:, 0:P].rearrange("p (a c) -> p a c", a=1)
    if residual:
        ins = nc.vector.tensor_tensor(core.s[:, tile, :], src, core.xn[:, tile, :], ALU.add)
    else:
        ins = nc.vector.tensor_copy(core.s[:, tile, :], src)
    sig.done(ins, "bank7_free")


def causal_attention_stage(core):
    nc, dram, bank = core.nc, core.dram, core.bank
    PAIRS, CH, FIRST_CHUNK = HEADS // 2, HEADS // 2 + 2 * TPB, 2
    with ExitStack() as ctx:
        def sb(name, shape, dt=F32):
            return ctx.enter_context(nc.sbuf_tensor("l2a_" + name, shape, dt))

        att = Softmax(core, sb, 64, False, "mask_causal", 1.0 / 8.0, ())
        proj = [16 * k + FIRST_CHUNK + r for k in range(NB) for r in range(CH)]
        number_at = {slot: i for i, slot in enumerate(proj)}
        when = dict(att.when)
        when.update({
            "x_ready": [16 * k + 1 for k in range(NB)],
            "proj_done": proj,
            "act_copied": [s + 1 for i, s in enumerate(proj) if i % 2 == 0],
            "dve_copied": [s + 1 for i, s in enumerate(proj) if i % 2 == 1],
        })
        names = tuple(when)
        sems, zero = ctx.enter_context(signals(nc, ["l2a_" + n for n in names]))
        sig = att.sig = Signals(dict(zip(names, sems)), when)
        w = {n: sb("w" + n, [P, HEADS, 64]) for n in "qkv"}
        gamma, beta, xb = sb("gamma", [P, P]), sb("beta", [P, P]), sb("xb", [P, SEQ])
        load(core, [(w[n][:, :, :], dram["L2_attn_W" + n].rearrange("h d e -> d h e")) for n in w] +
             [(att.wo[:, :, :], dram["L2_attn_Wo"].rearrange("(c p) n -> p c n", p=P)), (att.mask[:, :, :], att.mask_src),
              (gamma[:, :], spread(dram["L2_attn_gamma"])), (beta[:, :], spread(dram["L2_attn_beta"]))])

        def pair(n, hp):
            return w[n][:, 2 * hp:2 * hp + 2, :].rearrange("p h e -> p (h e)")

        def copy_chunk(eng, copy, i, done):
            k, c = i // CH, i % CH
            sig.wait(eng, "proj_done", i + 1)
            src = bank[5 + i % 2]
            if c < PAIRS:
                copy(att.qt[:, k % 2, c, :], src[:, 0:SEQ])
                sig.done(copy(att.kt[:, k % 2, c, :], src[:, SEQ:2 * SEQ]), done)
            else:
                t, half = (c - PAIRS) // 2, (c - PAIRS) % 2
                sig.done(copy(att.v[:, k % 2, t, half * 512:(half + 1) * 512], src[:, :]), done)

        def emit(block, slots, shift):
            @block.scalar
            def _(act):
                for slot in slots:
                    att.copy_turned(act, slot - 19)
                    att.exps(act, slot - 17)
                    if slot % 16 == 1 and slot // 16 < NB:
                        k = slot // 16
                        sig.wait(act, "proj_done", CH * k)
                        sig.done(nc.scalar.copy(xb[:, :], core.xnt[:, bass.ds((shift + k) * SEQ, SEQ)]), "x_ready")
                    i = number_at.get(slot - 1, 1)
                    if i % 2 == 0:
                        copy_chunk(act, nc.scalar.copy, i, "act_copied")

            @block.tensor
            def _(pe):
                for slot in slots:
                    i = number_at.get(slot)
                    if i is not None:
                        k, c = i // CH, i % CH
                        if c == 0:
                            sig.wait(pe, "x_ready", k + 1)
                        if i >= 2:
                            sig.wait(pe, "dve_copied" if i % 2 else "act_copied", i // 2)
                        to = bank[5 + i % 2]
                        if c < PAIRS:
                            nc.tensor.matmul(to[:, 0:SEQ], pair("q", c), xb[:, :], start=True, stop=True)
                            ins = nc.tensor.matmul(to[:, SEQ:2 * SEQ], pair("k", c), xb[:, :], start=True, stop=True)
                        else:
                            t, half = (c - PAIRS) // 2, (c - PAIRS) % 2
                            ins = nc.tensor.matmul(to[:, :], xb[:, t * P:(t + 1) * P],
                                                   w["v"][:, 8 * half:8 * half + 8, :].rearrange("p h e -> p (h e)"),
                                                   start=True, stop=True)
                        sig.done(ins, "proj_done")
                    att.values(pe, slot - 20)
                    if slot in att.at:
                        kind, k, j = att.at[slot]
                        (att.turn_part if kind == "part" else att.project_out)(pe, k, j)
                    att.turn(pe, slot - 18)
                    att.scores(pe, slot - 16)

            @block.vector
            def _(dve):
                for slot in slots:
                    att.mask_and_max(dve, slot - 17)
                    kind, k, j = att.at.get(slot - 1, (None, 0, 0))
                    if kind == "part":
                        att.copy_part(dve, nc.vector.tensor_copy, k, j)
                    elif kind == "y":
                        store_tile(core, sig, dve, att, shift, k, j, residual=True)
                    i = number_at.get(slot - 1, 0)
                    if i % 2 == 1:
                        copy_chunk(dve, nc.vector.tensor_copy, i, "dve_copied")
                    att.normalise(dve, slot - 21)

        run_windows(nc, sig, zero, emit, att.last_slot)
        layer_norm_of_branch(core, 1e-3, gamma[:, :], beta[:, :])


def routed_ffn_stage(core):
    nc, dram, bank = core.nc, core.dram, core.bank
    with ExitStack() as ctx:
        def sb(name, shape, dt=F32):
            return ctx.enter_context(nc.sbuf_tensor("cd_" + name, shape, dt))

        weight = sb("weight", [P, NT])
        with ExitStack() as ctx2:
            def sb2(name, shape, dt=F32):
                return ctx2.enter_context(nc.sbuf_tensor("cd_" + name, shape, dt))

            names = ("rt_ready", "s_done", "dve_step", "max_ready", "sum_ready", "log_ready", "z_ready", "score_ready",
                     "stored", "spread_")
            sems, zero = ctx2.enter_context(signals(nc, ["cd_" + n for n in names]))
            sem = dict(zip(names, sems))
            rt, rtm = sb2("rt", [P, 1]), sb2("rtm", [P, NB, NB])
            s, r, u, e = sb2("s", [NB, SEQ]), sb2("r", [NB, SEQ]), sb2("u", [NB, SEQ]), sb2("e", [NB, SEQ])
            m, nm, total, log, a = (sb2(n, [NB, 1]) for n in ("m", "nm", "total", "log", "a"))
            row, mine, before = sb2("row", [P, NB, SEQ]), sb2("mine", [P, NT]), sb2("before", [P, TPB, SEQ])
            junk, more, same = sb2("junk", [P, 2, SEQ]), sb2("more", [P, NT]), sb2("same", [P, NT])
            score_dram = nc.dram_tensor("route_score", (NB, SEQ), F32, kind="Internal").ap()
            load(core, [(rt[:, :], column(dram["L2_ffn_routing_token"])), (before[:, :, :], dram["before"])])
            with nc.Block() as block:
                @block.vector
                def _(dve):
                    after = chain(dve, sem["dve_step"])
                    after(nc.vector.memset(rtm[:, :, :], 0.0))
                    for b in range(NB):
                        last = nc.vector.tensor_copy(rtm[:, b, b:b + 1], rt[:, :])
                    last.then_inc(sem["rt_ready"], 1)
                    dve.wait_ge(sem["s_done"], 1)
                    after(nc.vector.tensor_copy(s[:, :], bank[0][0:NB, 0:SEQ]))
                    after(nc.vector.tensor_scalar(r[:, :], s[:, :], 0.0, None, ALU.max))

                @block.tensor
                def _(pe):
                    pe.wait_ge(sem["rt_ready"], 1)
                    for b in range(NB):
                        last = nc.tensor.matmul(bank[0][0:NB, 0:SEQ], rtm[:, b, :], core.xnt[:, b * SEQ:(b + 1) * SEQ],
                                                start=(b == 0), stop=(b == NB - 1))
                    last.then_inc(sem["s_done"], 1)
            zero()
            UNROLL = 10
            with nc.Fori(0, ROUTE_ITERS // UNROLL) as _i:
                with nc.Block() as block:
                    @block.vector
                    def _(dve):
                        after = chain(dve, sem["dve_step"])
                        for k in range(UNROLL):
                            after(nc.vector.tensor_tensor_reduce(u[:, :], s[:, :], r[:, :], 1.0 / EPS_ROUTE, LOWEST,
                                                                 ALU.subtract, ALU.max, m[:, :]))
                            nc.vector.tensor_scalar(nm[:, :], m[:, :], -1.0, None, ALU.mult).then_inc(sem["max_ready"], 1)
                            dve.wait_ge(sem["log_ready"], k + 1)
                            after(nc.vector.tensor_tensor(a[:, :], log[:, :], m[:, :], ALU.add))
                            after(nc.vector.tensor_scalar(a[:, :], a[:, :], -EPS_ROUTE, float(np.float32(EPS_ROUTE) * np.log(np.float32(K_ROUTE))),
                                                          ALU.mult, ALU.add))
                            after(nc.vector.tensor_scalar(r[:, :], s[:, :], a[:, 0:1], 0.0, ALU.add, ALU.max))

                    @block.scalar
                    def _(act):
                        for k in range(UNROLL):
                            act.wait_ge(sem["max_ready"], k + 1)
                            nc.scalar.activation(e[:, :], u[:, :], ACT.Exp, bias=nm[:, 0:1], accum_out=total[:, :]).then_inc(sem["sum_ready"], 1)
                            act.wait_ge(sem["sum_ready"], k + 1)
                            nc.scalar.activation(log[:, :], total[:, :], ACT.Ln).then_inc(sem["log_ready"], 1)
                zero()
            with nc.Block() as block:
                @block.vector
                def _(dve):
                    after = chain(dve, sem["dve_step"])
                    after(nc.vector.scalar_tensor_tensor(out=u[:, :], in0=s[:, :], scalar=a[:, 0:1], in1=r[:, :],
                                                         op0=ALU.add, op1=ALU.subtract))
                    nc.vector.tensor_scalar(u[:, :], u[:, :], 1.0 / EPS_ROUTE, -87.336545, ALU.mult, ALU.max).then_inc(sem["z_ready"], 1)
                    dve.wait_ge(sem["spread_"], 32)
                    for b in range(NB):
                        for t in range(TPB):
                            i = b * TPB + t
                            after(nc.vector.tensor_scalar(junk[:, 0, :], row[:, b, :], mine[:, i:i + 1], 0.0, ALU.is_gt, ALU.add,
                                                          accum_out=more[:, i:i + 1]))
                            after(nc.vector.scalar_tensor_tensor(out=junk[:, 1, :], in0=row[:, b, :], scalar=mine[:, i:i + 1],
                                                                 in1=before[:, t, :], op0=ALU.is_equal, op1=ALU.mult,
                                                                 accum_out=same[:, i:i + 1]))
                    after(nc.vector.tensor_tensor(more[:, :], more[:, :], same[:, :], ALU.add))
                    after(nc.vector.tensor_scalar(more[:, :], more[:, :], float(NUM_HEAVY), None, ALU.is_lt))
                    after(nc.vector.tensor_scalar(same[:, :], mine[:, :], -1.0, 1.0, ALU.mult, ALU.add))
                    after(nc.vector.tensor_tensor(same[:, :], same[:, :], mine[:, :], ALU.add))
                    after(nc.vector.tensor_tensor(weight[:, :], same[:, :], more[:, :], ALU.mult))

                @block.scalar
                def _(act):
                    act.wait_ge(sem["z_ready"], 1)
                    nc.scalar.activation(e[:, :], u[:, :], ACT.Exp).then_inc(sem["score_ready"], 1)

                @block.sync
                def _(sp):
                    sp.wait_ge(sem["score_ready"], 1)
                    sp.dma_start(score_dram, e[:, :]).then_inc(sem["stored"], 16)
                    sp.wait_ge(sem["stored"], 16)
                    sp.dma_start(row[:, :, :].rearrange("p b q -> p (b q)"),
                                 score_dram.rearrange("(a b) q -> a (b q)", a=1).to_broadcast([P, TOK])).then_inc(sem["spread_"], 16)
                    sp.dma_start(mine[:, :], score_dram.rearrange("b (t p) -> p (b t)", p=P)).then_inc(sem["spread_"], 16)
            zero()
        names = ("dve_step", "xr_ready", "cols_done", "xg_ready", "hid_done", "h_ready", "out_done", "sum_ready", "light_added", "stored")
        sems, zero = ctx.enter_context(signals(nc, ["lh_" + n for n in names]))
        sem = dict(zip(names, sems))
        w1l, w2l = sb("w1l", [P, LIGHT]), sb("w2l", [LIGHT, P])
        w1h, w2h = sb("w1h", [P, HEAVY]), sb("w2h", [P, 4, P])
        b1l, b2l, b1h, b2h = sb("b1l", [LIGHT, 1]), sb("b2l", [P, P]), sb("b1h", [P, 4]), sb("b2h", [P, P])
        gl, gh = sb("gl", [P, 1]), sb("gh", [P, 1])
        xr, n2, rn, tmp = sb("xr", [P, 4, P]), sb("n2", [P, 4]), sb("rn", [P, 4]), sb("tmp", [P, 4])
        xl, xh = sb("xl", [P, 512]), sb("xh", [P, 512])
        hl, hh = sb("hl", [LIGHT, 512]), sb("hh", [P, 4, 512])
        heavy, both = sb("heavy", [P, 4, P]), sb("both", [P, 4, P])
        load(core, [(w1l[:, :], dram["L2_ffn_w1_light"]), (w2l[:, :], dram["L2_ffn_w2_light"]),
                    (w1h[:, :], dram["L2_ffn_w1_heavy"]), (w2h[:, :, :], dram["L2_ffn_w2_heavy"].rearrange("(c p) n -> p c n", p=P)),
                    (b1l[:, :], column(dram["L2_ffn_b1_light"])), (b2l[:, :], spread(dram["L2_ffn_b2_light"])),
                    (b1h[:, :], dram["L2_ffn_b1_heavy"].rearrange("(c p) -> p c", p=P)), (b2h[:, :], spread(dram["L2_ffn_b2_heavy"])),
                    (gl[:, :], column(dram["L2_ffn_gamma_light"])), (gh[:, :], column(dram["L2_ffn_gamma_heavy"]))])
        with nc.Fori(0, NT // 4) as i:
            with nc.Block() as block:
                @block.vector
                def _(dve):
                    after = chain(dve, sem["dve_step"])
                    for j in range(4):
                        x = core.xn[:, bass.ds(i * 4 + j, 1), :]
                        last = nc.vector.tensor_tensor(xr[:, j:j + 1, :], x, x, ALU.mult)
                    after(last)
                    after(nc.vector.tensor_reduce(n2[:, :], xr[:, :, :], AX.X, ALU.add))
                    after(nc.vector.tensor_scalar(n2[:, :], n2[:, :], 1e-24, None, ALU.max))
                    rsqrt(nc, after, rn[:, :], n2[:, :], tmp[:, :])
                    after(nc.vector.tensor_scalar(rn[:, :], rn[:, :], float(np.sqrt(P)), None, ALU.mult))
                    for j in range(4):
                        last = nc.vector.tensor_scalar(xr[:, j:j + 1, :], core.xn[:, bass.ds(i * 4 + j, 1), :], rn[:, j:j + 1], None,
                                                       ALU.mult)
                    last.then_inc(sem["xr_ready"], 1)
                    dve.wait_ge(sem["out_done"], 2)
                    after(nc.vector.tensor_tensor(heavy[:, :, :], bank[7][:, :].rearrange("p (j c) -> p j c", j=4),
                                                  b2h[:, :].rearrange("p (a c) -> p a c", a=1).to_broadcast([P, 4, P]), ALU.add))
                    for j in range(4):
                        last = nc.vector.scalar_tensor_tensor(out=both[:, j, :], in0=heavy[:, j, :],
                                                              scalar=weight[:, bass.ds(i * 4 + j, 1)],
                                                              in1=bank[6][:, j * P:(j + 1) * P], op0=ALU.mult, op1=ALU.add)
                    after(last)
                    nc.vector.tensor_tensor(core.y[:, bass.ds(i * 4, 4), :], both[:, :, :],
                                            b2l[:, :].rearrange("p (a c) -> p a c", a=1).to_broadcast([P, 4, P]),
                                            ALU.add).then_inc(sem["stored"], 1)

                @block.tensor
                def _(pe):
                    pe.wait_ge(sem["xr_ready"], 1)
                    for j in range(4):
                        last = nc.tensor.transpose(bank[0][:, j * P:(j + 1) * P], xr[:, j, :], core.ident[:, :])
                    last.then_inc(sem["cols_done"], 1)
                    pe.wait_ge(sem["xg_ready"], 2)
                    nc.tensor.matmul(bank[1][0:LIGHT, :], w1l[:, :], xl[:, :], start=True, stop=True).then_inc(sem["hid_done"], 1)
                    for c in range(4):
                        nc.tensor.matmul(bank[2 + c][:, :], w1h[:, c * P:(c + 1) * P], xh[:, :], start=True,
                                         stop=True).then_inc(sem["hid_done"], 1)
                    pe.wait_ge(sem["h_ready"], 1)
                    for j in range(4):
                        last = nc.tensor.matmul(bank[6][:, j * P:(j + 1) * P], hl[:, j * P:(j + 1) * P], w2l[:, :],
                                                start=True, stop=True)
                    last.then_inc(sem["out_done"], 1)
                    pe.wait_ge(sem["h_ready"], 5)
                    for j in range(4):
                        for c in range(4):
                            last = nc.tensor.matmul(bank[7][:, j * P:(j + 1) * P], hh[:, c, j * P:(j + 1) * P], w2h[:, c, :],
                                                    start=(c == 0), stop=(c == 3))
                    last.then_inc(sem["out_done"], 1)

                @block.scalar
                def _(act):
                    act.wait_ge(sem["cols_done"], 1)
                    nc.scalar.activation(xl[:, :], bank[0][:, :], ACT.Copy, scale=gl[:, 0:1]).then_inc(sem["xg_ready"], 1)
                    nc.scalar.activation(xh[:, :], bank[0][:, :], ACT.Copy, scale=gh[:, 0:1]).then_inc(sem["xg_ready"], 1)
                    act.wait_ge(sem["hid_done"], 1)
                    nc.scalar.activation(hl[:, :], bank[1][0:LIGHT, :], ACT.Gelu, bias=b1l[:, 0:1]).then_inc(sem["h_ready"], 1)
                    for c in range(4):
                        act.wait_ge(sem["hid_done"], c + 2)
                        nc.scalar.activation(hh[:, c, :], bank[2 + c][:, :], ACT.Gelu, bias=b1h[:, c:c + 1]).then_inc(sem["h_ready"], 1)
            zero()


def small_head_attention_stage(core):
    nc, dram, bank = core.nc, core.dram, core.bank
    with ExitStack() as ctx:
        def sb(name, shape, dt=F32):
            return ctx.enter_context(nc.sbuf_tensor("l3a_" + name, shape, dt))

        att = Softmax(core, sb, 8, False, "mask_causal", float(1.0 / np.sqrt(np.float32(8.0))), ())
        at = lambda *slots: [16 * k + s for k in range(NB) for s in slots]
        when = dict(att.when)
        when.update({
            "x_ready": at(1),
            "proj_done": at(2), "rot_done": at(3),
            "v_proj": at(4),
            "cos_ready": at(3),
            "sin_ready": at(4, 4), "roped": at(5, 5),
            "heads_ready": at(6, 6, 6, 6),
            "v_ready": at(5),
        })
        names = tuple(when) + ("w_ready",)
        sems, zero = ctx.enter_context(signals(nc, ["l3a_" + n for n in names]))
        sem = dict(zip(names, sems))
        sig = att.sig = Signals(sem, when)
        w, wr = {n: sb("w" + n, [P, P]) for n in "qkv"}, {n: sb("wr" + n, [P, P]) for n in "qk"}
        rope, head4 = sb("rope", [P, 2, SEQ]), sb("head4", [P, 4])
        xb, part, q = sb("xb", [P, SEQ]), sb("part", [P, 2, SEQ]), sb("q", [P, SEQ])
        load(core, [(w[n][:, :], dram["L3_attn_W" + n]) for n in w] +
             [(att.wo[:, 0, :], dram["L3_attn_Wo"]), (att.mask[:, :, :], att.mask_src), (rope[:, :, :], dram["rope_l3"]),
              (head4[:, :], dram["head_of_4"])])
        with nc.Block() as block:
            @block.vector
            def _(dve):
                for n in "qk":
                    src, dst = (z[n][:, :].rearrange("p (c s) -> p c s", s=2) for z in (w, wr))
                    nc.vector.tensor_scalar(dst[:, :, 0], src[:, :, 1], -1.0, None, ALU.mult)
                    last = nc.vector.tensor_copy(dst[:, :, 1], src[:, :, 0])
                last.then_inc(sem["w_ready"], 1)
                nc.vector.memset(att.v[:, :, :, :], 0.0).then_inc(sem["w_ready"], 1)
        zero()
        both = lambda z: z.rearrange("p (n q) -> p n q", n=2)
        cos = rope[:, 0, :].rearrange("p (a q) -> p a q", a=1).to_broadcast([P, 2, SEQ])

        def emit(block, slots, shift):
            @block.scalar
            def _(act):
                for slot in slots:
                    k, s = slot // 16, slot % 16
                    att.copy_turned(act, slot - 20)
                    att.exps(act, slot - 17)
                    if k < NB and s == 1:
                        sig.wait(act, "v_proj", k)
                        sig.done(nc.scalar.copy(xb[:, :], core.xnt[:, bass.ds((shift + k) * SEQ, SEQ)]), "x_ready")
                    if k < NB and s == 5:
                        sig.wait(act, "v_proj", k + 1)
                        for t in range(TPB):
                            last = nc.scalar.copy(att.v[:, k % 2, t, :].rearrange("p (h c) -> p h c", h=HEADS)[:, :, 0:8],
                                                  bank[5][:, t * P:(t + 1) * P].rearrange("p (h d) -> p h d", d=8))
                        sig.done(last, "v_ready")

            @block.tensor
            def _(pe):
                for slot in slots:
                    k, s = slot // 16, slot % 16
                    if k < NB and s in (2, 3):
                        if s == 2:
                            sig.wait(pe, "x_ready", k + 1)
                            sig.wait(pe, "v_ready", k)
                        else:
                            sig.wait(pe, "sin_ready", 2 * k)
                        for i, n in enumerate("qk"):
                            last = nc.tensor.matmul(bank[3 + s][:, i * SEQ:(i + 1) * SEQ], (w if s == 2 else wr)[n][:, :],
                                                    xb[:, :], start=True, stop=True)
                        sig.done(last, "proj_done" if s == 2 else "rot_done")
                    if k < NB and s == 4:
                        sig.wait(pe, "cos_ready", k + 1)
                        for t in range(TPB):
                            last = nc.tensor.matmul(bank[5][:, t * P:(t + 1) * P], xb[:, t * P:(t + 1) * P], w["v"][:, :],
                                                    start=True, stop=True)
                        sig.done(last, "v_proj")
                    att.values_to_columns(pe, slot - 21)
                    if slot in att.at:
                        kind, kk, j = att.at[slot]
                        att.project_out(pe, kk, j)
                    att.turn(pe, slot - 19)
                    if slot % 16 == 0 and 1 <= k <= NB:
                        sig.wait(pe, "heads_ready", 4 * k)
                        sig.wait(pe, "roped", 2 * k)
                    att.scores(pe, slot - 16)

            @block.gpsimd
            def _(pool):
                for slot in slots:
                    k, s = slot // 16, slot % 16
                    if k < NB and s == 6:
                        sig.wait(pool, "roped", 2 * k + 1)
                        for j in range(4):
                            sig.done(nc.gpsimd.tensor_scalar(att.qt[:, k % 2, j, :], q[:, :], head4[:, j:j + 1], None, ALU.mult),
                                     "heads_ready")

            @block.vector
            def _(dve):
                for slot in slots:
                    k, s = slot // 16, slot % 16
                    att.mask_and_max(dve, slot - 17)
                    att.divide(dve, slot - 18)
                    kind, kk, j = att.at.get(slot - 1, (None, 0, 0))
                    if kind == "y":
                        store_tile(core, sig, dve, att, shift, kk, j, residual=False)
                    kt = att.kt[:, k % 2, 0, :]
                    if k < NB and s == 3:
                        sig.wait(dve, "proj_done", k + 1)
                        sig.wait(dve, "roped", 2 * k)
                        sig.done(nc.vector.tensor_tensor(part[:, :, :], both(bank[5][:, :]), cos, ALU.mult), "cos_ready")
                    if k < NB and s == 4:
                        sig.wait(dve, "rot_done", k + 1)
                        sig.wait(dve, "heads_ready", 4 * k)
                        for i, dst in enumerate((q[:, :], kt)):
                            sig.done(nc.vector.tensor_tensor(dst, bank[6][:, i * SEQ:(i + 1) * SEQ], rope[:, 1, :], ALU.mult),
                                     "sin_ready")
                    if k < NB and s == 5:
                        sig.wait(dve, "sin_ready", 2 * (k + 1))
                        sig.wait(dve, "cos_ready", k + 1)
                        for i, dst in enumerate((q[:, :], kt)):
                            sig.done(nc.vector.tensor_tensor(dst, dst, part[:, i, :], ALU.add), "roped")
                    att.copy_columns(dve, slot - 22)

        run_windows(nc, sig, zero, emit, att.last_slot)


def grouped_ffn_stage(core):
    nc, dram, bank = core.nc, core.dram, core.bank
    with ExitStack() as ctx:
        def sb(name, shape, dt=F32):
            return ctx.enter_context(nc.sbuf_tensor("grp_" + name, shape, dt))

        names = ("loaded", "turned", "w_ready", "hid_done", "h_ready", "out_done", "stored")
        sems, zero = ctx.enter_context(signals(nc, ["grp_" + n for n in names]))
        sem = dict(zip(names, sems))
        w1, w2, w1t, w2t = (sb(n, [P, 4, P]) for n in ("w1", "w2", "w1t", "w2t"))
        b1, b2, h = sb("b1", [P, 4]), sb("b2", [P, P]), sb("h", [P, 4, GTOK])
        with nc.Fori(0, NG) as g:
            with nc.Block() as block:
                @block.sync
                def _(sp):
                    one = bass.ds(g, 1)
                    sp.dma_start(w1[:, :, :], dram["L3_ffn_W1"][one, :, :].rearrange("a (c p) h -> p (a c) h", p=P)).then_inc(sem["loaded"], 16)
                    sp.dma_start(w2[:, :, :], dram["L3_ffn_W2"][one, :, :].rearrange("a p (c o) -> p (a c) o", o=P)).then_inc(sem["loaded"], 16)
                    sp.dma_start(b1[:, :], dram["L3_ffn_b1"][one, :].rearrange("a (c p) -> p (a c)", p=P)).then_inc(sem["loaded"], 16)
                    sp.dma_start(b2[:, :], dram["L3_ffn_b2"][one, :].to_broadcast([P, P])).then_inc(sem["loaded"], 16)
                    sp.wait_ge(sem["loaded"], 64)

                @block.tensor
                def _(pe):
                    pe.wait_ge(sem["loaded"], 64)
                    for i, w in enumerate((w1, w2)):
                        for c in range(4):
                            last = nc.tensor.transpose(bank[i][:, c * P:(c + 1) * P], w[:, c, :], core.ident[:, :])
                        last.then_inc(sem["turned"], 1)
                    pe.wait_ge(sem["w_ready"], 1)
                    for c in range(4):
                        nc.tensor.matmul(bank[2 + c][:, :], w1t[:, c, :], core.xnt[:, bass.ds(g * GTOK, GTOK)], start=True,
                                         stop=True).then_inc(sem["hid_done"], 1)
                    pe.wait_ge(sem["w_ready"], 2)
                    pe.wait_ge(sem["h_ready"], 4)
                    for j in range(4):
                        for c in range(4):
                            last = nc.tensor.matmul(bank[6][:, j * P:(j + 1) * P], h[:, c, j * P:(j + 1) * P], w2t[:, c, :],
                                                    start=(c == 0), stop=(c == 3))
                    last.then_inc(sem["out_done"], 1)

                @block.scalar
                def _(act):
                    for c in range(4):
                        act.wait_ge(sem["hid_done"], c + 1)
                        nc.scalar.activation(h[:, c, :], bank[2 + c][:, :], ACT.Identity, bias=b1[:, c:c + 1]).then_inc(sem["h_ready"], 1)

                @block.vector
                def _(dve):
                    for i, wt in enumerate((w1t, w2t)):
                        dve.wait_ge(sem["turned"], i + 1)
                        nc.vector.tensor_copy(wt[:, :, :], bank[i][:, :].rearrange("p (c q) -> p c q", c=4)).then_inc(sem["w_ready"], 1)
                    dve.wait_ge(sem["out_done"], 1)
                    nc.vector.tensor_tensor(core.y[:, bass.ds(g * 4, 4), :], bank[6][:, :].rearrange("p (j c) -> p j c", j=4),
                                            b2[:, :].rearrange("p (a c) -> p a c", a=1).to_broadcast([P, 4, P]),
                                            ALU.add).then_inc(sem["stored"], 1)
            zero()


LAYERS_RUN = DEPTH


def program(nc, dram, out, stop=None):
    with ExitStack() as ctx:
        ctx.enter_context(nc.allow_non_contiguous_dma(reason="vectors of a few hundred elements laid over partitions"))
        core = Core(nc, dram, ctx)
        load(core, [(core.x[:, :, :], dram["L0_attn_x"].rearrange("b (t p) c -> p (b t) c", p=P)),
                    (core.ident[:, :], dram["ident"])])

        def store(rows):
            with signals(nc, ["out_stored"]) as ((out_stored,), zero):
                with nc.Block() as block:
                    @block.sync
                    def _(sp):
                        sp.dma_start(out.rearrange("b (t p) c -> p (b t) c", p=P), rows[:, :, :]).then_inc(out_stored, 16)
                        sp.wait_ge(out_stored, 16)

        for name, stage, shown in stages():
            stage(core)
            core.stage += 1
            if stop == name:
                return store(shown(core))
        store(core.x)


def stages():
    return [
        ("ln0", layer_norm_stage, lambda c: c.xn),
        ("s0", linear_attention_stage, lambda c: c.s),
        ("g0", local_transformer_stage, lambda c: c.y),
        ("x0", combine_stage, lambda c: c.x),
        ("ln1", layer_norm_stage, lambda c: c.xn),
        ("s1", gelu_linear_attention_stage, lambda c: c.s),
        ("g1", experts_stage, lambda c: c.y),
        ("x1", combine_stage, lambda c: c.x),
        ("ln2", layer_norm_stage, lambda c: c.xn),
        ("s2", causal_attention_stage, lambda c: c.s),
        ("g2", routed_ffn_stage, lambda c: c.y),
        ("x2", combine_stage, lambda c: c.x),
        ("ln3", layer_norm_stage, lambda c: c.xn),
        ("s3", small_head_attention_stage, lambda c: c.s),
        ("g3", grouped_ffn_stage, lambda c: c.y),
        ("x3", combine_stage, lambda c: c.x),
    ]


def kernel(**inputs):
    import concourse.bacc as bacc
    from concourse.bass_utils import run_bass_kernel_spmd

    arrays = {f"in_{k}": np.ascontiguousarray(v) for k, v in inputs.items()}
    arrays.update({f"table_{k}": v for k, v in shape_constants().items()})
    nc = bacc.Bacc("TRN2", target_bir_lowering=False, num_devices=1)
    dram = {n.split("_", 1)[1]: nc.dram_tensor(n, a.shape, F32, kind="ExternalInput").ap() for n, a in arrays.items()}
    out = nc.dram_tensor("out", (NB, SEQ, P), F32, kind="ExternalOutput").ap()
    program(nc, dram, out)
    r = run_bass_kernel_spmd(nc, [arrays], core_ids=[0])
    return r.results[0]["out"]
```

```python
from contextlib import ExitStack, contextmanager

import numpy as np

import concourse.bass as bass
from concourse import mybir

F32 = mybir.dt.float32
I32 = mybir.dt.int32
BF16 = mybir.dt.bfloat16
ALU = mybir.AluOpType
ACT = mybir.ActivationFunctionType
AX = mybir.AxisListType

P = 128
NB, SEQ = 16, 256
TPB = SEQ // P
NT = NB * TPB
TOK = NB * SEQ
HEADS = 16
NEG = -1.0e20
LOWEST = -3.0e38

DEPTH, DH, WINDOW = 6, 64, 32
LOOP_WINDOWS = 6
INNER = HEADS * DH
DIM_INNER = int(P * 4 * 2 / 3)
HID_CHUNKS = [(0, 128), (128, 128), (256, DIM_INNER - 256)]
QK_SCALE = 8.0
NE, DFF = 8, 512
CAPACITY = int(np.ceil(TOK / NE * 1.25))
ROUTE_ITERS, EPS_ROUTE, K_ROUTE, NUM_HEAVY = 50, 0.1, 8.0, 128
LIGHT, HEAVY = 64, 512
NG, INTER = 8, 512
GTOK = TOK // NG


def shape_constants():
    c = {}
    i = np.arange(P)
    c["ident"] = np.eye(P, dtype=np.float32)
    c["upto"] = (i[:, None] <= i[None, :]).astype(np.float32)
    causal = np.full((P, TPB, SEQ), NEG, np.float32)
    local = np.full((P, TPB, SEQ), NEG, np.float32)
    for t in range(TPB):
        q = t * P + i
        k = np.arange(SEQ)
        causal[:, t][k[None, :] <= q[:, None]] = 0.0
        first = local_first_key(t)
        w = local_width(t)
        kk = first + np.arange(w)
        ok = (kk[None, :] <= q[:, None]) & (q[:, None] <= kk[None, :] + WINDOW)
        ok &= (kk[None, :] // WINDOW) >= (q[:, None] // WINDOW - 1)
        local[:, t, :w][ok] = 0.0
    c["mask_causal"], c["mask_local"] = causal, local
    half = np.arange(0, DH, 2, dtype=np.float32)
    inv_freq = (np.float32(1.0) / np.float32(10000.0) ** (half / np.float32(DH))).astype(np.float32)
    t = np.arange(SEQ, dtype=np.float32)
    freqs = (t[:, None] * inv_freq[None, :]).astype(np.float32)
    freqs = np.concatenate([freqs, freqs], -1)
    base = ((half + np.float32(0.4 * DH)) / np.float32(1.4 * DH)).astype(np.float32)
    power = ((t - SEQ // 2) / np.float32(WINDOW // 2)).astype(np.float32)
    scale = (base[None, :] ** power[:, None]).astype(np.float32)
    scale = np.concatenate([scale, scale], -1)
    sign = np.where(np.arange(DH) < DH // 2, -1.0, 1.0).astype(np.float32)
    cos, sin = np.cos(freqs), np.sin(freqs) * sign
    inv = (np.float32(1.0) / scale).astype(np.float32)
    tab = np.stack([cos * scale, sin * scale, cos * inv, sin * inv], 1)
    c["rope_local"] = np.ascontiguousarray(tab.reshape(TPB, P, 4, DH).transpose(1, 0, 2, 3)).astype(np.float32)
    for name, d in (("rope_l1", P), ("rope_l3", 8)):
        f = (np.float32(1.0) / np.float32(10000.0) ** (np.arange(0, d, 2, dtype=np.float32) / np.float32(d))).astype(np.float32)
        ang = (t[:, None] * f[None, :]).astype(np.float32)
        both = np.stack([np.repeat(np.cos(ang), 2, 1), np.repeat(np.sin(ang), 2, 1)], 0)
        c[name] = np.ascontiguousarray(np.tile(both, (1, 1, P // d)).transpose(2, 0, 1)).astype(np.float32)
    swap = np.zeros((P, P), np.float32)
    swap[np.arange(1, P, 2), np.arange(0, P, 2)] = -1.0
    swap[np.arange(0, P, 2), np.arange(1, P, 2)] = 1.0
    c["swap"] = swap
    c["strictly_before"] = (i[:, None] < i[None, :]).astype(np.float32)
    c["head_block"] = (i[:, None] // 8 == i[None, :] // 8).astype(np.float32)
    c["head_of_4"] = (((i[:, None] // 8) % 4) == np.arange(4)[None, :]).astype(np.float32)
    before = np.arange(SEQ)[None, None, :] < (np.arange(TPB)[None, :, None] * P + i[:, None, None])
    c["before"] = before.astype(np.float32)
    c["expert_no"] = np.tile(np.arange(NE, dtype=np.float32), (P, NT, 1))
    return c


def local_first_key(t):
    return 0 if t == 0 else t * P - WINDOW


def local_width(t):
    return (t + 1) * P - local_first_key(t)


@contextmanager
def signals(nc, names):
    with ExitStack() as c:
        s = [c.enter_context(nc.semaphore(n)) for n in names]

        def zero():
            numbers = sorted(x.num for x in s)
            starts = [n for n in numbers if n - 1 not in numbers]
            for first in starts:
                end = first
                while end in numbers:
                    end += 1
                nc.sync.sem_clear(range(first, end))
            nc.all_engine_barrier(sem_only=True)

        zero()
        yield s, zero


def chain(eng, sem):
    n = [0]

    def after(ins):
        n[0] += 1
        ins.then_inc(sem, 1)
        eng.wait_ge(sem, n[0])

    return after


def slots_before(slots, slot):
    low, high = 0, len(slots)
    while low < high:
        middle = (low + high) // 2
        low, high = (middle + 1, high) if slots[middle] < slot else (low, middle)
    return low


class Signals:

    def __init__(self, sem, when):
        self.sem, self.when, self.start, self.sent = sem, {n: sorted(w) for n, w in when.items()}, 0, {}

    def begin(self, start):
        self.start, self.sent = start, {}

    def end(self, stop):
        for n, slots in self.when.items():
            due = slots_before(slots, stop) - slots_before(slots, self.start)
            assert self.sent.get(n, 0) == due, (n, self.start, self.sent.get(n, 0), due)

    def wait(self, eng, name, count):
        here = count - slots_before(self.when[name], self.start)
        if here > 0:
            eng.wait_ge(self.sem[name], here)

    def done(self, ins, name):
        self.sent[name] = self.sent.get(name, 0) + 1
        ins.then_inc(self.sem[name], 1)


def run_windows(nc, sig, zero, emit, last_slot):
    first = 3 * 16
    span = LOOP_WINDOWS * 16
    turns = (NB - 1 - 3) // LOOP_WINDOWS
    rest = first + turns * span

    def part(start, stop, shift):
        sig.begin(start)
        with nc.Block() as block:
            emit(block, range(start, stop), shift)
        sig.end(stop)
        zero()

    part(0, first, 0)
    with nc.Fori(0, turns) as turn:
        part(first, first + span, turn * LOOP_WINDOWS)
    part(rest, last_slot, 0)


def rsqrt(nc, after, out, x, tmp):
    after(nc.vector.tensor_scalar(tmp.bitcast(I32), x.bitcast(I32), 1, None, ALU.logical_shift_right))
    after(nc.vector.tensor_scalar(out.bitcast(I32), tmp.bitcast(I32), -1.0, float(0x5F3759DF), ALU.mult, ALU.add))
    after(nc.vector.tensor_scalar(x, x, -0.5, None, ALU.mult))
    for _ in range(3):
        after(nc.vector.tensor_tensor(tmp, out, out, ALU.mult))
        after(nc.vector.tensor_tensor(tmp, tmp, x, ALU.mult))
        after(nc.vector.scalar_tensor_tensor(out=out, in0=tmp, scalar=1.5, in1=out, op0=ALU.add, op1=ALU.mult))


class Core:

    def __init__(self, nc, dram, ctx):
        self.nc, self.dram, self.stage = nc, dram, 0

        def sb(name, shape, dt=F32):
            return ctx.enter_context(nc.sbuf_tensor(name, shape, dt))

        self.x = sb("x_rows", [P, NT, P])
        self.xn = sb("xn_rows", [P, NT, P])
        self.xnt = sb("xn_cols", [P, TOK])
        self.s = sb("s_rows", [P, NT, P])
        self.y = sb("y_rows", [P, NT, P])
        self.ident = sb("ident", [P, P])
        self.bank = [ctx.enter_context(nc.psum_tensor(f"bank{i}", [P, 512], F32)) for i in range(8)]

    def name(self, base):
        return f"{base}_{self.stage}"


def load(core, pairs):
    nc = core.nc
    with signals(nc, ["loaded"]) as ((loaded,), zero):
        with nc.Block() as block:
            @block.sync
            def _(sp):
                for dst, src in pairs:
                    sp.dma_start(dst, src).then_inc(loaded, 16)
                sp.wait_ge(loaded, 16 * len(pairs))
        zero()


def column(ap):
    return ap.rearrange("(p a) -> p a", a=1)


def spread(ap):
    return ap.rearrange("(a n) -> a n", a=1).to_broadcast([P, ap.shape[0]])


def normalise_rows(nc, after, x_tiles, out_tiles, stats, mv, rstd, tmp, eps):
    n = len(x_tiles)
    for j in range(n):
        last = nc.vector.bn_stats(stats[:, j, :], x_tiles[j])
    after(last)
    return normalise_by(nc, after, x_tiles, out_tiles, stats, mv, rstd, tmp, eps)


def normalise_by(nc, after, x_tiles, out_tiles, stats, mv, rstd, tmp, eps):
    n = len(x_tiles)
    for j in range(n):
        last = nc.vector.bn_aggr(mv[:, j, :], stats[:, j, :])
    after(last)
    after(nc.vector.tensor_scalar(mv[:, 0:n, 1], mv[:, 0:n, 1], eps, None, ALU.add))
    rsqrt(nc, after, rstd[:, 0:n], mv[:, 0:n, 1], tmp[:, 0:n])
    return [nc.vector.tensor_scalar(out_tiles[j], x_tiles[j], mv[:, j, 0:1], rstd[:, j:j + 1], ALU.subtract, ALU.mult)
            for j in range(n)]


def layer_norm_stage(core):
    nc, bank, G = core.nc, core.bank, 4
    with ExitStack() as ctx:
        stats = ctx.enter_context(nc.sbuf_tensor(core.name("ln_stats"), [P, NT, 6], F32))
        mv = ctx.enter_context(nc.sbuf_tensor(core.name("ln_mv"), [P, NT, 2], F32))
        rstd = ctx.enter_context(nc.sbuf_tensor(core.name("ln_rstd"), [P, NT], F32))
        tmp = ctx.enter_context(nc.sbuf_tensor(core.name("ln_tmp"), [P, NT], F32))
        (dve_step, rows_ready, turned, copied), zero = ctx.enter_context(
            signals(nc, [core.name(n) for n in ("ln_dve_step", "ln_rows_ready", "ln_turned", "ln_copied")]))
        with nc.Block() as block:
            @block.vector
            def _(dve):
                after = chain(dve, dve_step)
                tiles = [core.x[:, j, :] for j in range(NT)]
                for ins in normalise_rows(nc, after, tiles, [core.xn[:, j, :] for j in range(NT)], stats, mv, rstd, tmp, 1e-5):
                    ins.then_inc(rows_ready, 1)

            @block.tensor
            def _(pe):
                for j in range(NT):
                    pe.wait_ge(rows_ready, j + 1)
                    if j % G == 0 and j >= 2 * G:
                        pe.wait_ge(copied, j // G - 1)
                    ins = nc.tensor.transpose(bank[j // G % 2][:, (j % G) * P:(j % G + 1) * P], core.xn[:, j, :], core.ident[:, :])
                    if j % G == G - 1:
                        ins.then_inc(turned, 1)

            @block.scalar
            def _(act):
                for g in range(NT // G):
                    act.wait_ge(turned, g + 1)
                    nc.scalar.copy(core.xnt[:, g * G * P:(g + 1) * G * P], bank[g % 2][:, :]).then_inc(copied, 1)
        zero()


def layer_norm_of_branch(core, eps, gamma, beta):
    nc = core.nc
    with ExitStack() as ctx:
        stats = ctx.enter_context(nc.sbuf_tensor(core.name("bn_stats"), [P, NT, 6], F32))
        mv = ctx.enter_context(nc.sbuf_tensor(core.name("bn_mv"), [P, NT, 2], F32))
        rstd = ctx.enter_context(nc.sbuf_tensor(core.name("bn_rstd"), [P, NT], F32))
        tmp = ctx.enter_context(nc.sbuf_tensor(core.name("bn_tmp"), [P, NT], F32))
        (dve_step, rows_ready, scaled, pool_step, stored), zero = ctx.enter_context(
            signals(nc, [core.name(n) for n in ("bn_dve_step", "bn_rows_ready", "bn_scaled", "bn_pool_step", "bn_stored")]))
        half = NT // 2
        wide = lambda v: v.rearrange("p (a c) -> p a c", a=1).to_broadcast([P, half, P])
        with nc.Block() as block:
            @block.vector
            def _(dve):
                after = chain(dve, dve_step)
                tiles = [core.s[:, j, :] for j in range(NT)]
                for ins in normalise_rows(nc, after, tiles, tiles, stats, mv, rstd, tmp, eps):
                    ins.then_inc(rows_ready, 1)
                dve.wait_ge(rows_ready, NT)
                nc.vector.tensor_tensor(core.s[:, half:NT, :], core.s[:, half:NT, :], wide(gamma), ALU.mult).then_inc(scaled, 1)
                dve.wait_ge(scaled, 1)
                nc.vector.tensor_tensor(core.s[:, half:NT, :], core.s[:, half:NT, :], wide(beta), ALU.add).then_inc(stored, 1)

            @block.gpsimd
            def _(pool):
                n = half // 2
                wide = lambda v: v.rearrange("p (a c) -> p a c", a=1).to_broadcast([P, n, P])
                for g in range(2):
                    rows = core.s[:, g * n:(g + 1) * n, :]
                    pool.wait_ge(rows_ready, (g + 1) * n)
                    nc.gpsimd.tensor_tensor(rows, rows, wide(gamma), ALU.mult).then_inc(pool_step, 1)
                    pool.wait_ge(pool_step, g + 1)
                    nc.gpsimd.tensor_tensor(rows, rows, wide(beta), ALU.add).then_inc(stored, 1)
        zero()


def combine_stage(core):
    nc, G = core.nc, 8
    with ExitStack() as ctx:
        (gated, multiplied, added), zero = ctx.enter_context(signals(nc, [core.name(n) for n in ("cb_gated", "cb_multiplied", "cb_added")]))
        groups = [slice(i * G, (i + 1) * G) for i in range(NT // G)]
        with nc.Block() as block:
            @block.scalar
            def _(act):
                for g in groups:
                    nc.scalar.activation(core.y[:, g, :], core.y[:, g, :], ACT.Silu).then_inc(gated, 1)

            @block.vector
            def _(dve):
                for i, g in enumerate(groups):
                    dve.wait_ge(gated, i + 1)
                    nc.vector.tensor_tensor(core.y[:, g, :], core.y[:, g, :], core.s[:, g, :], ALU.mult).then_inc(multiplied, 1)
                    dve.wait_ge(multiplied, i + 1)
                    nc.vector.tensor_tensor(core.x[:, g, :], core.y[:, g, :], core.x[:, g, :], ALU.add).then_inc(added, 1)
        zero()


def linear_attention_stage(core):
    nc, dram, bank = core.nc, core.dram, core.bank
    TURN, SLOTS, DIAG = 8, 8, P + 8
    with ExitStack() as ctx:
        def sb(name, shape, dt=F32):
            return ctx.enter_context(nc.sbuf_tensor("l0a_" + name, shape, dt))

        names = ("set_up", "x_ready", "qk_proj", "v_proj", "low_ready", "high_ready", "exp_ready", "qk_ready", "v_ready",
                 "kh_ready", "kr_done", "kr_ready", "kv_done", "state_ready", "kc_ready", "den_done", "den_added", "rec_ready",
                 "scored", "masked", "o_done", "ot_ready", "y_done", "stored")
        sems, zero = ctx.enter_context(signals(nc, ["l0a_" + n for n in names]))
        sem = dict(zip(names, sems))
        w = {n: sb(n, [P, P]) for n in ("wq", "wk", "wv", "wo")}
        bq, bk = sb("bq", [P, 1]), sb("bk", [P, 1])
        bv, bo = sb("bv", [P, P]), sb("bo", [P, P])
        upto, ones, block_, head4 = sb("upto", [P, P]), sb("ones", [P, P]), sb("block", [P, P]), sb("head4", [P, 4])
        xb, low, qk = sb("xb", [P, 2, SEQ]), sb("low", [P, 2, SEQ]), sb("qk", [P, 2, 2, SEQ])
        kh, kr = sb("kh", [P, 2, 4, SEQ]), sb("kr", [P, TPB, P])
        vz = sb("vz", [P, 2, TPB, HEADS * DIAG])
        state, kc, rec = sb("state", [P, 2, P]), sb("kc", [P, SEQ]), sb("rec", [P, 2, SEQ])
        st, ot = sb("st", [P, 2, 4, P]), sb("ot", [P, 2, SEQ])
        load(core, [(w[n][:, :], dram["L0_attn_" + n]) for n in w] +
             [(bq[:, :], column(dram["L0_attn_bq"])), (bk[:, :], column(dram["L0_attn_bk"])),
              (bv[:, :], spread(dram["L0_attn_bv"])), (bo[:, :], spread(dram["L0_attn_bo"])),
              (upto[:, :], dram["upto"]), (block_[:, :], dram["head_block"]), (head4[:, :], dram["head_of_4"])])
        with nc.Block() as block:
            @block.vector
            def _(dve):
                nc.vector.memset(vz[:, :, :, :], 0.0).then_inc(sem["set_up"], 1)
                nc.vector.memset(ones[:, :], 1.0).then_inc(sem["set_up"], 1)
        zero()
        by_head = lambda m, t: vz[:, m, t, :].rearrange("p (h c) -> p h c", c=DIAG)[:, :, 0:8]
        slots = range(SLOTS * (TURN + 1) + 5)

        def batch(slot, step):
            j, s = divmod(slot - step, SLOTS)
            return j if s == 0 and 0 <= j < TURN else None

        def unit(n):
            return n // SLOTS, n % SLOTS // 4, n % 4

        with nc.Fori(0, NB // TURN) as turn:
            with nc.Block() as block:
                @block.scalar
                def _(act):
                    for slot in slots:
                        if (j := batch(slot, 0)) is not None:
                            if j >= 2:
                                act.wait_ge(sem["v_proj"], j - 1)
                            nc.scalar.copy(xb[:, j % 2, :], core.xnt[:, bass.ds((turn * TURN + j) * SEQ, SEQ)]).then_inc(sem["x_ready"], 1)
                        if (j := batch(slot, 3)) is not None:
                            act.wait_ge(sem["low_ready"], 2 * (j + 1))
                            nc.scalar.activation(low[:, :, :], low[:, :, :], ACT.Exp).then_inc(sem["exp_ready"], 1)
                        if (j := batch(slot, 6)) is not None:
                            act.wait_ge(sem["kr_done"], j + 1)
                            if j >= 1:
                                act.wait_ge(sem["kv_done"], j)
                            nc.scalar.copy(kr[:, :, :], bank[1][:, SEQ:2 * SEQ].rearrange("p (t c) -> p t c", t=TPB)).then_inc(sem["kr_ready"], 1)

                @block.gpsimd
                def _(pool):
                    for j in range(TURN):
                        pool.wait_ge(sem["qk_ready"], j + 1)
                        if j >= 2:
                            pool.wait_ge(sem["scored"], SLOTS * (j - 1))
                        for i in range(4):
                            nc.gpsimd.tensor_scalar(kh[:, j % 2, i, :], qk[:, j % 2, 1, :], head4[:, i:i + 1], None,
                                                    ALU.mult).then_inc(sem["kh_ready"], 1)

                @block.tensor
                def _(pe):
                    for slot in slots:
                        if 0 <= (n := slot - 10) < SLOTS * TURN:
                            (j, t, g), to = unit(n), bank[6 + n // SLOTS % 2]
                            if n % SLOTS == 0 and j >= 2:
                                pe.wait_ge(sem["stored"], j - 1)
                            if t == 1 and g == 0:
                                pe.wait_ge(sem["state_ready"], j + 1)
                                nc.tensor.matmul(to[:, P:2 * P], state[:, j % 2, :], qk[:, j % 2, 0, P:SEQ], start=True, stop=False)
                            pe.wait_ge(sem["masked"], n + 1)
                            for i in range(4):
                                h = 4 * g + i
                                last = nc.tensor.matmul(to[:, t * P:(t + 1) * P], vz[:, j % 2, t, h * P:(h + 1) * P], st[:, n % 2, i, :],
                                                        start=(t == 0 and h == 0), stop=(h == HEADS - 1))
                            last.then_inc(sem["o_done"], 1)
                        if (j := batch(slot, 1)) is not None:
                            pe.wait_ge(sem["x_ready"], j + 1)
                            if j >= 1:
                                pe.wait_ge(sem["high_ready"], 2 * j)
                                pe.wait_ge(sem["kr_ready"], j)
                            for i, n in enumerate(("wq", "wk")):
                                last = nc.tensor.matmul(bank[0][:, i * SEQ:(i + 1) * SEQ], w[n][:, :], xb[:, j % 2, :], start=True, stop=True)
                            last.then_inc(sem["qk_proj"], 1)
                            for t in range(TPB):
                                last = nc.tensor.matmul(bank[1][:, t * P:(t + 1) * P], xb[:, j % 2, t * P:(t + 1) * P], w["wv"][:, :],
                                                        start=True, stop=True)
                            last.then_inc(sem["v_proj"], 1)
                        if (j := batch(slot, 5)) is not None:
                            pe.wait_ge(sem["qk_ready"], j + 1)
                            pe.wait_ge(sem["v_ready"], j + 1)
                            for t in range(TPB):
                                last = nc.tensor.transpose(bank[1][:, SEQ + t * P:SEQ + (t + 1) * P], qk[:, j % 2, 1, t * P:(t + 1) * P],
                                                           core.ident[:, :])
                            last.then_inc(sem["kr_done"], 1)
                        if (j := batch(slot, 7)) is not None:
                            pe.wait_ge(sem["kr_ready"], j + 1)
                            if j >= 1:
                                pe.wait_ge(sem["kc_ready"], j)
                            nc.tensor.matmul(bank[2][:, 0:P], kr[:, 0, :], by_head(j % 2, 0), start=True, stop=True)
                            nc.tensor.matmul(bank[2][:, P:2 * P], kr[:, 0, :], upto[:, :], start=True, stop=True)
                            nc.tensor.matmul(bank[2][:, 2 * P:3 * P], kr[:, 0, :], ones[:, :], start=True, stop=False)
                            nc.tensor.matmul(bank[2][:, 2 * P:3 * P], kr[:, 1, :], upto[:, :], start=False,
                                             stop=True).then_inc(sem["kv_done"], 1)
                        if (j := batch(slot, 8)) is not None:
                            pe.wait_ge(sem["kc_ready"], j + 1)
                            if j >= 1:
                                pe.wait_ge(sem["den_added"], j)
                            nc.tensor.matmul(bank[3][:, 0:SEQ], block_[:, :], kc[:, :], start=True, stop=True).then_inc(sem["den_done"], 1)
                            pe.wait_ge(sem["kh_ready"], 4 * (j + 1))
                        if (j := batch(slot, 19)) is not None:
                            pe.wait_ge(sem["ot_ready"], j + 1)
                            for t in range(TPB):
                                last = nc.tensor.matmul(bank[6 + j % 2][:, SEQ + t * P:SEQ + (t + 1) * P], ot[:, j % 2, t * P:(t + 1) * P],
                                                        w["wo"][:, :], start=True, stop=True)
                            last.then_inc(sem["y_done"], 1)
                        if 0 <= (n := slot - 8) < SLOTS * TURN:
                            j, t, g = unit(n)
                            if n >= 2:
                                pe.wait_ge(sem["masked"], n - 1)
                            for i in range(4):
                                last = nc.tensor.matmul(bank[4 + n % 2][:, i * P:(i + 1) * P],
                                                        kh[32 * g:32 * g + 32, j % 2, i, t * P:(t + 1) * P],
                                                        qk[32 * g:32 * g + 32, j % 2, 0, t * P:(t + 1) * P], start=True, stop=True)
                            last.then_inc(sem["scored"], 1)

                @block.vector
                def _(dve):
                    for slot in slots:
                        if 0 <= (n := slot - 9) < SLOTS * TURN:
                            dve.wait_ge(sem["scored"], n + 1)
                            if n >= 2:
                                dve.wait_ge(sem["o_done"], n - 1)
                            nc.vector.tensor_tensor(st[:, n % 2, :, :], bank[4 + n % 2][:, :].rearrange("p (i q) -> p i q", i=4),
                                                    upto[:, None, :].to_broadcast([P, 4, P]), ALU.mult).then_inc(sem["masked"], 1)
                        if (j := batch(slot, 2)) is not None:
                            dve.wait_ge(sem["qk_proj"], j + 1)
                            if j >= 1:
                                dve.wait_ge(sem["qk_ready"], j)
                            if j >= 2:
                                dve.wait_ge(sem["o_done"], SLOTS * (j - 1))
                                dve.wait_ge(sem["kh_ready"], 4 * (j - 1))
                            for n, bias in enumerate((bq, bk)):
                                pre = bank[0][:, n * SEQ:(n + 1) * SEQ]
                                nc.vector.tensor_scalar(low[:, n, :], pre, bias[:, 0:1], 0.0, ALU.add, ALU.min).then_inc(sem["low_ready"], 1)
                            for n, bias in enumerate((bq, bk)):
                                pre = bank[0][:, n * SEQ:(n + 1) * SEQ]
                                nc.vector.tensor_scalar(qk[:, j % 2, n, :], pre, bias[:, 0:1], 0.0, ALU.add, ALU.max).then_inc(sem["high_ready"], 1)
                        if (j := batch(slot, 3)) is not None:
                            dve.wait_ge(sem["v_proj"], j + 1)
                            for t in range(TPB):
                                last = nc.vector.tensor_tensor(
                                    by_head(j % 2, t), bank[1][:, t * P:(t + 1) * P].rearrange("p (h d) -> p h d", d=8),
                                    bv[:, :].rearrange("p (h d) -> p h d", d=8), ALU.add)
                            last.then_inc(sem["v_ready"], 1)
                        if (j := batch(slot, 4)) is not None:
                            dve.wait_ge(sem["exp_ready"], j + 1)
                            dve.wait_ge(sem["high_ready"], 2 * (j + 1))
                            nc.vector.tensor_tensor(qk[:, j % 2, :, :], qk[:, j % 2, :, :], low[:, :, :], ALU.add).then_inc(sem["qk_ready"], 1)
                        if (j := batch(slot, 7)) is not None:
                            dve.wait_ge(sem["kv_done"], j + 1)
                            dve.wait_ge(sem["qk_ready"], j + 1)
                            if j >= 1:
                                dve.wait_ge(sem["den_done"], j)
                            nc.vector.tensor_tensor(state[:, j % 2, :], bank[2][:, 0:P], block_[:, :], ALU.mult).then_inc(sem["state_ready"], 1)
                            nc.vector.tensor_tensor(kc[:, :], bank[2][:, P:3 * P], qk[:, j % 2, 0, :], ALU.mult).then_inc(sem["kc_ready"], 1)
                        if (j := batch(slot, 9)) is not None:
                            dve.wait_ge(sem["den_done"], j + 1)
                            if j >= 2:
                                dve.wait_ge(sem["ot_ready"], j - 1)
                            nc.vector.tensor_scalar(rec[:, j % 2, :], bank[3][:, 0:SEQ], 1e-6, None, ALU.add).then_inc(sem["den_added"], 1)
                            dve.wait_ge(sem["den_added"], j + 1)
                            nc.vector.reciprocal(rec[:, j % 2, :], rec[:, j % 2, :]).then_inc(sem["rec_ready"], 1)
                        if (j := batch(slot, 18)) is not None:
                            dve.wait_ge(sem["o_done"], SLOTS * (j + 1))
                            dve.wait_ge(sem["rec_ready"], j + 1)
                            if j >= 2:
                                dve.wait_ge(sem["y_done"], j - 1)
                            nc.vector.tensor_tensor(ot[:, j % 2, :], bank[6 + j % 2][:, 0:SEQ], rec[:, j % 2, :], ALU.mult).then_inc(sem["ot_ready"], 1)
                        if (j := batch(slot, 20)) is not None:
                            dve.wait_ge(sem["y_done"], j + 1)
                            nc.vector.tensor_tensor(
                                core.s[:, bass.ds((turn * TURN + j) * TPB, TPB), :],
                                bank[6 + j % 2][:, SEQ:2 * SEQ].rearrange("p (t c) -> p t c", t=TPB),
                                bo[:, None, :].to_broadcast([P, TPB, P]), ALU.add).then_inc(sem["stored"], 1)
            zero()


class Softmax:

    UNITS = TPB * HEADS // 2

    def __init__(self, core, sb, dh, local, mask_name, scale, stage_turns, qt=None, v=None):
        self.core, self.dh, self.local, self.scale = core, dh, local, scale
        self.parts = TPB * HEADS * dh // 512 if dh == 64 else TPB
        self.part_units = self.UNITS // self.parts
        self.chunks = HEADS * dh // P
        groups = HEADS // 2 if dh == 64 else 4
        self.qt = qt if qt is not None else sb("qt", [P, 2, groups, SEQ])
        self.kt = sb("kt", [P, 2, groups if dh == 64 else 1, SEQ])
        if v is not None:
            self.v = v
        elif dh == 64:
            self.v = sb("v", [P, 2, TPB, HEADS * dh])
        else:
            self.v = sb("v", [P, 2, TPB, HEADS * (P + dh)])
        self.wo = sb("wo", [P, self.chunks, P])
        self.mask = sb("mask", [P, TPB, SEQ])
        self.sm = sb("sm", [P, 2, 2, SEQ])
        self.p = sb("p", [P, 4, 2, SEQ])
        self.pt = sb("pt", [P, 2, 4, P])
        self.mx, self.nb, self.sums, self.rec = (sb(n, [P, 2, TPB * HEADS]) for n in ("mx", "nb", "sums", "rec"))
        self.ot = sb("ot", [P, 2, self.chunks, P])
        self.factor = self.nfactor = None
        self.mask_src = core.dram[mask_name]
        self.plan = [(16 * k + s, "stage", k, i) for k in range(NB) for i, s in enumerate(stage_turns)]
        self.plan += [(16 * (k + 1) + (t + 1) * HEADS // 2 + 9, "y", k, t) for k in range(NB) for t in range(TPB)]
        self.plan.sort()
        slots = [use[0] for use in self.plan]
        assert len(set(slots)) == len(slots)
        self.number = {use[1:]: n for n, use in enumerate(self.plan)}
        self.at = {use[0]: use[1:] for use in self.plan}
        self.last_slot = slots[-1] + 2
        ends = [16 + g for g in range(NB * self.UNITS) if (g + 1) % self.part_units == 0]
        units = range(16, 16 + NB * self.UNITS)
        after = lambda lag, n=1: [u + lag for u in units for _ in range(n)]
        self.when = {"scored": after(0), "masked": after(1, 2), "bias_ready": after(1), "p_ready": after(1, 2),
                     "rec_ready": after(2), "p_divided": after(2), "pt_done": after(4), "pt_ready": after(5),
                     "o_ready": after(6), "ot_dve": [u + 9 for n, u in enumerate(ends) if n % 2 == 0 or not local],
                     "bank7_full": slots, "bank7_free": [u + 1 for u in slots]}
        if local:
            self.when["ot_act"] = [u + 9 for u in ends[1::2]]

    def full(self, eng, kind, k, i):
        self.sig.wait(eng, "bank7_full", self.number[kind, k, i] + 1)

    def take_bank7(self, pe, kind, k, i):
        self.sig.wait(pe, "bank7_free", self.number[kind, k, i])

    def copied(self, pe, parts):
        if self.local:
            self.sig.wait(pe, "ot_dve", (parts + 1) // 2)
            self.sig.wait(pe, "ot_act", parts // 2)
        else:
            self.sig.wait(pe, "ot_dve", parts)

    def first(self, t):
        return local_first_key(t) if self.local else 0

    def width(self, t):
        return local_width(t) if self.local else (t + 1) * P

    def key_chunks(self, t):
        if t == 0:
            return [(0, P, 0, 0)]
        if self.local:
            return [(WINDOW, P, 1, 0), (0, WINDOW, 0, P - WINDOW)]
        return [(0, P, 0, 0), (P, P, 1, 0)]

    def unit(self, g):
        if not 0 <= g < NB * self.UNITS:
            return None
        u = g % self.UNITS
        return g // self.UNITS, u // (HEADS // 2), u % (HEADS // 2)

    def scores(self, pe, g):
        if not self.unit(g):
            return
        nc, sig, bank = self.core.nc, self.sig, self.core.bank
        k, t, hp = self.unit(g)
        sig.wait(pe, "masked", 2 * g)
        w, k0 = self.width(t), self.first(t)
        for i in range(2):
            h = 2 * hp + i
            if self.dh == 64:
                rows, group, key_group = slice(64 * i, 64 * i + 64), hp, hp
            else:
                rows, group, key_group = slice(32 * (h // 4), 32 * (h // 4) + 32), h % 4, 0
            last = nc.tensor.matmul(bank[i][:, 0:w], self.qt[rows, k % 2, group, t * P:(t + 1) * P],
                                    self.kt[rows, k % 2, key_group, k0:k0 + w], start=True, stop=True)
        sig.done(last, "scored")

    def turn(self, pe, g):
        if not self.unit(g):
            return
        nc, core, sig = self.core.nc, self.core, self.sig
        k, t, hp = self.unit(g)
        sig.wait(pe, "p_divided", g + 1)
        sig.wait(pe, "pt_ready", g)
        for c, (c0, n, _, _) in enumerate(self.key_chunks(t)):
            for i in range(2):
                last = nc.tensor.transpose(core.bank[2][0:n, (2 * c + i) * P:(2 * c + i) * P + n],
                                           self.p[0:n, g % 4, i, c0:c0 + n], core.ident[0:n, 0:n])
        sig.done(last, "pt_done")

    def values(self, pe, g):
        if not self.unit(g):
            return
        nc, sig, bank = self.core.nc, self.sig, self.core.bank
        k, t, hp = self.unit(g)
        sig.wait(pe, "pt_ready", g + 1)
        part, place = g // self.part_units, g % self.part_units
        if place == 0:
            self.copied(pe, part - 1)
        to = bank[3 + part % 2]
        for i in range(2):
            h = 2 * hp + i
            for c, (_, n, vt, p0) in enumerate(self.key_chunks(t)):
                if self.dh == 64:
                    last = nc.tensor.matmul(to[64 * i:64 * i + 64, place * P:place * P + n],
                                            self.v[p0:p0 + n, k % 2, vt, h * 64:(h + 1) * 64],
                                            self.pt[p0:p0 + n, g % 2, 2 * c + i, 0:n], start=(c == 0), stop=(self.local or c == t),
                                            skip_group_check=(n < P))
                else:
                    last = nc.tensor.matmul(to[:, 0:P], self.v[:, k % 2, vt, h * P:(h + 1) * P], self.pt[:, g % 2, 2 * c + i, :],
                                            start=(h == 0 and c == 0), stop=(h == HEADS - 1 and c == t))
        sig.done(last, "o_ready")

    def project_out(self, pe, k, t):
        nc, core, sig = self.core.nc, self.core, self.sig
        self.take_bank7(pe, "y", k, t)
        self.copied(pe, k * self.parts + (t + 1) * self.parts // TPB)
        for c in range(self.chunks):
            last = nc.tensor.matmul(core.bank[7][:, 0:P], self.ot[:, t, c, :], self.wo[:, c, :],
                                    start=(c == 0), stop=(c == self.chunks - 1))
        sig.done(last, "bank7_full")

    def mask_and_max(self, dve, g):
        if not self.unit(g):
            return
        nc, sig, bank = self.core.nc, self.sig, self.core.bank
        k, t, hp = self.unit(g)
        w = self.width(t)
        sig.wait(dve, "scored", g + 1)
        sig.wait(dve, "p_ready", 2 * (g - 1))
        for i in range(2):
            col = t * HEADS + 2 * hp + i
            ins = nc.vector.tensor_tensor_reduce(self.sm[:, g % 2, i, 0:w], bank[i][:, 0:w], self.mask[:, t, 0:w], 1.0,
                                                 LOWEST, ALU.add, ALU.max, self.mx[:, k % 2, col:col + 1])
            sig.done(ins, "masked")
        sig.wait(dve, "masked", 2 * (g + 1))
        c = slice(t * HEADS + 2 * hp, t * HEADS + 2 * hp + 2)
        if self.nfactor is not None:
            ins = nc.vector.tensor_tensor(self.nb[:, k % 2, c], self.mx[:, k % 2, c], self.nfactor[:, k % 2, c], ALU.mult)
        else:
            ins = nc.vector.tensor_scalar(self.nb[:, k % 2, c], self.mx[:, k % 2, c], -self.scale, None, ALU.mult)
        sig.done(ins, "bias_ready")

    def reciprocals(self, dve, g):
        if not self.unit(g):
            return
        k, t, hp = self.unit(g)
        c = slice(t * HEADS + 2 * hp, t * HEADS + 2 * hp + 2)
        self.sig.wait(dve, "p_ready", 2 * (g + 1))
        self.sig.done(self.core.nc.vector.reciprocal(self.rec[:, k % 2, c], self.sums[:, k % 2, c]), "rec_ready")

    def divide(self, eng, g):
        if not self.unit(g):
            return
        nc, sig = self.core.nc, self.sig
        k, t, hp = self.unit(g)
        c, w = t * HEADS + 2 * hp, self.width(t)
        sig.wait(eng, "rec_ready", g + 1)
        if eng is nc.gpsimd:
            sig.wait(eng, "p_ready", 2 * (g + 1))
            p = self.p[:, g % 4, :, 0:w]
            last = eng.tensor_tensor(p, p, self.rec[:, k % 2, c:c + 2].rearrange("p (h a) -> p h a", a=1).to_broadcast([P, 2, w]),
                                     ALU.mult)
        else:
            for i in range(2):
                p = self.p[:, g % 4, i, 0:w]
                last = eng.tensor_scalar(p, p, self.rec[:, k % 2, c + i:c + i + 1], None, ALU.mult)
        sig.done(last, "p_divided")

    def copy_columns(self, eng, copy, g):
        k, n = g // self.UNITS, g // self.part_units
        nc, sig = self.core.nc, self.sig
        act = self.local and n % 2 == 1
        if not self.unit(g) or (g + 1) % self.part_units or act != (eng is nc.scalar):
            return
        t = n % self.parts // (self.parts // TPB)
        sig.wait(eng, "o_ready", g + 1)
        if k >= 1:
            self.full(eng, "y", k - 1, t)
        m = self.chunks * TPB // self.parts
        c0 = n * m % self.chunks
        sig.done(copy(self.ot[:, t, c0:c0 + m, :], self.core.bank[3 + n % 2][:, 0:m * P].rearrange("p (c q) -> p c q", c=m)),
                 "ot_act" if act else "ot_dve")

    def exps(self, act, g):
        if not self.unit(g):
            return
        nc, sig = self.core.nc, self.sig
        k, t, hp = self.unit(g)
        w = self.width(t)
        sig.wait(act, "bias_ready", g + 1)
        sig.wait(act, "pt_done", g - 3)
        for i in range(2):
            col = t * HEADS + 2 * hp + i
            scale = self.factor[:, k % 2, col:col + 1] if self.factor is not None else self.scale
            ins = nc.scalar.activation(self.p[:, g % 4, i, 0:w], self.sm[:, g % 2, i, 0:w], ACT.Exp,
                                       bias=self.nb[:, k % 2, col:col + 1], scale=scale,
                                       accum_out=self.sums[:, k % 2, col:col + 1])
            sig.done(ins, "p_ready")

    def copy_turned(self, act, g):
        if not self.unit(g):
            return
        nc, sig, bank = self.core.nc, self.sig, self.core.bank
        k, t, hp = self.unit(g)
        sig.wait(act, "pt_done", g + 1)
        sig.wait(act, "o_ready", g - 1)
        kc = self.key_chunks(t)
        if all(n == P for _, n, _, _ in kc):
            m = 2 * len(kc)
            last = nc.scalar.copy(self.pt[:, g % 2, 0:m, :], bank[2][:, 0:m * P].rearrange("p (m q) -> p m q", m=m))
        else:
            for c, (_, n, _, p0) in enumerate(kc):
                last = nc.scalar.copy(self.pt[p0:p0 + n, g % 2, 2 * c:2 * c + 2, 0:n],
                                      bank[2][0:n, 2 * c * P:(2 * c + 2) * P].rearrange("p (m q) -> p m q", m=2)[:, :, 0:n])
        sig.done(last, "pt_ready")


def local_attention_stage(core, l):
    nc, dram, bank = core.nc, core.dram, core.bank
    NCH = 3 * INNER // 512
    CH = TPB * NCH
    CHUNKS = [(8 * t + s, t, c) for t in range(TPB) for s, c in ((2, 0), (3, 4), (4, 1), (6, 2), (7, 5), (8, 3))]
    TURNS = (0, 8, 10, 13, 14, 18, 19, 21, 22)
    with ExitStack() as ctx:
        def sb(name, shape, dt=F32):
            return ctx.enter_context(nc.sbuf_tensor("loc_" + name, shape, dt))

        att = Softmax(core, sb, DH, True, "mask_local", None, TURNS,
                      qt=core.xn[:, :, :].rearrange("p t c -> p (t c)").rearrange("p (k g q) -> p k g q", k=2, g=HEADS // 2),
                      v=core.xnt[:, :].rearrange("p (k t c) -> p k t c", k=2, t=TPB))
        proj = [16 * k + slot for k in range(NB) for slot, _, _ in CHUNKS]
        chunk = lambda i: (i // CH,) + CHUNKS[i % CH][1:]
        qk = [i for i in range(NB * CH) if chunk(i)[2] < 4]
        qk_number = {i: n for n, i in enumerate(qk)}
        number_at = {slot: i for i, slot in enumerate(proj)}
        lasts = [proj[i] for i in qk if chunk(i)[2] == 3]
        yb_slot = [max(0, 16 * k - 3) for k in range(NB)]
        when = dict(att.when)
        when.update({
            "yb_ready": yb_slot,
            "xb_ready": [16 * k + 1 for k in range(NB) for _ in range(2)],
            "proj_done": proj,
            "squared": [proj[i] + 1 for i in qk],
            "turned": [proj[i] + 1 for i in qk],
            "summed": [proj[i] + 1 for i in qk],
            "rk_ready": [s + 2 for s in lasts for _ in range(2)],
            "v_act": [proj[i] + 1 for i in range(NB * CH) if chunk(i)[2] == 4],
            "v_dve": [proj[i] + 1 for i in range(NB * CH) if chunk(i)[2] == 5],
            "added": [proj[i] + 2 for i in qk],
            "final": [s + 3 for s in lasts for _ in range(2)],
            "stored": [use[0] + 1 for use in att.plan if use[1] == "y"],
        })
        names = tuple(when) + ("dve_step", "tables_loaded", "loaded")
        sems, zero = ctx.enter_context(signals(nc, ["loc_" + n for n in names]))
        sem = dict(zip(names, sems))
        sig = att.sig = Signals(sem, when)
        wqkv = sb("wqkv", [P, 3 * INNER])
        rope, qks = sb("rope", [P, TPB, 4, DH]), sb("qks", [P, 2, DH])
        yb, xb = sb("yb", [P, 2, TPB, P]), sb("xb", [P, 2, SEQ])
        a, b_ = sb("a", [P, TPB, 4, 512]), sb("b", [P, 2, 512])
        sq = sb("sq", [P, 2, 512])
        n2, rn, tmp = sb("n2", [P, TPB, 32]), sb("rn", [P, TPB, 32]), sb("tmp", [P, 32])
        att.factor, att.nfactor = sb("f", [P, 2, TPB * HEADS]), sb("nf", [P, 2, TPB * HEADS])
        tables = [(rope[:, :, :, :], dram["rope_local"]),
                  (qks[:, 0, :], dram["L0_ffn_q_scale"][bass.ds(l, 1), :].to_broadcast([P, DH])),
                  (qks[:, 1, :], dram["L0_ffn_k_scale"][bass.ds(l, 1), :].to_broadcast([P, DH]))]
        rest = [(wqkv[:, :], dram["L0_ffn_Wqkv"][bass.ds(l, 1), :, :].rearrange("a p n -> p (a n)")),
                (att.wo[:, :, :], dram["L0_ffn_Wo"][bass.ds(l, 1), :, :].rearrange("a (c p) n -> p (a c) n", p=P)),
                (att.mask[:, :, :], att.mask_src)]
        with nc.Block() as block:
            @block.sync
            def _(sp):
                for dst, src in tables:
                    sp.dma_start(dst, src).then_inc(sem["tables_loaded"], 16)
                for dst, src in rest:
                    sp.dma_start(dst, src).then_inc(sem["loaded"], 16)
                sp.wait_ge(sem["tables_loaded"], 16 * len(tables))
                sp.wait_ge(sem["loaded"], 16 * len(rest))

            @block.vector
            def _(dve):
                after = chain(dve, sem["dve_step"])
                dve.wait_ge(sem["tables_loaded"], 16 * len(tables))
                for n in range(2):
                    wide = qks[:, n, :].rearrange("p (a d) -> p a d", a=1).to_broadcast([P, TPB, DH])
                    after(nc.vector.tensor_tensor(rope[:, :, 2 * n, :], rope[:, :, 2 * n, :], wide, ALU.mult))
                    for half in range(2):
                        d, s = half * 32, 32 - half * 32
                        wide = qks[:, n, s:s + 32].rearrange("p (a d) -> p a d", a=1).to_broadcast([P, TPB, 32])
                        after(nc.vector.tensor_tensor(rope[:, :, 2 * n + 1, d:d + 32], rope[:, :, 2 * n + 1, d:d + 32],
                                                      wide, ALU.mult))
                after(nc.vector.memset(xb[64:128, :, 0:1], 0.0))
        zero()

        def left_bank(pe, i):
            if i < 0:
                return
            k, t, c = chunk(i)
            if c < 4:
                sig.wait(pe, "turned", qk_number[i] + 1)
            else:
                sig.wait(pe, "v_act" if c == 4 else "v_dve", k * TPB + t + 1)

        def copy_heads(copy, k, t, c):
            dst = att.qt if c < 2 else att.kt
            sig.done(copy(dst[:, k % 2, (c % 2) * 4:(c % 2) * 4 + 4, t * P:(t + 1) * P],
                          bank[7][:, :].rearrange("p (j q) -> p j q", j=4)), "bank7_free")

        def emit(block, slots, shift):
            @block.gpsimd
            def _(pool):
                for slot in slots:
                    att.divide(pool, slot - 18)
                    i = number_at.get(slot - 2)
                    if i is not None and chunk(i)[2] < 4:
                        (k, t, c), n = chunk(i), qk_number[i]
                        sig.wait(pool, "turned", n + 1)
                        sig.done(nc.gpsimd.tensor_tensor(a[:, t, c, :], a[:, t, c, :], b_[:, n % 2, :], ALU.add), "added")
                    i = number_at.get(slot - 3)
                    if i is not None and chunk(i)[2] == 3:
                        (k, t, _), n = chunk(i), qk_number[i]
                        sig.wait(pool, "added", n + 1)
                        sig.wait(pool, "rk_ready", (k * TPB + t) * 2 + 1)
                        for c in (2, 3):
                            k0 = 16 + (c - 2) * 8
                            ins = nc.gpsimd.tensor_tensor(
                                a[:, t, c, :].rearrange("p (h d) -> p h d", d=DH),
                                a[:, t, c, :].rearrange("p (h d) -> p h d", d=DH),
                                rn[:, t, k0:k0 + 8].rearrange("p (h a) -> p h a", a=1).to_broadcast([P, 8, DH]), ALU.mult)
                            sig.done(ins, "final")
                    if slot in yb_slot:
                        k = yb_slot.index(slot)
                        if k >= 2:
                            att.full(pool, "stage", k - 2, 0)
                        sig.done(nc.gpsimd.tensor_copy(yb[:, k % 2, :, :], core.y[:, bass.ds((shift + k) * TPB, TPB), :]),
                                 "yb_ready")

            @block.tensor
            def _(pe):
                for slot in slots:
                    i = number_at.get(slot)
                    if i is not None:
                        k, t, c = chunk(i)
                        if i % CH == 0:
                            sig.wait(pe, "xb_ready", 2 * (k + 1))
                        left_bank(pe, i - 2)
                        ins = nc.tensor.matmul(bank[5 + i % 2][:, :], xb[:, k % 2, t * P:(t + 1) * P], wqkv[:, c * 512:(c + 1) * 512],
                                               start=True, stop=True)
                        sig.done(ins, "proj_done")
                    att.scores(pe, slot - 16)
                    att.values(pe, slot - 22)
                    if slot in att.at:
                        kind, k, j = att.at[slot]
                        if kind == "y":
                            att.project_out(pe, k, j)
                        elif j == 0:
                            att.take_bank7(pe, kind, k, j)
                            sig.wait(pe, "yb_ready", k + 1)
                            for t in range(TPB):
                                last = nc.tensor.transpose(bank[7][:, t * P:(t + 1) * P], yb[:, k % 2, t, :], core.ident[:, :])
                            sig.done(last, "bank7_full")
                        else:
                            t, c = (j - 1) // 4, (j - 1) % 4
                            att.take_bank7(pe, kind, k, j)
                            if c < 2:
                                sig.wait(pe, "added", (k * TPB + t) * 4 + c + 1)
                            else:
                                sig.wait(pe, "final", (k * TPB + t) * 2 + c - 1)
                            for m in range(4):
                                last = nc.tensor.transpose(bank[7][:, m * P:(m + 1) * P], a[:, t, c, m * P:(m + 1) * P],
                                                           core.ident[:, :])
                            sig.done(last, "bank7_full")
                    att.turn(pe, slot - 20)

            @block.scalar
            def _(act):
                for slot in slots:
                    i = number_at.get(slot - 1)
                    if i is not None and chunk(i)[2] < 4:
                        n = qk_number[i]
                        sig.wait(act, "proj_done", i + 1)
                        sig.wait(act, "summed", n - 1)
                        sig.done(nc.scalar.activation(sq[:, n % 2, :], bank[5 + i % 2][:, :], ACT.Square), "squared")
                    elif i is not None and chunk(i)[2] == 4:
                        k, t, _ = chunk(i)
                        sig.wait(act, "proj_done", i + 1)
                        sig.done(nc.scalar.copy(att.v[:, k % 2, t, 0:512], bank[5 + i % 2][:, :]), "v_act")
                    kind, k, j = att.at.get(slot - 1, (None, 0, 0))
                    if kind == "stage" and j == 0:
                        att.full(act, kind, k, j)
                        sig.wait(act, "proj_done", CH * (k - 1))
                        sig.done(nc.scalar.copy(xb[0:64, k % 2, :], bank[7][0:64, 0:SEQ]), "xb_ready")
                        sig.done(nc.scalar.copy(xb[64:128, k % 2, 1:SEQ], bank[7][64:128, 0:SEQ - 1]), "xb_ready")
                        sig.wait(act, "xb_ready", 2 * (k + 1))
                        sig.done(nc.scalar.copy(spare[0:1, 0:1], core.ident[0:1, 0:1]), "bank7_free")
                    elif kind == "stage":
                        att.full(act, kind, k, j)
                        copy_heads(nc.scalar.copy, k, (j - 1) // 4, (j - 1) % 4)
                    att.copy_columns(act, nc.scalar.copy, slot - 25)
                    att.copy_turned(act, slot - 21)
                    att.exps(act, slot - 17)

            @block.vector
            def _(dve):
                after = chain(dve, sem["dve_step"])
                for slot in slots:
                    att.mask_and_max(dve, slot - 17)
                    kind, k, j = att.at.get(slot - 1, (None, 0, 0))
                    if kind == "y":
                        att.full(dve, kind, k, j)
                        row = core.y[:, bass.ds((shift + k) * TPB + j, 1), :]
                        sig.done(nc.vector.tensor_tensor(row, bank[7][:, 0:P].rearrange("p (a c) -> p a c", a=1), row, ALU.add),
                                 "stored")
                        sig.wait(dve, "stored", k * TPB + j + 1)
                        sig.done(nc.vector.tensor_copy(spare[0:1, 1:2], core.ident[0:1, 0:1]), "bank7_free")
                    i = number_at.get(slot - 1)
                    if i is not None:
                        k, t, c = chunk(i)
                        src_bank = bank[5 + i % 2]
                        if c < 4:
                            n, which = qk_number[i], c // 2
                            sig.wait(dve, "squared", n + 1)
                            sig.wait(dve, "added", n - 1)
                            if k >= 1:
                                att.full(dve, "stage", k - 1, 1 + t * 4 + c)
                            src = src_bank[:, :].rearrange("p (h d) -> p h d", d=DH)
                            cos = rope[:, t, 2 * which, :].rearrange("p (a d) -> p a d", a=1).to_broadcast([P, 8, DH])
                            nc.vector.tensor_tensor(a[:, t, c, :].rearrange("p (h d) -> p h d", d=DH), src, cos, ALU.mult)
                            halves = src_bank[:, :].rearrange("p (h s d) -> p h s d", s=2, d=32)[:, :, ::-1, :]
                            sin = rope[:, t, 2 * which + 1, :].rearrange("p (a s d) -> p a s d", a=1, s=2).to_broadcast([P, 8, 2, 32])
                            ins = nc.vector.tensor_tensor(b_[:, n % 2, :].rearrange("p (h s d) -> p h s d", s=2, d=32), halves,
                                                          sin, ALU.mult)
                            sig.done(ins, "turned")
                            ins = nc.vector.tensor_reduce(n2[:, t, c * 8:(c + 1) * 8],
                                                          sq[:, n % 2, :].rearrange("p (h d) -> p h d", d=DH), AX.X, ALU.add)
                            sig.done(ins, "summed")
                        elif c == 5:
                            sig.wait(dve, "proj_done", i + 1)
                            sig.done(nc.vector.tensor_copy(att.v[:, k % 2, t, 512:1024], src_bank[:, :]), "v_dve")
                    att.reciprocals(dve, slot - 18)
                    i = number_at.get(slot - 2)
                    if i is not None and chunk(i)[2] == 3:
                        k, t, _ = chunk(i)
                        tile = k * TPB + t
                        sig.wait(dve, "summed", 4 * (tile + 1))
                        sig.wait(dve, "final", 2 * (tile - 1))
                        after(nc.vector.tensor_scalar(n2[:, t, :], n2[:, t, :], 1e-24, None, ALU.max))
                        rsqrt(nc, after, rn[:, t, :], n2[:, t, :], tmp[:, :])
                        for f, scale in ((att.factor, QK_SCALE), (att.nfactor, -QK_SCALE)):
                            ins = nc.vector.tensor_scalar(f[:, k % 2, t * HEADS:(t + 1) * HEADS], rn[:, t, 0:16], scale, None,
                                                          ALU.mult)
                            sig.done(ins, "rk_ready")
                        sig.wait(dve, "rk_ready", 2 * (tile + 1))
                    att.copy_columns(dve, nc.vector.tensor_copy, slot - 25)

        spare = sb("spare", [1, 2])
        run_windows(nc, sig, zero, emit, att.last_slot)


def glu_stage(core, l):
    nc, dram, bank = core.nc, core.dram, core.bank
    rows, cols, G = core.xn, core.xnt, 4
    NGRP, GB = NT // G, G // TPB
    CH, TURN = len(HID_CHUNKS), 8
    with ExitStack() as ctx:
        def sb(name, shape, dt=F32):
            return ctx.enter_context(nc.sbuf_tensor("glu_" + name, shape, dt))

        names = ("loaded", "zeroed", "cols_done", "shifted", "rows_done", "rows_ready", "normalised", "turned", "biased", "xn_ready",
                 "hid_done", "gelu_ready", "h_ready", "y_done", "stored", "dve_step")
        sems, zero = ctx.enter_context(signals(nc, ["glu_" + n for n in names]))
        sem = dict(zip(names, sems))
        w1, w2 = sb("w1", [P, 2 * DIM_INNER]), sb("w2", [P, CH, P])
        b1, b2, gain, shift = sb("b1", [P, 2, CH]), sb("b2", [P, P]), sb("gain", [P, 1]), sb("shift", [P, 1])
        xs = sb("xs", [P, 2, GB, SEQ])
        gel, h = sb("gel", [P, CH, SEQ]), sb("h", [P, 2, CH, SEQ])
        stats, mv, rstd, tmp = sb("stats", [P, NT, 6]), sb("mv", [P, NT, 2]), sb("rstd", [P, NT]), sb("tmp", [P, NT])
        row = lambda name: dram["L0_ffn_" + name][bass.ds(l, 1), :]
        loads = ([(w1[:, :], dram["L0_ffn_W1"][bass.ds(l, 1), :, :].rearrange("a p n -> p (a n)")),
                  (b2[:, :], row("b2").to_broadcast([P, P])),
                  (gain[:, :], row("ln_g").rearrange("a p -> p a")), (shift[:, :], row("ln_b").rearrange("a p -> p a"))] +
                 [(w2[0:n, c, :], dram["L0_ffn_W2"][bass.ds(l, 1), c0:c0 + n, :].rearrange("a p n -> p (a n)"))
                  for c, (c0, n) in enumerate(HID_CHUNKS)] +
                 [(b1[0:n, g, c:c + 1], dram["L0_ffn_b1"][bass.ds(l, 1), g * DIM_INNER + c0:g * DIM_INNER + c0 + n].rearrange("a p -> p a"))
                  for c, (c0, n) in enumerate(HID_CHUNKS) for g in range(2)])
        tiles = lambda ap: ap.rearrange("p (t c) -> p t c", c=P)
        with nc.Block() as block:
            @block.sync
            def _(sp):
                for dst, src in loads:
                    sp.dma_start(dst, src).then_inc(sem["loaded"], 16)
                sp.wait_ge(sem["loaded"], 16 * len(loads))

            @block.tensor
            def _(pe):
                for g in range(NGRP + 1):
                    if g < NGRP:
                        if g >= 2:
                            pe.wait_ge(sem["shifted"], 2 * (g - 1))
                        for i in range(G):
                            last = nc.tensor.transpose(bank[g % 2][:, i * P:(i + 1) * P], core.y[:, g * G + i, :], core.ident[:, :])
                        last.then_inc(sem["cols_done"], 1)
                    if g >= 1:
                        pe.wait_ge(sem["shifted"], 2 * g)
                        if g >= 3:
                            pe.wait_ge(sem["rows_ready"], g - 2)
                        for i in range(G):
                            b, t = i // TPB, i % TPB
                            last = nc.tensor.transpose(bank[2 + (g - 1) % 2][:, i * P:(i + 1) * P],
                                                       xs[:, (g - 1) % 2, b, t * P:(t + 1) * P], core.ident[:, :])
                        last.then_inc(sem["rows_done"], 1)
                for g in range(NGRP):
                    pe.wait_ge(sem["normalised"], G * (g + 1))
                    if g >= 2:
                        pe.wait_ge(sem["xn_ready"], g - 1)
                    for i in range(G):
                        last = nc.tensor.transpose(bank[4 + g % 2][:, i * P:(i + 1) * P], rows[:, g * G + i, :], core.ident[:, :])
                    last.then_inc(sem["turned"], 1)

            @block.scalar
            def _(act):
                act.wait_ge(sem["zeroed"], 1)
                for g in range(NGRP + 1):
                    if g < NGRP:
                        src = bank[g % 2][:, :].rearrange("p (b q) -> p b q", b=GB)
                        act.wait_ge(sem["cols_done"], g + 1)
                        if g >= 2:
                            act.wait_ge(sem["rows_done"], g - 1)
                        nc.scalar.copy(xs[0:64, g % 2, :, :], src[0:64, :, :]).then_inc(sem["shifted"], 1)
                        nc.scalar.copy(xs[64:128, g % 2, :, 1:SEQ], src[64:128, :, 0:SEQ - 1]).then_inc(sem["shifted"], 1)
                    if g >= 1:
                        act.wait_ge(sem["rows_done"], g)
                        nc.scalar.copy(rows[:, (g - 1) * G:g * G, :], tiles(bank[2 + (g - 1) % 2][:, :])).then_inc(sem["rows_ready"], 1)
                act.wait_ge(sem["loaded"], 16 * len(loads))
                for g in range(NGRP):
                    act.wait_ge(sem["turned"], g + 1)
                    nc.scalar.activation(cols[:, g * G * P:(g + 1) * G * P], bank[4 + g % 2][:, :], ACT.Identity,
                                         bias=shift[:, 0:1], scale=gain[:, 0:1]).then_inc(sem["xn_ready"], 1)

            @block.vector
            def _(dve):
                after = chain(dve, sem["dve_step"])
                nc.vector.memset(xs[64:128, :, :, 0:1], 0.0).then_inc(sem["zeroed"], 1)
                for g in range(NGRP):
                    dve.wait_ge(sem["rows_ready"], g + 1)
                    for i in range(G):
                        last = nc.vector.bn_stats(stats[:, g * G + i, :], rows[:, g * G + i, :])
                after(last)
                for ins in normalise_by(nc, after, [rows[:, j, :] for j in range(NT)], [rows[:, j, :] for j in range(NT)],
                                        stats, mv, rstd, tmp, 1e-5):
                    ins.then_inc(sem["normalised"], 1)

            @block.gpsimd
            def _(pool):
                pool.wait_ge(sem["loaded"], 16 * len(loads))
                for g in range(NGRP):
                    pool.wait_ge(sem["cols_done"], g + 1)
                    y = core.y[:, g * G:(g + 1) * G, :]
                    nc.gpsimd.tensor_tensor(y, y, b2[:, :].rearrange("p (a c) -> p a c", a=1).to_broadcast([P, G, P]),
                                            ALU.add).then_inc(sem["biased"], 1)
        zero()
        with nc.Fori(0, NB // TURN) as turn:
            with nc.Block() as block:
                @block.tensor
                def _(pe):
                    for j in range(TURN + 1):
                        if j < TURN:
                            for c, (c0, n) in enumerate(HID_CHUNKS):
                                m = CH * j + c
                                if m >= 6:
                                    pe.wait_ge(sem["h_ready"], m - 5)
                                for g in (1, 0):
                                    last = nc.tensor.matmul(bank[m % 6][0:n, g * SEQ:(g + 1) * SEQ],
                                                            w1[:, g * DIM_INNER + c0:g * DIM_INNER + c0 + n],
                                                            cols[:, bass.ds((turn * TURN + j) * SEQ, SEQ)], start=True, stop=True)
                                last.then_inc(sem["hid_done"], 1)
                        if j >= 1:
                            i = j - 1
                            pe.wait_ge(sem["h_ready"], CH * (i + 1))
                            if i >= 2:
                                pe.wait_ge(sem["stored"], i - 1)
                            for t in range(TPB):
                                for c, (c0, n) in enumerate(HID_CHUNKS):
                                    last = nc.tensor.matmul(bank[6 + i % 2][:, t * P:(t + 1) * P], h[0:n, i % 2, c, t * P:(t + 1) * P],
                                                            w2[0:n, c, :], start=(c == 0), stop=(c == CH - 1))
                            last.then_inc(sem["y_done"], 1)

                @block.scalar
                def _(act):
                    for m in range(CH * TURN):
                        c, n = m % CH, HID_CHUNKS[m % CH][1]
                        act.wait_ge(sem["hid_done"], m + 1)
                        if m >= CH:
                            act.wait_ge(sem["h_ready"], m - CH + 1)
                        nc.scalar.activation(gel[0:n, c, :], bank[m % 6][0:n, SEQ:2 * SEQ], ACT.Gelu,
                                             bias=b1[0:n, 1, c:c + 1]).then_inc(sem["gelu_ready"], 1)

                @block.vector
                def _(dve):
                    for j in range(TURN + 1):
                        if j < TURN:
                            if j >= 2:
                                dve.wait_ge(sem["y_done"], j - 1)
                            for c, (c0, n) in enumerate(HID_CHUNKS):
                                m = CH * j + c
                                dve.wait_ge(sem["gelu_ready"], m + 1)
                                nc.vector.scalar_tensor_tensor(out=h[0:n, j % 2, c, :], in0=bank[m % 6][0:n, 0:SEQ],
                                                               scalar=b1[0:n, 0, c:c + 1], in1=gel[0:n, c, :],
                                                               op0=ALU.add, op1=ALU.mult).then_inc(sem["h_ready"], 1)
                        if j >= 1:
                            i = j - 1
                            dve.wait_ge(sem["y_done"], i + 1)
                            y = core.y[:, bass.ds((turn * TURN + i) * TPB, TPB), :]
                            nc.vector.tensor_tensor(y, tiles(bank[6 + i % 2][:, 0:SEQ]), y, ALU.add).then_inc(sem["stored"], 1)
            zero()


def local_transformer_stage(core):
    nc = core.nc
    with signals(nc, ["y_started"]) as ((started,), zero):
        with nc.Block() as block:
            @block.vector
            def _(dve):
                nc.vector.tensor_copy(core.y[:, :, :], core.xn[:, :, :]).then_inc(started, 1)
        zero()
    with nc.Fori(0, LAYERS_RUN) as l:
        local_attention_stage(core, l)
        glu_stage(core, l)


def gelu_linear_attention_stage(core):
    nc, dram, bank = core.nc, core.dram, core.bank
    with ExitStack() as ctx:
        def sb(name, shape, dt=F32):
            return ctx.enter_context(nc.sbuf_tensor("l1a_" + name, shape, dt))

        names = ("turned", "w_ready", "x_ready", "qk_proj", "v_proj", "gelu_ready", "qk_ready", "mean_ready", "cos_ready",
                 "kmean_ready", "v_ready", "rot_done", "sin_ready", "qkr_ready", "krt_done", "krt_ready", "kv_done",
                 "z_done", "kv_ready", "o_done", "z_read", "rec_ready", "divided", "stored")
        sems, zero = ctx.enter_context(signals(nc, ["l1a_" + n for n in names]))
        sem = dict(zip(names, sems))
        w, wt = sb("w", [P, 3, P]), sb("wt", [P, 3, P])
        bq, bk, bv = sb("bq", [P, 1]), sb("bk", [P, 1]), sb("bv", [P, P])
        gamma, beta = sb("gamma", [P, P]), sb("beta", [P, P])
        rope, swap, block_ = sb("rope", [P, 2, SEQ]), sb("swap", [P, P]), sb("block", [P, P])
        xb, part = sb("xb", [P, 2, SEQ]), sb("part", [P, 2, 2, SEQ])
        qk, qkr = sb("qk", [P, 4, 2, SEQ]), sb("qkr", [P, 4, 2, SEQ])
        v, krt = sb("v", [P, 4, TPB, P]), sb("krt", [P, 2, TPB, P])
        mean, kmean, kv = sb("mean", [P, 2]), sb("kmean", [P, 4, P]), sb("kv", [P, 2, P])
        rec, res = sb("rec", [P, TPB, P]), sb("res", [P, 2, TPB, P])
        load(core, [(w[:, i, :], dram["L1_attn_W" + n]) for i, n in enumerate("qkv")] +
             [(bq[:, :], column(dram["L1_attn_bq"])), (bk[:, :], column(dram["L1_attn_bk"])),
              (bv[:, :], spread(dram["L1_attn_bv"])), (gamma[:, :], spread(dram["L1_attn_gamma"])),
              (beta[:, :], spread(dram["L1_attn_beta"])), (rope[:, :, :], dram["rope_l1"]),
              (swap[:, :], dram["swap"]), (block_[:, :], dram["head_block"])])
        with nc.Block() as block:
            @block.tensor
            def _(pe):
                for i in range(3):
                    last = nc.tensor.transpose(bank[0][:, i * P:(i + 1) * P], w[:, i, :], core.ident[:, :])
                last.then_inc(sem["turned"], 1)

            @block.vector
            def _(dve):
                dve.wait_ge(sem["turned"], 1)
                nc.vector.tensor_copy(wt[:, :, :].rearrange("p a b -> p (a b)"), bank[0][:, 0:3 * P]).then_inc(sem["w_ready"], 1)
        zero()
        TURN = 8
        tiles = lambda ap: ap.rearrange("p (t c) -> p t c", t=TPB)
        table = lambda n: rope[:, n, :].rearrange("p (a q) -> p a q", a=1).to_broadcast([P, 2, SEQ])
        at = lambda slot, late: [slot - late] if 0 <= slot - late < TURN else []
        with nc.Fori(0, NB // TURN) as turn:
            with nc.Block() as block:
                @block.scalar
                def _(act):
                    for slot in range(TURN + 5):
                        for j in at(slot, 0):
                            if j >= 2:
                                act.wait_ge(sem["v_proj"], j - 1)
                            nc.scalar.copy(xb[:, j % 2, :], core.xnt[:, bass.ds((turn * TURN + j) * SEQ, SEQ)]).then_inc(sem["x_ready"], 1)
                            act.wait_ge(sem["qk_proj"], j + 1)
                            if j >= 2:
                                act.wait_ge(sem["qkr_ready"], j - 1)
                            for n, bias in enumerate((bq, bk)):
                                nc.scalar.activation(part[:, j % 2, n, :], bank[0][:, n * SEQ:(n + 1) * SEQ], ACT.Gelu,
                                                     bias=bias[:, 0:1]).then_inc(sem["gelu_ready"], 1)
                        for j in at(slot, 2):
                            act.wait_ge(sem["krt_done"], j + 1)
                            if j >= 2:
                                act.wait_ge(sem["kv_done"], j - 1)
                            nc.scalar.copy(krt[:, j % 2, :, :], tiles(bank[7][:, 0:SEQ])).then_inc(sem["krt_ready"], 1)

                @block.tensor
                def _(pe):
                    for slot in range(TURN + 5):
                        for j in at(slot, 0):
                            pe.wait_ge(sem["x_ready"], j + 1)
                            if j >= 1:
                                pe.wait_ge(sem["gelu_ready"], 2 * j)
                                pe.wait_ge(sem["v_ready"], j)
                            for n in range(2):
                                last = nc.tensor.matmul(bank[0][:, n * SEQ:(n + 1) * SEQ], wt[:, n, :], xb[:, j % 2, :], start=True, stop=True)
                            last.then_inc(sem["qk_proj"], 1)
                            for t in range(TPB):
                                last = nc.tensor.matmul(bank[1][:, t * P:(t + 1) * P], xb[:, j % 2, t * P:(t + 1) * P], wt[:, 2, :],
                                                        start=True, stop=True)
                            last.then_inc(sem["v_proj"], 1)
                        for j in at(slot, 1):
                            pe.wait_ge(sem["qk_ready"], j + 1)
                            if j >= 1:
                                pe.wait_ge(sem["sin_ready"], j)
                            nc.tensor.matmul(bank[2][:, :], swap[:, :], qk[:, j % 4, :, :].rearrange("p n q -> p (n q)"), start=True,
                                             stop=True).then_inc(sem["rot_done"], 1)
                        for j in at(slot, 2):
                            pe.wait_ge(sem["qkr_ready"], j + 1)
                            if j >= 1:
                                pe.wait_ge(sem["krt_ready"], j)
                            for t in range(TPB):
                                last = nc.tensor.transpose(bank[7][:, t * P:(t + 1) * P], qkr[:, j % 4, 1, t * P:(t + 1) * P], core.ident[:, :])
                            last.then_inc(sem["krt_done"], 1)
                        for j in at(slot, 3):
                            pe.wait_ge(sem["krt_ready"], j + 1)
                            pe.wait_ge(sem["v_ready"], j + 1)
                            if j >= 1:
                                pe.wait_ge(sem["kv_ready"], j)
                            for t in range(TPB):
                                last = nc.tensor.matmul(bank[3][:, 0:P], krt[:, j % 2, t, :], v[:, j % 4, t, :], start=(t == 0), stop=(t == TPB - 1))
                            last.then_inc(sem["kv_done"], 1)
                            pe.wait_ge(sem["kmean_ready"], j + 1)
                            if j >= 2:
                                pe.wait_ge(sem["z_read"], j - 1)
                            for t in range(TPB):
                                last = nc.tensor.matmul(bank[4 + 2 * (j % 2)][:, t * P:(t + 1) * P], qk[:, j % 4, 0, t * P:(t + 1) * P],
                                                        kmean[:, j % 4, :], start=True, stop=True)
                            last.then_inc(sem["z_done"], 1)
                        for j in at(slot, 4):
                            pe.wait_ge(sem["kv_ready"], j + 1)
                            if j >= 1:
                                pe.wait_ge(sem["divided"], j)
                            for t in range(TPB):
                                last = nc.tensor.matmul(bank[5][:, t * P:(t + 1) * P], qkr[:, j % 4, 0, t * P:(t + 1) * P], kv[:, j % 2, :],
                                                        start=True, stop=True)
                            last.then_inc(sem["o_done"], 1)

                @block.vector
                def _(dve):
                    for slot in range(TURN + 5):
                        for j in at(slot, 0):
                            if j >= 4:
                                dve.wait_ge(sem["z_done"], j - 3)
                            dve.wait_ge(sem["gelu_ready"], 2 * (j + 1))
                            nc.vector.tensor_scalar(qk[:, j % 4, :, :], part[:, j % 2, :, :], 0.21, None, ALU.add).then_inc(sem["qk_ready"], 1)
                            dve.wait_ge(sem["v_proj"], j + 1)
                            nc.vector.tensor_tensor(v[:, j % 4, :, :], tiles(bank[1][:, 0:SEQ]),
                                                    bv[:, :].rearrange("p (a c) -> p a c", a=1).to_broadcast([P, TPB, P]),
                                                    ALU.add).then_inc(sem["v_ready"], 1)
                            dve.wait_ge(sem["qk_ready"], j + 1)
                            nc.vector.tensor_reduce(mean[:, j % 2:j % 2 + 1], qk[:, j % 4, 1, :], AX.X, ALU.add).then_inc(sem["mean_ready"], 1)
                            nc.vector.tensor_tensor(part[:, j % 2, :, :], qk[:, j % 4, :, :], table(0), ALU.mult).then_inc(sem["cos_ready"], 1)
                            dve.wait_ge(sem["mean_ready"], j + 1)
                            nc.vector.tensor_scalar(kmean[:, j % 4, :], block_[:, :], mean[:, j % 2:j % 2 + 1], 1.0 / SEQ, ALU.mult,
                                                    ALU.mult).then_inc(sem["kmean_ready"], 1)
                        for j in at(slot, 1):
                            dve.wait_ge(sem["rot_done"], j + 1)
                            if j >= 4:
                                dve.wait_ge(sem["o_done"], j - 3)
                            nc.vector.tensor_tensor(qkr[:, j % 4, :, :], bank[2][:, :].rearrange("p (n q) -> p n q", n=2), table(1),
                                                    ALU.mult).then_inc(sem["sin_ready"], 1)
                            dve.wait_ge(sem["sin_ready"], j + 1)
                            dve.wait_ge(sem["cos_ready"], j + 1)
                            nc.vector.tensor_tensor(qkr[:, j % 4, :, :], qkr[:, j % 4, :, :], part[:, j % 2, :, :],
                                                    ALU.add).then_inc(sem["qkr_ready"], 1)
                        for j in at(slot, 3):
                            dve.wait_ge(sem["kv_done"], j + 1)
                            if j >= 2:
                                dve.wait_ge(sem["o_done"], j - 1)
                            nc.vector.scalar_tensor_tensor(out=kv[:, j % 2, :], in0=bank[3][:, 0:P], scalar=1.0 / SEQ, in1=block_[:, :],
                                                           op0=ALU.mult, op1=ALU.mult).then_inc(sem["kv_ready"], 1)
                        for j in at(slot, 4):
                            dve.wait_ge(sem["z_done"], j + 1)
                            if j >= 1:
                                dve.wait_ge(sem["divided"], j)
                            nc.vector.tensor_scalar(rec[:, :, :], tiles(bank[4 + 2 * (j % 2)][:, 0:SEQ]), 1e-6, None, ALU.add).then_inc(sem["z_read"], 1)
                            dve.wait_ge(sem["z_read"], j + 1)
                            nc.vector.reciprocal(rec[:, :, :], rec[:, :, :]).then_inc(sem["rec_ready"], 1)
                            dve.wait_ge(sem["rec_ready"], j + 1)
                            dve.wait_ge(sem["o_done"], j + 1)
                            if j >= 2:
                                dve.wait_ge(sem["stored"], j - 1)
                            nc.vector.tensor_tensor(res[:, j % 2, :, :], tiles(bank[5][:, 0:SEQ]), rec[:, :, :], ALU.mult).then_inc(sem["divided"], 1)

                @block.gpsimd
                def _(pool):
                    for j in range(TURN):
                        pool.wait_ge(sem["divided"], j + 1)
                        tile = bass.ds((turn * TURN + j) * TPB, TPB)
                        nc.gpsimd.tensor_tensor(core.s[:, tile, :], res[:, j % 2, :, :], core.xn[:, tile, :], ALU.add).then_inc(sem["stored"], 1)
            zero()
        layer_norm_of_branch(core, 1e-12, gamma[:, :], beta[:, :])


def experts_stage(core):
    nc, dram, bank = core.nc, core.dram, core.bank
    with ExitStack() as ctx:
        def sb(name, shape, dt=F32):
            return ctx.enter_context(nc.sbuf_tensor("moe_" + name, shape, dt))

        chosen = sb("chosen", [P, NT, NE])
        with ExitStack() as ctx2:
            def sb2(name, shape, dt=F32):
                return ctx2.enter_context(nc.sbuf_tensor("route_" + name, shape, dt))

            names = ("turned", "router_ready", "logits_done", "exp_ready", "shifted", "top_ready", "top_stored", "top_spread",
                     "onehot_ready", "compared", "counted", "dve_step")
            sems, zero = ctx2.enter_context(signals(nc, ["route_" + n for n in names]))
            sem = dict(zip(names, sems))
            router, router_t = sb2("router", [NE, P]), sb2("router_t", [P, NE])
            expert_no, earlier = sb2("expert_no", [P, NT, NE]), sb2("earlier", [P, P])
            prob, onehot, cand = sb2("prob", [P, NT, NE]), sb2("onehot", [P, NT, NE]), sb2("cand", [P, NT, NE])
            onehot_b = sb2("onehot_b", [P, NT, NE], BF16)
            red, top, keep, count = sb2("red", [P, NT]), sb2("top", [P, NT]), sb2("keep", [P, NT]), sb2("count", [P, NT])
            row = sb2("row", [P, TOK])
            above, tie = sb2("above", [P, 2, TOK], BF16), sb2("tie", [P, P], BF16)
            top_dram = nc.dram_tensor("top_prob", (NT, P), F32, kind="Internal").ap()
            load(core, [(router[:, :], dram["L1_ffn_router_w"]), (expert_no[:, :, :], dram["expert_no"]),
                        (earlier[:, :], dram["strictly_before"])])
            wide = lambda v: v.rearrange("p (t a) -> p t a", a=1).to_broadcast([P, NT, NE])
            with nc.Block() as block:
                @block.tensor
                def _(pe):
                    nc.tensor.transpose(bank[0][:, 0:NE], router[:, :], core.ident[0:NE, 0:NE]).then_inc(sem["turned"], 1)
                    pe.wait_ge(sem["router_ready"], 1)
                    for i in range(NT):
                        last = nc.tensor.matmul(bank[1][:, i * NE:(i + 1) * NE], core.xnt[:, i * P:(i + 1) * P], router_t[:, :],
                                                start=True, stop=True)
                    last.then_inc(sem["logits_done"], 1)
                    pe.wait_ge(sem["onehot_ready"], 1)
                    for j in range(NT):
                        pe.wait_ge(sem["compared"], j + 1)
                        for i in range(NT):
                            last = nc.tensor.matmul(bank[2][:, i * NE:(i + 1) * NE], above[:, j % 2, i * P:(i + 1) * P],
                                                    onehot_b[:, j, :], start=(i == 0 and j == 0), stop=(j == NT - 1),
                                                    skip_group_check=True)
                        last.then_inc(sem["counted"], 1)

                @block.scalar
                def _(act):
                    act.wait_ge(sem["shifted"], 1)
                    nc.scalar.activation(prob[:, :, :], prob[:, :, :], ACT.Exp).then_inc(sem["exp_ready"], 1)

                @block.sync
                def _(sp):
                    sp.wait_ge(sem["top_ready"], 1)
                    sp.dma_start(top_dram.rearrange("t p -> p t"), top[:, :]).then_inc(sem["top_stored"], 16)
                    sp.wait_ge(sem["top_stored"], 16)
                    sp.dma_start(row[:, :], top_dram.rearrange("(a t) p -> a (t p)", a=1).to_broadcast([P, TOK])).then_inc(sem["top_spread"], 16)

                @block.vector
                def _(dve):
                    after = chain(dve, sem["dve_step"])
                    dve.wait_ge(sem["turned"], 1)
                    nc.vector.tensor_copy(router_t[:, :], bank[0][:, 0:NE]).then_inc(sem["router_ready"], 1)
                    dve.wait_ge(sem["logits_done"], 1)
                    logits = bank[1][:, 0:NT * NE].rearrange("p (t e) -> p t e", e=NE)
                    after(nc.vector.tensor_reduce(red[:, :], logits, AX.X, ALU.max))
                    nc.vector.tensor_tensor(prob[:, :, :], logits, wide(red[:, :]), ALU.subtract).then_inc(sem["shifted"], 1)
                    dve.wait_ge(sem["exp_ready"], 1)
                    after(nc.vector.tensor_reduce(red[:, :], prob[:, :, :], AX.X, ALU.add))
                    after(nc.vector.reciprocal(red[:, :], red[:, :]))
                    after(nc.vector.tensor_tensor(prob[:, :, :], prob[:, :, :], wide(red[:, :]), ALU.mult))
                    nc.vector.tensor_reduce(top[:, :], prob[:, :, :], AX.X, ALU.max).then_inc(sem["top_ready"], 1)
                    dve.wait_ge(sem["top_ready"], 1)
                    after(nc.vector.tensor_tensor(cand[:, :, :], prob[:, :, :], wide(top[:, :]), ALU.is_equal))
                    after(nc.vector.scalar_tensor_tensor(out=cand[:, :, :].rearrange("p t e -> p (t e)"),
                                                         in0=cand[:, :, :].rearrange("p t e -> p (t e)"), scalar=-100.0,
                                                         in1=expert_no[:, :, :].rearrange("p t e -> p (t e)"),
                                                         op0=ALU.mult, op1=ALU.add))
                    after(nc.vector.tensor_reduce(red[:, :], cand[:, :, :], AX.X, ALU.min))
                    after(nc.vector.tensor_tensor(onehot[:, :, :], cand[:, :, :], wide(red[:, :]), ALU.is_equal))
                    nc.vector.tensor_copy(onehot_b[:, :, :], onehot[:, :, :]).then_inc(sem["onehot_ready"], 1)
                    dve.wait_ge(sem["top_spread"], 16)
                    for j in range(NT):
                        if j >= 2:
                            dve.wait_ge(sem["counted"], j - 1)
                        m, mine = j % 2, top[:, j:j + 1]
                        d0, d1 = j * P, (j + 1) * P
                        after(nc.vector.tensor_scalar(above[:, m, 0:d1], row[:, 0:d1], mine, None, ALU.is_lt))
                        after(nc.vector.scalar_tensor_tensor(out=tie[:, :], in0=row[:, d0:d1], scalar=mine, in1=earlier[:, :],
                                                             op0=ALU.is_equal, op1=ALU.mult))
                        if j < NT - 1:
                            nc.vector.tensor_scalar(above[:, m, d1:TOK], row[:, d1:TOK], mine, None, ALU.is_le)
                        nc.vector.tensor_tensor(above[:, m, d0:d1], above[:, m, d0:d1], tie[:, :], ALU.add).then_inc(sem["compared"], 1)
                    dve.wait_ge(sem["counted"], NT)
                    counts = bank[2][:, 0:NT * NE].rearrange("p (t e) -> p t e", e=NE)
                    after(nc.vector.tensor_tensor(cand[:, :, :], counts, onehot[:, :, :], ALU.mult))
                    after(nc.vector.tensor_reduce(count[:, :], cand[:, :, :], AX.X, ALU.add))
                    after(nc.vector.tensor_scalar(keep[:, :], count[:, :], float(CAPACITY), None, ALU.is_lt))
                    after(nc.vector.tensor_tensor(chosen[:, :, :], onehot[:, :, :], wide(keep[:, :]), ALU.mult))
                    after(nc.vector.tensor_scalar(keep[:, :], keep[:, :], -1.0, 1.0, ALU.mult, ALU.add))
                    after(nc.vector.tensor_tensor(chosen[:, :, 0], chosen[:, :, 0], keep[:, :], ALU.add))
            zero()
        names = ("turned", "copied", "b2_done", "y_started", "hid_done", "h_act", "h_dve", "out_done", "added")
        sems, zero = ctx.enter_context(signals(nc, ["moe_" + n for n in names]))
        sem = dict(zip(names, sems))
        w1, w2, b1, b2 = sb("w1", [P, DFF]), sb("w2", [P, 4, P]), sb("b1", [P, 4]), sb("b2", [NE, P])
        sel_t = sb("sel_t", [NE, NT, P])
        h = sb("h", [P, 2, 4, 512])
        load(core, [(b2[:, :], dram["L1_ffn_b2"])])
        with nc.Block() as block:
            @block.tensor
            def _(pe):
                for g in range(NT // 4):
                    if g >= 2:
                        pe.wait_ge(sem["copied"], g - 1)
                    for i in range(4):
                        last = nc.tensor.transpose(bank[g % 2][0:NE, i * P:(i + 1) * P], chosen[:, 4 * g + i, :], core.ident[:, :])
                    last.then_inc(sem["turned"], 1)
                for g in range(NT // 4):
                    pe.wait_ge(sem["copied"], g + 1)
                    if g >= 2:
                        pe.wait_ge(sem["y_started"], g - 1)
                    for i in range(4):
                        last = nc.tensor.matmul(bank[2 + g % 2][:, i * P:(i + 1) * P], sel_t[:, 4 * g + i, :], b2[:, :],
                                                start=True, stop=True)
                    last.then_inc(sem["b2_done"], 1)

            @block.scalar
            def _(act):
                for g in range(NT // 4):
                    act.wait_ge(sem["turned"], g + 1)
                    nc.scalar.copy(sel_t[:, 4 * g:4 * g + 4, :], bank[g % 2][0:NE, :].rearrange("p (i q) -> p i q", i=4)).then_inc(sem["copied"], 1)

            @block.vector
            def _(dve):
                for g in range(NT // 4):
                    dve.wait_ge(sem["b2_done"], g + 1)
                    nc.vector.tensor_copy(core.y[:, 4 * g:4 * g + 4, :],
                                          bank[2 + g % 2][:, :].rearrange("p (i c) -> p i c", i=4)).then_inc(sem["y_started"], 1)
        zero()
        NBLK = TOK // 512
        with nc.Fori(0, NE) as e:
            load(core, [(w1[:, :], dram["L1_ffn_W1"][bass.ds(e, 1), :, :].rearrange("a p n -> p (a n)")),
                        (w2[:, :, :], dram["L1_ffn_W2"][bass.ds(e, 1), :, :].rearrange("a (c p) n -> p (a c) n", p=P)),
                        (b1[:, :], dram["L1_ffn_b1"][bass.ds(e, 1), :].rearrange("a (c p) -> p (a c)", p=P))])
            with nc.Block() as block:
                @block.tensor
                def _(pe):
                    def hidden(k):
                        for c in range(4):
                            if k >= 1:
                                pe.wait_ge(sem["h_act"] if c % 2 == 0 else sem["h_dve"], 2 * (k - 1) + c // 2 + 1)
                            nc.tensor.matmul(bank[c][:, :], w1[:, c * P:(c + 1) * P], core.xnt[:, k * 512:(k + 1) * 512],
                                             start=True, stop=True).then_inc(sem["hid_done"], 1)

                    def outputs(k):
                        pe.wait_ge(sem["h_act"], 2 * (k + 1))
                        pe.wait_ge(sem["h_dve"], 2 * (k + 1))
                        for i in range(4):
                            if k >= 1:
                                pe.wait_ge(sem["added"], 4 * (k - 1) + i + 1)
                            for c in range(4):
                                last = nc.tensor.matmul(bank[4 + i][:, 0:P], h[:, k % 2, c, i * P:(i + 1) * P], w2[:, c, :],
                                                        start=(c == 0), stop=(c == 3))
                            last.then_inc(sem["out_done"], 1)

                    for k in range(NBLK + 1):
                        if k < NBLK:
                            hidden(k)
                        if k >= 1:
                            outputs(k - 1)

                @block.scalar
                def _(act):
                    for k in range(NBLK):
                        if k >= 2:
                            act.wait_ge(sem["out_done"], 4 * (k - 1))
                        for c in (0, 2):
                            act.wait_ge(sem["hid_done"], 4 * k + c + 1)
                            nc.scalar.activation(h[:, k % 2, c, :], bank[c][:, :], ACT.Relu, bias=b1[:, c:c + 1]).then_inc(sem["h_act"], 1)

                @block.vector
                def _(dve):
                    for k in range(NBLK + 1):
                        if k < NBLK:
                            if k >= 2:
                                dve.wait_ge(sem["out_done"], 4 * (k - 1))
                            for c in (1, 3):
                                dve.wait_ge(sem["hid_done"], 4 * k + c + 1)
                                nc.vector.tensor_scalar(h[:, k % 2, c, :], bank[c][:, :], b1[:, c:c + 1], 0.0, ALU.add,
                                                        ALU.max).then_inc(sem["h_dve"], 1)
                        if k >= 1:
                            for i in range(4):
                                tile = 4 * (k - 1) + i
                                dve.wait_ge(sem["out_done"], tile + 1)
                                nc.vector.scalar_tensor_tensor(out=core.y[:, tile, :], in0=bank[4 + i][:, 0:P],
                                                               scalar=chosen[:, tile, bass.ds(e, 1)], in1=core.y[:, tile, :],
                                                               op0=ALU.mult, op1=ALU.add).then_inc(sem["added"], 1)
            zero()


def store_tile(core, sig, dve, att, shift, k, t, residual):
    nc = core.nc
    att.full(dve, "y", k, t)
    tile = bass.ds((shift + k) * TPB + t, 1)
    src = core.bank[7][:, 0:P].rearrange("p (a c) -> p a c", a=1)
    if residual:
        ins = nc.vector.tensor_tensor(core.s[:, tile, :], src, core.xn[:, tile, :], ALU.add)
    else:
        ins = nc.vector.tensor_copy(core.s[:, tile, :], src)
    sig.done(ins, "bank7_free")


def causal_attention_stage(core):
    nc, dram, bank = core.nc, core.dram, core.bank
    PAIRS, CH, FIRST_CHUNK = HEADS // 2, HEADS // 2 + 2 * TPB, 2
    with ExitStack() as ctx:
        def sb(name, shape, dt=F32):
            return ctx.enter_context(nc.sbuf_tensor("l2a_" + name, shape, dt))

        att = Softmax(core, sb, 64, False, "mask_causal", 1.0 / 8.0, ())
        proj = [16 * k + FIRST_CHUNK + r for k in range(NB) for r in range(CH)]
        number_at = {slot: i for i, slot in enumerate(proj)}
        when = dict(att.when)
        when.update({
            "x_ready": [16 * k + 1 for k in range(NB)],
            "proj_done": proj,
            "act_copied": [s + 1 for i, s in enumerate(proj) if i % 2 == 0],
            "dve_copied": [s + 1 for i, s in enumerate(proj) if i % 2 == 1],
        })
        names = tuple(when)
        sems, zero = ctx.enter_context(signals(nc, ["l2a_" + n for n in names]))
        sig = att.sig = Signals(dict(zip(names, sems)), when)
        w = {n: sb("w" + n, [P, HEADS, 64]) for n in "qkv"}
        gamma, beta, xb = sb("gamma", [P, P]), sb("beta", [P, P]), sb("xb", [P, SEQ])
        load(core, [(w[n][:, :, :], dram["L2_attn_W" + n].rearrange("h d e -> d h e")) for n in w] +
             [(att.wo[:, :, :], dram["L2_attn_Wo"].rearrange("(c p) n -> p c n", p=P)), (att.mask[:, :, :], att.mask_src),
              (gamma[:, :], spread(dram["L2_attn_gamma"])), (beta[:, :], spread(dram["L2_attn_beta"]))])

        def pair(n, hp):
            return w[n][:, 2 * hp:2 * hp + 2, :].rearrange("p h e -> p (h e)")

        def copy_chunk(eng, copy, i, done):
            k, c = i // CH, i % CH
            sig.wait(eng, "proj_done", i + 1)
            src = bank[5 + i % 2]
            if c < PAIRS:
                copy(att.qt[:, k % 2, c, :], src[:, 0:SEQ])
                sig.done(copy(att.kt[:, k % 2, c, :], src[:, SEQ:2 * SEQ]), done)
            else:
                t, half = (c - PAIRS) // 2, (c - PAIRS) % 2
                sig.done(copy(att.v[:, k % 2, t, half * 512:(half + 1) * 512], src[:, :]), done)

        def emit(block, slots, shift):
            @block.scalar
            def _(act):
                for slot in slots:
                    att.copy_turned(act, slot - 21)
                    att.exps(act, slot - 17)
                    if slot % 16 == 1 and slot // 16 < NB:
                        k = slot // 16
                        sig.wait(act, "proj_done", CH * k)
                        sig.done(nc.scalar.copy(xb[:, :], core.xnt[:, bass.ds((shift + k) * SEQ, SEQ)]), "x_ready")
                    i = number_at.get(slot - 1, 1)
                    if i % 2 == 0:
                        copy_chunk(act, nc.scalar.copy, i, "act_copied")

            @block.tensor
            def _(pe):
                for slot in slots:
                    i = number_at.get(slot)
                    if i is not None:
                        k, c = i // CH, i % CH
                        if c == 0:
                            sig.wait(pe, "x_ready", k + 1)
                        if i >= 2:
                            sig.wait(pe, "dve_copied" if i % 2 else "act_copied", i // 2)
                        to = bank[5 + i % 2]
                        if c < PAIRS:
                            nc.tensor.matmul(to[:, 0:SEQ], pair("q", c), xb[:, :], start=True, stop=True)
                            ins = nc.tensor.matmul(to[:, SEQ:2 * SEQ], pair("k", c), xb[:, :], start=True, stop=True)
                        else:
                            t, half = (c - PAIRS) // 2, (c - PAIRS) % 2
                            ins = nc.tensor.matmul(to[:, :], xb[:, t * P:(t + 1) * P],
                                                   w["v"][:, 8 * half:8 * half + 8, :].rearrange("p h e -> p (h e)"),
                                                   start=True, stop=True)
                        sig.done(ins, "proj_done")
                    att.scores(pe, slot - 16)
                    att.values(pe, slot - 22)
                    if slot in att.at:
                        kind, k, j = att.at[slot]
                        att.project_out(pe, k, j)
                    att.turn(pe, slot - 20)

            @block.vector
            def _(dve):
                for slot in slots:
                    att.mask_and_max(dve, slot - 17)
                    att.reciprocals(dve, slot - 18)
                    att.divide(dve, slot - 18)
                    kind, k, j = att.at.get(slot - 1, (None, 0, 0))
                    if kind == "y":
                        store_tile(core, sig, dve, att, shift, k, j, residual=True)
                    i = number_at.get(slot - 1, 0)
                    if i % 2 == 1:
                        copy_chunk(dve, nc.vector.tensor_copy, i, "dve_copied")
                    att.copy_columns(dve, nc.vector.tensor_copy, slot - 25)

        run_windows(nc, sig, zero, emit, att.last_slot)
        layer_norm_of_branch(core, 1e-3, gamma[:, :], beta[:, :])


def routed_ffn_stage(core):
    nc, dram, bank = core.nc, core.dram, core.bank
    with ExitStack() as ctx:
        def sb(name, shape, dt=F32):
            return ctx.enter_context(nc.sbuf_tensor("cd_" + name, shape, dt))

        weight = sb("weight", [P, NT])
        with ExitStack() as ctx2:
            def sb2(name, shape, dt=F32):
                return ctx2.enter_context(nc.sbuf_tensor("cd_" + name, shape, dt))

            names = ("rt_ready", "s_done", "dve_step", "max_ready", "sum_ready", "log_ready", "z_ready", "score_ready",
                     "stored", "spread_")
            sems, zero = ctx2.enter_context(signals(nc, ["cd_" + n for n in names]))
            sem = dict(zip(names, sems))
            rt, rtm = sb2("rt", [P, 1]), sb2("rtm", [P, NB, NB])
            s, r, u, e = sb2("s", [NB, SEQ]), sb2("r", [NB, SEQ]), sb2("u", [NB, SEQ]), sb2("e", [NB, SEQ])
            m, nm, total, log, a = (sb2(n, [NB, 1]) for n in ("m", "nm", "total", "log", "a"))
            row, mine, before = sb2("row", [P, NB, SEQ]), sb2("mine", [P, NT]), sb2("before", [P, TPB, SEQ])
            junk, more, same = sb2("junk", [P, 2, SEQ]), sb2("more", [P, NT]), sb2("same", [P, NT])
            score_dram = nc.dram_tensor("route_score", (NB, SEQ), F32, kind="Internal").ap()
            load(core, [(rt[:, :], column(dram["L2_ffn_routing_token"])), (before[:, :, :], dram["before"])])
            with nc.Block() as block:
                @block.vector
                def _(dve):
                    after = chain(dve, sem["dve_step"])
                    after(nc.vector.memset(rtm[:, :, :], 0.0))
                    for b in range(NB):
                        last = nc.vector.tensor_copy(rtm[:, b, b:b + 1], rt[:, :])
                    last.then_inc(sem["rt_ready"], 1)
                    dve.wait_ge(sem["s_done"], 1)
                    after(nc.vector.tensor_copy(s[:, :], bank[0][0:NB, 0:SEQ]))
                    after(nc.vector.tensor_scalar(r[:, :], s[:, :], 0.0, None, ALU.max))

                @block.tensor
                def _(pe):
                    pe.wait_ge(sem["rt_ready"], 1)
                    for b in range(NB):
                        last = nc.tensor.matmul(bank[0][0:NB, 0:SEQ], rtm[:, b, :], core.xnt[:, b * SEQ:(b + 1) * SEQ],
                                                start=(b == 0), stop=(b == NB - 1))
                    last.then_inc(sem["s_done"], 1)
            zero()
            UNROLL = 10
            with nc.Fori(0, ROUTE_ITERS // UNROLL) as _i:
                with nc.Block() as block:
                    @block.vector
                    def _(dve):
                        after = chain(dve, sem["dve_step"])
                        for k in range(UNROLL):
                            after(nc.vector.tensor_tensor_reduce(u[:, :], s[:, :], r[:, :], 1.0 / EPS_ROUTE, LOWEST,
                                                                 ALU.subtract, ALU.max, m[:, :]))
                            nc.vector.tensor_scalar(nm[:, :], m[:, :], -1.0, None, ALU.mult).then_inc(sem["max_ready"], 1)
                            dve.wait_ge(sem["log_ready"], k + 1)
                            after(nc.vector.tensor_tensor(a[:, :], log[:, :], m[:, :], ALU.add))
                            after(nc.vector.tensor_scalar(a[:, :], a[:, :], -EPS_ROUTE, float(np.float32(EPS_ROUTE) * np.log(np.float32(K_ROUTE))),
                                                          ALU.mult, ALU.add))
                            after(nc.vector.tensor_scalar(r[:, :], s[:, :], a[:, 0:1], 0.0, ALU.add, ALU.max))

                    @block.scalar
                    def _(act):
                        for k in range(UNROLL):
                            act.wait_ge(sem["max_ready"], k + 1)
                            nc.scalar.activation(e[:, :], u[:, :], ACT.Exp, bias=nm[:, 0:1], accum_out=total[:, :]).then_inc(sem["sum_ready"], 1)
                            act.wait_ge(sem["sum_ready"], k + 1)
                            nc.scalar.activation(log[:, :], total[:, :], ACT.Ln).then_inc(sem["log_ready"], 1)
                zero()
            with nc.Block() as block:
                @block.vector
                def _(dve):
                    after = chain(dve, sem["dve_step"])
                    after(nc.vector.scalar_tensor_tensor(out=u[:, :], in0=s[:, :], scalar=a[:, 0:1], in1=r[:, :],
                                                         op0=ALU.add, op1=ALU.subtract))
                    nc.vector.tensor_scalar(u[:, :], u[:, :], 1.0 / EPS_ROUTE, -87.336545, ALU.mult, ALU.max).then_inc(sem["z_ready"], 1)
                    dve.wait_ge(sem["spread_"], 32)
                    for b in range(NB):
                        for t in range(TPB):
                            i = b * TPB + t
                            after(nc.vector.tensor_scalar(junk[:, 0, :], row[:, b, :], mine[:, i:i + 1], 0.0, ALU.is_gt, ALU.add,
                                                          accum_out=more[:, i:i + 1]))
                            after(nc.vector.scalar_tensor_tensor(out=junk[:, 1, :], in0=row[:, b, :], scalar=mine[:, i:i + 1],
                                                                 in1=before[:, t, :], op0=ALU.is_equal, op1=ALU.mult,
                                                                 accum_out=same[:, i:i + 1]))
                    after(nc.vector.tensor_tensor(more[:, :], more[:, :], same[:, :], ALU.add))
                    after(nc.vector.tensor_scalar(more[:, :], more[:, :], float(NUM_HEAVY), None, ALU.is_lt))
                    after(nc.vector.tensor_scalar(same[:, :], mine[:, :], -1.0, 1.0, ALU.mult, ALU.add))
                    after(nc.vector.tensor_tensor(same[:, :], same[:, :], mine[:, :], ALU.add))
                    after(nc.vector.tensor_tensor(weight[:, :], same[:, :], more[:, :], ALU.mult))

                @block.scalar
                def _(act):
                    act.wait_ge(sem["z_ready"], 1)
                    nc.scalar.activation(e[:, :], u[:, :], ACT.Exp).then_inc(sem["score_ready"], 1)

                @block.sync
                def _(sp):
                    sp.wait_ge(sem["score_ready"], 1)
                    sp.dma_start(score_dram, e[:, :]).then_inc(sem["stored"], 16)
                    sp.wait_ge(sem["stored"], 16)
                    sp.dma_start(row[:, :, :].rearrange("p b q -> p (b q)"),
                                 score_dram.rearrange("(a b) q -> a (b q)", a=1).to_broadcast([P, TOK])).then_inc(sem["spread_"], 16)
                    sp.dma_start(mine[:, :], score_dram.rearrange("b (t p) -> p (b t)", p=P)).then_inc(sem["spread_"], 16)
            zero()
        G, TURN = 4, 4
        NGRP = NT // G
        names = ("dve_step", "squared", "xr_ready", "cols_done", "cols_ready", "hid_done", "light_gelu", "heavy_gelu",
                 "light_done", "heavy_done", "heavy_biased", "weighted", "stored")
        sems, zero = ctx.enter_context(signals(nc, ["lh_" + n for n in names]))
        sem = dict(zip(names, sems))
        w1l, w2l = sb("w1l", [P, LIGHT]), sb("w2l", [LIGHT, P])
        w1h, w2h = sb("w1h", [P, HEAVY]), sb("w2h", [P, 4, P])
        b1l, b2l, b1h, b2h = sb("b1l", [LIGHT, 1]), sb("b2l", [P, P]), sb("b1h", [P, 4]), sb("b2h", [P, P])
        gl, gh = sb("gl", [P, 1]), sb("gh", [P, 1])
        n2, rn, tmp = sb("n2", [P, NT]), sb("rn", [P, NT]), sb("tmp", [P, NT])
        sq, xc = sb("sq", [P, NT // 2, P]), sb("xc", [P, TOK])
        hl, hh = sb("hl", [LIGHT, 2, 512]), sb("hh", [P, 2, 4, 512])
        heavy, both = sb("heavy", [P, G, P]), sb("both", [P, G, P])
        load(core, [(w1l[:, :], dram["L2_ffn_w1_light"]), (w2l[:, :], dram["L2_ffn_w2_light"]),
                    (w1h[:, :], dram["L2_ffn_w1_heavy"]), (w2h[:, :, :], dram["L2_ffn_w2_heavy"].rearrange("(c p) n -> p c n", p=P)),
                    (b1l[:, :], column(dram["L2_ffn_b1_light"])), (b2l[:, :], spread(dram["L2_ffn_b2_light"])),
                    (b1h[:, :], dram["L2_ffn_b1_heavy"].rearrange("(c p) -> p c", p=P)), (b2h[:, :], spread(dram["L2_ffn_b2_heavy"])),
                    (gl[:, :], column(dram["L2_ffn_gamma_light"])), (gh[:, :], column(dram["L2_ffn_gamma_heavy"]))])
        with nc.Block() as block:
            @block.vector
            def _(dve):
                after = chain(dve, sem["dve_step"])
                for half in range(2):
                    rows = slice(half * NT // 2, (half + 1) * NT // 2)
                    dve.wait_ge(sem["squared"], half + 1)
                    after(nc.vector.tensor_reduce(n2[:, rows], sq[:, :, :] if half == 0 else core.y[:, rows, :], AX.X, ALU.add))
                after(nc.vector.tensor_scalar(n2[:, :], n2[:, :], 1e-24, None, ALU.max))
                rsqrt(nc, after, rn[:, :], n2[:, :], tmp[:, :])
                after(nc.vector.tensor_scalar(rn[:, :], rn[:, :], float(np.sqrt(P)), None, ALU.mult))
                for i in range(NT):
                    nc.vector.tensor_scalar(core.y[:, i, :], core.xn[:, i, :], rn[:, i:i + 1], None, ALU.mult).then_inc(sem["xr_ready"], 1)
                after(nc.vector.tensor_scalar(w1l[:, :], w1l[:, :], gl[:, 0:1], None, ALU.mult))
                after(nc.vector.tensor_scalar(w1h[:, :], w1h[:, :], gh[:, 0:1], None, ALU.mult))

            @block.tensor
            def _(pe):
                for g in range(NGRP):
                    pe.wait_ge(sem["xr_ready"], G * (g + 1))
                    if g >= 2:
                        pe.wait_ge(sem["cols_ready"], g - 1)
                    for i in range(G):
                        last = nc.tensor.transpose(bank[g % 2][:, i * P:(i + 1) * P], core.y[:, G * g + i, :], core.ident[:, :])
                    last.then_inc(sem["cols_done"], 1)

            @block.scalar
            def _(act):
                half = NT // 2
                nc.scalar.activation(sq[:, :, :], core.xn[:, 0:half, :], ACT.Square).then_inc(sem["squared"], 1)
                nc.scalar.activation(core.y[:, half:NT, :], core.xn[:, half:NT, :], ACT.Square).then_inc(sem["squared"], 1)
                for g in range(NGRP):
                    act.wait_ge(sem["cols_done"], g + 1)
                    nc.scalar.copy(xc[:, g * 512:(g + 1) * 512], bank[g % 2][:, :]).then_inc(sem["cols_ready"], 1)
        zero()
        with nc.Fori(0, NGRP // TURN) as turn:
            with nc.Block() as block:
                @block.tensor
                def _(pe):
                    def hidden(i):
                        x = xc[:, bass.ds((turn * TURN + i) * 512, 512)]
                        if i >= 1:
                            pe.wait_ge(sem["light_gelu"], i)
                        nc.tensor.matmul(bank[0][0:LIGHT, :], w1l[:, :], x, start=True, stop=True).then_inc(sem["hid_done"], 1)
                        for c in range(4):
                            if i >= 1:
                                pe.wait_ge(sem["heavy_gelu"], 4 * (i - 1) + c + 1)
                            nc.tensor.matmul(bank[1 + c][:, :], w1h[:, c * P:(c + 1) * P], x, start=True, stop=True).then_inc(sem["hid_done"], 1)

                    def outputs(i):
                        pe.wait_ge(sem["light_gelu"], i + 1)
                        if i >= 1:
                            pe.wait_ge(sem["weighted"], i)
                        for j in range(G):
                            last = nc.tensor.matmul(bank[5][:, j * P:(j + 1) * P], hl[:, i % 2, j * P:(j + 1) * P], w2l[:, :],
                                                    start=True, stop=True)
                        last.then_inc(sem["light_done"], 1)
                        pe.wait_ge(sem["heavy_gelu"], 4 * (i + 1))
                        if i >= 2:
                            pe.wait_ge(sem["heavy_biased"], i - 1)
                        for j in range(G):
                            for c in range(4):
                                last = nc.tensor.matmul(bank[6 + i % 2][:, j * P:(j + 1) * P], hh[:, i % 2, c, j * P:(j + 1) * P],
                                                        w2h[:, c, :], start=(c == 0), stop=(c == 3))
                        last.then_inc(sem["heavy_done"], 1)

                    for i in range(TURN + 1):
                        if i < TURN:
                            hidden(i)
                        if i >= 1:
                            outputs(i - 1)

                @block.scalar
                def _(act):
                    for i in range(TURN):
                        act.wait_ge(sem["hid_done"], 5 * i + 1)
                        if i >= 2:
                            act.wait_ge(sem["heavy_done"], i - 1)
                        nc.scalar.activation(hl[:, i % 2, :], bank[0][0:LIGHT, :], ACT.Gelu, bias=b1l[:, 0:1]).then_inc(sem["light_gelu"], 1)
                        for c in range(4):
                            act.wait_ge(sem["hid_done"], 5 * i + c + 2)
                            nc.scalar.activation(hh[:, i % 2, c, :], bank[1 + c][:, :], ACT.Gelu, bias=b1h[:, c:c + 1]).then_inc(sem["heavy_gelu"], 1)

                @block.vector
                def _(dve):
                    for i in range(TURN):
                        wide = lambda v: v.rearrange("p (a c) -> p a c", a=1).to_broadcast([P, G, P])
                        tile = (turn * TURN + i) * G
                        dve.wait_ge(sem["heavy_done"], i + 1)
                        if i >= 1:
                            dve.wait_ge(sem["stored"], i)
                        nc.vector.tensor_tensor(heavy[:, :, :], bank[6 + i % 2][:, :].rearrange("p (j c) -> p j c", j=G), wide(b2h[:, :]),
                                                ALU.add).then_inc(sem["heavy_biased"], 1)
                        dve.wait_ge(sem["heavy_biased"], i + 1)
                        dve.wait_ge(sem["light_done"], i + 1)
                        for j in range(G):
                            last = nc.vector.scalar_tensor_tensor(out=both[:, j, :], in0=heavy[:, j, :], scalar=weight[:, bass.ds(tile + j, 1)],
                                                                  in1=bank[5][:, j * P:(j + 1) * P], op0=ALU.mult, op1=ALU.add)
                        last.then_inc(sem["weighted"], 1)
                        dve.wait_ge(sem["weighted"], i + 1)
                        nc.vector.tensor_tensor(core.y[:, bass.ds(tile, G), :], both[:, :, :], wide(b2l[:, :]), ALU.add).then_inc(sem["stored"], 1)
            zero()


def small_head_attention_stage(core):
    nc, dram, bank = core.nc, core.dram, core.bank
    with ExitStack() as ctx:
        def sb(name, shape, dt=F32):
            return ctx.enter_context(nc.sbuf_tensor("l3a_" + name, shape, dt))

        att = Softmax(core, sb, 8, False, "mask_causal", float(1.0 / np.sqrt(np.float32(8.0))), ())
        at = lambda *slots: [16 * k + s for k in range(NB) for s in slots]
        when = dict(att.when)
        when.update({
            "x_ready": at(1),
            "proj_done": at(2), "rot_done": at(3),
            "v_proj": at(4),
            "cos_ready": at(3),
            "sin_ready": at(4, 4), "roped": at(5, 5),
            "heads_ready": at(6, 6, 6, 6),
            "v_ready": at(5),
        })
        names = tuple(when) + ("w_ready",)
        sems, zero = ctx.enter_context(signals(nc, ["l3a_" + n for n in names]))
        sem = dict(zip(names, sems))
        sig = att.sig = Signals(sem, when)
        w, wr = {n: sb("w" + n, [P, P]) for n in "qkv"}, {n: sb("wr" + n, [P, P]) for n in "qk"}
        rope, head4 = sb("rope", [P, 2, SEQ]), sb("head4", [P, 4])
        xb, part, q = sb("xb", [P, SEQ]), sb("part", [P, 2, SEQ]), sb("q", [P, SEQ])
        load(core, [(w[n][:, :], dram["L3_attn_W" + n]) for n in w] +
             [(att.wo[:, 0, :], dram["L3_attn_Wo"]), (att.mask[:, :, :], att.mask_src), (rope[:, :, :], dram["rope_l3"]),
              (head4[:, :], dram["head_of_4"])])
        with nc.Block() as block:
            @block.vector
            def _(dve):
                for n in "qk":
                    src, dst = (z[n][:, :].rearrange("p (c s) -> p c s", s=2) for z in (w, wr))
                    nc.vector.tensor_scalar(dst[:, :, 0], src[:, :, 1], -1.0, None, ALU.mult)
                    last = nc.vector.tensor_copy(dst[:, :, 1], src[:, :, 0])
                last.then_inc(sem["w_ready"], 1)
                nc.vector.memset(att.v[:, :, :, :], 0.0).then_inc(sem["w_ready"], 1)
        zero()
        both = lambda z: z.rearrange("p (n q) -> p n q", n=2)
        cos = rope[:, 0, :].rearrange("p (a q) -> p a q", a=1).to_broadcast([P, 2, SEQ])

        def emit(block, slots, shift):
            @block.scalar
            def _(act):
                for slot in slots:
                    k, s = slot // 16, slot % 16
                    att.copy_turned(act, slot - 21)
                    att.exps(act, slot - 17)
                    if k < NB and s == 1:
                        sig.wait(act, "v_proj", k)
                        sig.done(nc.scalar.copy(xb[:, :], core.xnt[:, bass.ds((shift + k) * SEQ, SEQ)]), "x_ready")
                    if k < NB and s == 5:
                        sig.wait(act, "v_proj", k + 1)
                        sig.wait(act, "o_ready", 16 * (k - 1))
                        for t in range(TPB):
                            last = nc.scalar.copy(att.v[:, k % 2, t, :].rearrange("p (h c) -> p h c", h=HEADS)[:, :, 0:8],
                                                  bank[5][:, t * P:(t + 1) * P].rearrange("p (h d) -> p h d", d=8))
                        sig.done(last, "v_ready")

            @block.tensor
            def _(pe):
                for slot in slots:
                    k, s = slot // 16, slot % 16
                    if k < NB and s in (2, 3):
                        if s == 2:
                            sig.wait(pe, "x_ready", k + 1)
                            sig.wait(pe, "v_ready", k)
                        else:
                            sig.wait(pe, "sin_ready", 2 * k)
                        for i, n in enumerate("qk"):
                            last = nc.tensor.matmul(bank[3 + s][:, i * SEQ:(i + 1) * SEQ], (w if s == 2 else wr)[n][:, :],
                                                    xb[:, :], start=True, stop=True)
                        sig.done(last, "proj_done" if s == 2 else "rot_done")
                    if k < NB and s == 4:
                        sig.wait(pe, "cos_ready", k + 1)
                        for t in range(TPB):
                            last = nc.tensor.matmul(bank[5][:, t * P:(t + 1) * P], xb[:, t * P:(t + 1) * P], w["v"][:, :],
                                                    start=True, stop=True)
                        sig.done(last, "v_proj")
                    att.values(pe, slot - 22)
                    if slot in att.at:
                        kind, kk, j = att.at[slot]
                        att.project_out(pe, kk, j)
                    att.turn(pe, slot - 20)
                    if slot % 16 == 0 and 1 <= k <= NB:
                        sig.wait(pe, "heads_ready", 4 * k)
                        sig.wait(pe, "roped", 2 * k)
                    att.scores(pe, slot - 16)

            @block.gpsimd
            def _(pool):
                for slot in slots:
                    k, s = slot // 16, slot % 16
                    if k < NB and s == 6:
                        sig.wait(pool, "roped", 2 * k + 1)
                        for j in range(4):
                            sig.done(nc.gpsimd.tensor_scalar(att.qt[:, k % 2, j, :], q[:, :], head4[:, j:j + 1], None, ALU.mult),
                                     "heads_ready")

            @block.vector
            def _(dve):
                for slot in slots:
                    k, s = slot // 16, slot % 16
                    att.mask_and_max(dve, slot - 17)
                    att.reciprocals(dve, slot - 18)
                    att.divide(dve, slot - 18)
                    kind, kk, j = att.at.get(slot - 1, (None, 0, 0))
                    if kind == "y":
                        store_tile(core, sig, dve, att, shift, kk, j, residual=False)
                    kt = att.kt[:, k % 2, 0, :]
                    if k < NB and s == 3:
                        sig.wait(dve, "proj_done", k + 1)
                        sig.wait(dve, "roped", 2 * k)
                        sig.done(nc.vector.tensor_tensor(part[:, :, :], both(bank[5][:, :]), cos, ALU.mult), "cos_ready")
                    if k < NB and s == 4:
                        sig.wait(dve, "rot_done", k + 1)
                        sig.wait(dve, "heads_ready", 4 * k)
                        for i, dst in enumerate((q[:, :], kt)):
                            sig.done(nc.vector.tensor_tensor(dst, bank[6][:, i * SEQ:(i + 1) * SEQ], rope[:, 1, :], ALU.mult),
                                     "sin_ready")
                    if k < NB and s == 5:
                        sig.wait(dve, "sin_ready", 2 * (k + 1))
                        sig.wait(dve, "cos_ready", k + 1)
                        for i, dst in enumerate((q[:, :], kt)):
                            sig.done(nc.vector.tensor_tensor(dst, dst, part[:, i, :], ALU.add), "roped")
                    att.copy_columns(dve, nc.vector.tensor_copy, slot - 25)

        run_windows(nc, sig, zero, emit, att.last_slot)


def grouped_ffn_stage(core):
    nc, dram, bank = core.nc, core.dram, core.bank
    with ExitStack() as ctx:
        def sb(name, shape, dt=F32):
            return ctx.enter_context(nc.sbuf_tensor("grp_" + name, shape, dt))

        names = ("loaded", "turned", "w_ready", "hid_done", "h_ready", "out_done", "stored")
        sems, zero = ctx.enter_context(signals(nc, ["grp_" + n for n in names]))
        sem = dict(zip(names, sems))
        w1, w2, w1t, w2t = (sb(n, [P, 4, P]) for n in ("w1", "w2", "w1t", "w2t"))
        b1, b2, h = sb("b1", [P, 4]), sb("b2", [P, P]), sb("h", [P, 4, GTOK])
        with nc.Fori(0, NG) as g:
            with nc.Block() as block:
                @block.sync
                def _(sp):
                    one = bass.ds(g, 1)
                    sp.dma_start(w1[:, :, :], dram["L3_ffn_W1"][one, :, :].rearrange("a (c p) h -> p (a c) h", p=P)).then_inc(sem["loaded"], 16)
                    sp.dma_start(w2[:, :, :], dram["L3_ffn_W2"][one, :, :].rearrange("a p (c o) -> p (a c) o", o=P)).then_inc(sem["loaded"], 16)
                    sp.dma_start(b1[:, :], dram["L3_ffn_b1"][one, :].rearrange("a (c p) -> p (a c)", p=P)).then_inc(sem["loaded"], 16)
                    sp.dma_start(b2[:, :], dram["L3_ffn_b2"][one, :].to_broadcast([P, P])).then_inc(sem["loaded"], 16)
                    sp.wait_ge(sem["loaded"], 64)

                @block.tensor
                def _(pe):
                    pe.wait_ge(sem["loaded"], 64)
                    for i, w in enumerate((w1, w2)):
                        for c in range(4):
                            last = nc.tensor.transpose(bank[i][:, c * P:(c + 1) * P], w[:, c, :], core.ident[:, :])
                        last.then_inc(sem["turned"], 1)
                    pe.wait_ge(sem["w_ready"], 1)
                    for c in range(4):
                        nc.tensor.matmul(bank[2 + c][:, :], w1t[:, c, :], core.xnt[:, bass.ds(g * GTOK, GTOK)], start=True,
                                         stop=True).then_inc(sem["hid_done"], 1)
                    pe.wait_ge(sem["w_ready"], 2)
                    pe.wait_ge(sem["h_ready"], 4)
                    for j in range(4):
                        for c in range(4):
                            last = nc.tensor.matmul(bank[6][:, j * P:(j + 1) * P], h[:, c, j * P:(j + 1) * P], w2t[:, c, :],
                                                    start=(c == 0), stop=(c == 3))
                    last.then_inc(sem["out_done"], 1)

                @block.scalar
                def _(act):
                    for c in range(4):
                        act.wait_ge(sem["hid_done"], c + 1)
                        nc.scalar.activation(h[:, c, :], bank[2 + c][:, :], ACT.Identity, bias=b1[:, c:c + 1]).then_inc(sem["h_ready"], 1)

                @block.vector
                def _(dve):
                    for i, wt in enumerate((w1t, w2t)):
                        dve.wait_ge(sem["turned"], i + 1)
                        nc.vector.tensor_copy(wt[:, :, :], bank[i][:, :].rearrange("p (c q) -> p c q", c=4)).then_inc(sem["w_ready"], 1)
                    dve.wait_ge(sem["out_done"], 1)
                    nc.vector.tensor_tensor(core.y[:, bass.ds(g * 4, 4), :], bank[6][:, :].rearrange("p (j c) -> p j c", j=4),
                                            b2[:, :].rearrange("p (a c) -> p a c", a=1).to_broadcast([P, 4, P]),
                                            ALU.add).then_inc(sem["stored"], 1)
            zero()


LAYERS_RUN = DEPTH


def program(nc, dram, out, stop=None):
    with ExitStack() as ctx:
        ctx.enter_context(nc.allow_non_contiguous_dma(reason="vectors of a few hundred elements laid over partitions"))
        core = Core(nc, dram, ctx)
        load(core, [(core.x[:, :, :], dram["L0_attn_x"].rearrange("b (t p) c -> p (b t) c", p=P)),
                    (core.ident[:, :], dram["ident"])])

        def store(rows):
            with signals(nc, ["out_stored"]) as ((out_stored,), zero):
                with nc.Block() as block:
                    @block.sync
                    def _(sp):
                        sp.dma_start(out.rearrange("b (t p) c -> p (b t) c", p=P), rows[:, :, :]).then_inc(out_stored, 16)
                        sp.wait_ge(out_stored, 16)

        for name, stage, shown in stages():
            stage(core)
            core.stage += 1
            if stop == name:
                return store(shown(core))
        store(core.x)


def stages():
    return [
        ("ln0", layer_norm_stage, lambda c: c.xn),
        ("s0", linear_attention_stage, lambda c: c.s),
        ("g0", local_transformer_stage, lambda c: c.y),
        ("x0", combine_stage, lambda c: c.x),
        ("ln1", layer_norm_stage, lambda c: c.xn),
        ("s1", gelu_linear_attention_stage, lambda c: c.s),
        ("g1", experts_stage, lambda c: c.y),
        ("x1", combine_stage, lambda c: c.x),
        ("ln2", layer_norm_stage, lambda c: c.xn),
        ("s2", causal_attention_stage, lambda c: c.s),
        ("g2", routed_ffn_stage, lambda c: c.y),
        ("x2", combine_stage, lambda c: c.x),
        ("ln3", layer_norm_stage, lambda c: c.xn),
        ("s3", small_head_attention_stage, lambda c: c.s),
        ("g3", grouped_ffn_stage, lambda c: c.y),
        ("x3", combine_stage, lambda c: c.x),
    ]


def kernel(**inputs):
    import concourse.bacc as bacc
    from concourse.bass_utils import run_bass_kernel_spmd

    arrays = {f"in_{k}": np.ascontiguousarray(v) for k, v in inputs.items()}
    arrays.update({f"table_{k}": v for k, v in shape_constants().items()})
    nc = bacc.Bacc("TRN2", target_bir_lowering=False, num_devices=1)
    dram = {n.split("_", 1)[1]: nc.dram_tensor(n, a.shape, F32, kind="ExternalInput").ap() for n, a in arrays.items()}
    out = nc.dram_tensor("out", (NB, SEQ, P), F32, kind="ExternalOutput").ap()
    program(nc, dram, out)
    r = run_bass_kernel_spmd(nc, [arrays], core_ids=[0])
    return r.results[0]["out"]
```
